# Optimizing a Trainium2 kernel written in Bass

```python
import numpy as np
import jax
import jax.numpy as jnp

def _softmax(x, axis=-1):
    return jax.nn.softmax(x, axis=axis)

def _gelu(x):
    return jax.nn.gelu(x, approximate=True)

def _silu(x):
    return jax.nn.silu(x)

def _sigmoid(x):
    return jax.nn.sigmoid(x)

def _layernorm(x, axis=-1, eps=1e-05):
    m = jnp.mean(x, axis=axis, keepdims=True)
    v = jnp.var(x, axis=axis, keepdims=True)
    return (x - m) / jnp.sqrt(v + eps)

def _scatter_add(tgt, idx, src, axis=0):
    return tgt.at[idx].add(src)

def _segment_sum(src, seg, n):
    return jax.ops.segment_sum(src, seg, n)
kernel_name = 'mk_perceiver_d1_seqx_r4_e076cb'

def setup_inputs(seed: int=0):
    np.random.seed(seed)
    _w = jnp.asarray

    def _rec_inputs():
        import jax
        import jax.numpy as jnp
        _rk = jax.random.key(seed)
        x = 0.002226 + 0.9996 * jax.random.normal(jax.random.fold_in(_rk, 1), (16, 64, 256), jnp.float32)
        _lenS = 64 - jax.random.randint(jax.random.fold_in(_rk, 7), (16,), 0, max(1, 64 // 4) + 1, jnp.int32)
        _lenS2 = 1601 - jax.random.randint(jax.random.fold_in(_rk, 8), (16,), 0, max(1, 1601 // 4) + 1, jnp.int32)
        _ctx_1024P = jax.random.normal(jax.random.fold_in(_rk, 11), (16, 16, 256), jnp.float32)
        _ctx_1024c = jax.random.dirichlet(jax.random.fold_in(_rk, 511), 0.3 * jnp.ones((16,), jnp.float32), (16, 1601))
        _ctx_1024t = jnp.einsum('bsk,bkd->bsd', _ctx_1024c, _ctx_1024P)
        _ctx_1024t = _ctx_1024t * jax.lax.rsqrt(jnp.mean(jnp.square(_ctx_1024t)) + 1e-12) * 0.953939
        ctx_1024 = -0.000125008 + 0.999885 * (_ctx_1024t + 0.3 * jax.random.normal(jax.random.fold_in(_rk, 611), (16, 1601, 256), jnp.float32))
        _validS = jnp.arange(64)[None, :] < _lenS[:, None]
        _validS2 = jnp.arange(1601)[None, :] < _lenS2[:, None]
        _causal = jnp.tril(jnp.ones((64, 64), dtype=bool))
        mask_BxS2_bk0 = jnp.logical_not(jnp.broadcast_to(_validS2[:, :], (16, 1601)))
        return (x, ctx_1024, mask_BxS2_bk0)
    x, ctx_1024, mask_BxS2_bk0 = _rec_inputs()

    def _L0_xattn_setup():
        import jax, jax.numpy as jnp
        import numpy as np
        EPS = 1e-05

        def layer_norm(x, g, b):
            mu = jnp.mean(x, axis=-1, keepdims=True)
            var = jnp.mean((x - mu) ** 2, axis=-1, keepdims=True)
            return (x - mu) * jax.lax.rsqrt(var + EPS) * g + b
        key = jax.random.key(seed)
        ks = jax.random.split(key, 8)
        b, n, l, D = (8, 1024, 64, 256)
        heads, dim_head = (16, 64)
        inner = heads * dim_head
        x = jax.random.normal(ks[0], (b, n, D), dtype=jnp.float32)
        latents = jax.random.normal(ks[1], (b, l, D), dtype=jnp.float32)
        mask = jax.random.randint(ks[2], (b, n), 0, 2) > 0
        Wq = jax.random.normal(ks[3], (D, inner), dtype=jnp.float32) * D ** (-0.5)
        Wkv = jax.random.normal(ks[4], (D, 2 * inner), dtype=jnp.float32) * D ** (-0.5)
        Wout = jax.random.normal(ks[5], (inner, D), dtype=jnp.float32) * inner ** (-0.5)
        g1 = jnp.ones((D,), jnp.float32)
        b1 = jnp.zeros((D,), jnp.float32)
        g2 = jnp.ones((D,), jnp.float32)
        b2 = jnp.zeros((D,), jnp.float32)
        return {'x': x, 'latents': latents, 'mask': mask, 'g1': g1, 'b1': b1, 'g2': g2, 'b2': b2, 'Wq': Wq, 'Wkv': Wkv, 'Wout': Wout}
    _L0_xattn_all = _L0_xattn_setup()
    _L0_xattn_in = {k: v for k, v in _L0_xattn_all.items() if k in ('g1', 'b1', 'g2', 'b2', 'Wq', 'Wkv', 'Wout')}
    del _L0_xattn_all

    def _L0_attn_setup():
        import jax, jax.numpy as jnp
        import numpy as np
        B, T, D = (4, 512, 256)
        N_HEADS = 16
        HEAD_DIM = D // N_HEADS

        def rope(x):
            t, dh = (x.shape[-2], x.shape[-1])
            half = dh // 2
            theta = 1.0 / 10000.0 ** (jnp.arange(half, dtype=jnp.float32) / half)
            ang = jnp.arange(t, dtype=jnp.float32)[:, None] * theta[None, :]
            sin, cos = (jnp.sin(ang), jnp.cos(ang))
            x1 = x[..., 0::2]
            x2 = x[..., 1::2]
            return jnp.concatenate([x1 * cos - x2 * sin, x1 * sin + x2 * cos], axis=-1)
        key = jax.random.key(seed)
        ks = jax.random.split(key, 9)
        s = 0.02
        return {'x': jax.random.normal(ks[0], (B, T, D), dtype=jnp.float32), 'W_q': jax.random.normal(ks[1], (D, D), dtype=jnp.float32) * s, 'b_q': jnp.zeros((D,), dtype=jnp.float32), 'W_k': jax.random.normal(ks[2], (D, D), dtype=jnp.float32) * s, 'b_k': jnp.zeros((D,), dtype=jnp.float32), 'W_v': jax.random.normal(ks[3], (D, D), dtype=jnp.float32) * s, 'b_v': jnp.zeros((D,), dtype=jnp.float32), 'W_o': jax.random.normal(ks[4], (D, D), dtype=jnp.float32) * s, 'b_o': jnp.zeros((D,), dtype=jnp.float32)}
    _L0_attn_all = _L0_attn_setup()
    _L0_attn_in = {k: v for k, v in _L0_attn_all.items() if k in ('W_q', 'b_q', 'W_k', 'b_k', 'W_v', 'b_v', 'W_o', 'b_o')}
    del _L0_attn_all

    def _L0_ffn_setup():
        import jax, jax.numpy as jnp
        import numpy as np
        B, S, D, H, E, K = (4, 512, 256, 1024, 4, 2)
        key = jax.random.key(seed)
        ks = jax.random.split(key, 7)
        s1 = 1.0 / np.sqrt(D)
        s2 = 1.0 / np.sqrt(H)
        return {'x': jax.random.normal(ks[0], (B, S, D), jnp.float32), 'w1': jax.random.uniform(ks[1], (E, D, H), jnp.float32, -s1, s1), 'b1': jax.random.uniform(ks[2], (E, H), jnp.float32, -s1, s1), 'w2': jax.random.uniform(ks[3], (E, H, D), jnp.float32, -s2, s2), 'b2': jax.random.uniform(ks[4], (E, D), jnp.float32, -s2, s2), 'wr': jax.random.uniform(ks[5], (D, E), jnp.float32, -s1, s1), 'br': jax.random.uniform(ks[6], (E,), jnp.float32, -s1, s1)}
    _L0_ffn_all = _L0_ffn_setup()
    _L0_ffn_in = {k: v for k, v in _L0_ffn_all.items() if k in ('w1', 'b1', 'w2', 'b2', 'wr', 'br')}
    del _L0_ffn_all
    return {'x': x, 'ctx_1024': ctx_1024, 'mask_BxS2_bk0': mask_BxS2_bk0, 'L0_xattn_g1': _L0_xattn_in['g1'], 'L0_xattn_b1': _L0_xattn_in['b1'], 'L0_xattn_g2': _L0_xattn_in['g2'], 'L0_xattn_b2': _L0_xattn_in['b2'], 'L0_xattn_Wq': _L0_xattn_in['Wq'], 'L0_xattn_Wkv': _L0_xattn_in['Wkv'], 'L0_xattn_Wout': _L0_xattn_in['Wout'], 'L0_attn_W_q': _L0_attn_in['W_q'], 'L0_attn_b_q': _L0_attn_in['b_q'], 'L0_attn_W_k': _L0_attn_in['W_k'], 'L0_attn_b_k': _L0_attn_in['b_k'], 'L0_attn_W_v': _L0_attn_in['W_v'], 'L0_attn_b_v': _L0_attn_in['b_v'], 'L0_attn_W_o': _L0_attn_in['W_o'], 'L0_attn_b_o': _L0_attn_in['b_o'], 'L0_ffn_w1': _L0_ffn_in['w1'], 'L0_ffn_b1': _L0_ffn_in['b1'], 'L0_ffn_w2': _L0_ffn_in['w2'], 'L0_ffn_b2': _L0_ffn_in['b2'], 'L0_ffn_wr': _L0_ffn_in['wr'], 'L0_ffn_br': _L0_ffn_in['br']}

def reference(x, ctx_1024, mask_BxS2_bk0, L0_xattn_g1, L0_xattn_b1, L0_xattn_g2, L0_xattn_b2, L0_xattn_Wq, L0_xattn_Wkv, L0_xattn_Wout, L0_attn_W_q, L0_attn_b_q, L0_attn_W_k, L0_attn_b_k, L0_attn_W_v, L0_attn_b_v, L0_attn_W_o, L0_attn_b_o, L0_ffn_w1, L0_ffn_b1, L0_ffn_w2, L0_ffn_b2, L0_ffn_wr, L0_ffn_br):
    import jax
    import jax.numpy as jnp

    def _L0_xattn_ref(x, latents, mask, g1, b1, g2, b2, Wq, Wkv, Wout):
        import jax, jax.numpy as jnp
        import numpy as np
        EPS = 1e-05

        def layer_norm(x, g, b):
            mu = jnp.mean(x, axis=-1, keepdims=True)
            var = jnp.mean((x - mu) ** 2, axis=-1, keepdims=True)
            return (x - mu) * jax.lax.rsqrt(var + EPS) * g + b
        heads, dim_head = (16, 64)
        b, n, D = x.shape
        l = latents.shape[1]
        xn = layer_norm(x, g1, b1)
        ln_lat = layer_norm(latents, g2, b2)
        q = ln_lat @ Wq
        kv = jnp.concatenate([xn, ln_lat], axis=1) @ Wkv
        k, v = jnp.split(kv, 2, axis=-1)

        def to_heads(t):
            return t.reshape(t.shape[0], t.shape[1], heads, dim_head).transpose(0, 2, 1, 3)
        q, k, v = (to_heads(q), to_heads(k), to_heads(v))
        scale = 1.0 / np.sqrt(np.sqrt(dim_head)).astype(np.float32)
        weight = jnp.einsum('bhld,bhnd->bhln', q * scale, k * scale)
        full_mask = jnp.concatenate([mask, jnp.ones((b, l), dtype=bool)], axis=1)
        neg = -jnp.finfo(weight.dtype).max
        weight = jnp.where(full_mask[:, None, None, :], weight, neg)
        weight = jax.nn.softmax(weight.astype(jnp.float32), axis=-1).astype(q.dtype)
        out = jnp.einsum('bhln,bhnd->bhld', weight, v)
        out = out.transpose(0, 2, 1, 3).reshape(b, l, heads * dim_head)
        return out @ Wout

    def _L0_attn_ref(x, W_q, b_q, W_k, b_k, W_v, b_v, W_o, b_o):
        import jax, jax.numpy as jnp
        import numpy as np
        B, T, D = (4, 512, 256)
        N_HEADS = 16
        HEAD_DIM = D // N_HEADS

        def rope(x):
            t, dh = (x.shape[-2], x.shape[-1])
            half = dh // 2
            theta = 1.0 / 10000.0 ** (jnp.arange(half, dtype=jnp.float32) / half)
            ang = jnp.arange(t, dtype=jnp.float32)[:, None] * theta[None, :]
            sin, cos = (jnp.sin(ang), jnp.cos(ang))
            x1 = x[..., 0::2]
            x2 = x[..., 1::2]
            return jnp.concatenate([x1 * cos - x2 * sin, x1 * sin + x2 * cos], axis=-1)
        b, t, d = x.shape
        h, dh = (N_HEADS, d // N_HEADS)

        def heads(y):
            return y.reshape(b, t, h, dh).transpose(0, 2, 1, 3)
        q = rope(heads(x @ W_q.T + b_q))
        k = rope(heads(x @ W_k.T + b_k))
        v = heads(x @ W_v.T + b_v)
        scores = jnp.einsum('bhtd,bhsd->bhts', q, k)
        causal = jnp.tril(jnp.ones((t, t), dtype=bool))
        mask = jnp.where(causal, 0.0, -jnp.inf)
        probs = jax.nn.softmax((scores + mask) / jnp.sqrt(jnp.float32(dh)), axis=-1)
        out = jnp.einsum('bhts,bhsd->bhtd', probs, v)
        out = out.transpose(0, 2, 1, 3).reshape(b, t, d)
        return out @ W_o.T + b_o

    def _L0_ffn_ref(x, w1, b1, w2, b2, wr, br):
        import jax, jax.numpy as jnp
        import numpy as np
        B, S, D, H, E, K = (4, 512, 256, 1024, 4, 2)
        Bx, Sx, Dx = x.shape
        xf = x.reshape(-1, Dx)
        logits = xf @ wr + br
        topk_vals, topk_idx = jax.lax.top_k(logits, K)
        gates = jax.nn.softmax(topk_vals, axis=-1)
        h = jax.nn.gelu(jnp.einsum('nd,edh->enh', xf, w1) + b1[:, None, :], approximate=False)
        y = jnp.einsum('enh,ehd->end', h, w2) + b2[:, None, :]
        c = jnp.einsum('eh,ehd->ed', jax.nn.gelu(b1, approximate=False), w2) + b2
        c_sum = c.sum(axis=0)
        yt = jnp.transpose(y, (1, 0, 2))
        y_sel = jnp.take_along_axis(yt, topk_idx[:, :, None], axis=1)
        c_sel = c[topk_idx]
        out = jnp.einsum('nk,nkd->nd', gates, y_sel - c_sel + c_sum[None, None, :])
        return out.reshape(Bx, Sx, Dx)
    x = x + _L0_xattn_ref(ctx_1024, _layernorm(x, axis=-1), mask_BxS2_bk0, L0_xattn_g1, L0_xattn_b1, L0_xattn_g2, L0_xattn_b2, L0_xattn_Wq, L0_xattn_Wkv, L0_xattn_Wout)
    x = x + _L0_attn_ref(_layernorm(x, axis=-1), L0_attn_W_q, L0_attn_b_q, L0_attn_W_k, L0_attn_b_k, L0_attn_W_v, L0_attn_b_v, L0_attn_W_o, L0_attn_b_o)
    x = x + _L0_ffn_ref(_layernorm(x, axis=-1), L0_ffn_w1, L0_ffn_b1, L0_ffn_w2, L0_ffn_b2, L0_ffn_wr, L0_ffn_br)
    return x

_drawn_inputs = setup_inputs


def setup_inputs(seed=0):
    import zlib

    import numpy as np

    out = dict(_drawn_inputs(seed))
    spreads = {'L0_xattn_g1': (1.0, 0.2),
     'L0_xattn_b1': (0.0, 0.1),
     'L0_xattn_g2': (1.0, 0.2),
     'L0_xattn_b2': (0.0, 0.1),
     'L0_attn_b_q': (0.0, 0.8),
     'L0_attn_b_k': (0.0, 2.0),
     'L0_attn_b_v': (0.0, 0.1),
     'L0_attn_b_o': (0.0, 0.1)}
    factors = {'L0_attn_W_q': 8.0, 'L0_attn_W_k': 8.0, 'L0_ffn_b1': 2.884}
    for name, (base, spread) in spreads.items():
        noise = np.random.default_rng([zlib.crc32(name.encode()), seed]).standard_normal(out[name].shape)
        drawn = base * np.exp(spread * noise) if base else spread * noise
        out[name] = jnp.asarray(drawn.astype(out[name].dtype))
    for name, factor in factors.items():
        out[name] = (out[name] * factor).astype(out[name].dtype)
    return out
```

```python
from contextlib import ExitStack

import numpy as np

import concourse.bass as bass
from concourse import mybir

ALU = mybir.AluOpType
ACT = mybir.ActivationFunctionType
AX = mybir.AxisListType
F32 = mybir.dt.float32
F32R = mybir.dt.float32r
BF16 = mybir.dt.bfloat16
U8 = mybir.dt.uint8

P = 128
B, L, D = 16, 64, 256
N = 1601
KD = D // P
HX, DX = 16, 64
PAIRS = HX // 2
INNER = HX * DX
ROWS = B * L
RT = ROWS // P
CH = 13
KEYS = CH * P
LAST = N - 1
CPP = 12
TAIL = CPP * P
QTR = KEYS // 4
NEG = -3.0e38
EPS = 1e-5
GROUPS = [(0, 4), (4, 8), (8, 12), (12, 13)]

STAT = [*range(1, CH + 1), 0]

HL3 = ((0, 0), (0, 1), (1, 0))


X_UNITS = (0, 0, 0, 3, 3, 2, 2, 2, 2, 0, 0, 0, 0)
Y_UNITS = (2, 2, 2, 2, 2, 1, 1, 1, 0, 0, 0, 0, 0)


def plan_x(has_a, has_b, has_next):
    ev = []
    units = [(i, j) for i in range(4) for j in range(4)]
    at = 2
    if has_a:
        ev += [("K", 0, 0), ("K", 1, 0), ("Q", 0), ("K", 0, 1), ("K", 1, 1)]
    for c in range(CH):
        if has_a:
            if c == 1:
                ev += [("K", 0, 2), ("K", 1, 2)] + unit_events(0, 0, 0)
            if c == 2:
                ev += [("K", 0, 3), ("K", 1, 3)] + unit_events(0, 1, 0)
            for i, j in units[at:at + X_UNITS[c]]:
                ev += unit_events(i, j, 0)
            at += X_UNITS[c]
            if c == 9 and not has_b:
                ev += [("N", 0), ("N", 1)]
            if c == 10:
                ev += [("P", 3)]
            if c == 12:
                ev += [("T", 0, 0)]
        if has_b:
            if c + 2 < CH:
                ev += [("T", 1, c + 2)]
            ev += [("V", 1, c)]
            if c == 2:
                ev += [("Y", 0)]
            if has_a and c in (4, 8):
                ev += [("N", c // 4 - 1)]
        if has_next:
            ev += {6: [("S", 4)], 9: [("S", 0)], 12: [("S", 1)]}.get(c, [])
    if has_b:
        ev += [("O", 1)]
    if has_a:
        ev += [("C",)]
    return ev


def plan_y(has_prev, has_next):
    ev = [("T", 0, 1)]
    units = [(i, j) for i in range(4, 8) for j in range(4)]
    at = 3
    for i, j in units[:at]:
        ev += unit_events(i, j, 4)
    for c in range(CH):
        for i, j in units[at:at + Y_UNITS[c]]:
            ev += unit_events(i, j, 4)
        at += Y_UNITS[c]
        ev += [("T", 0, c + 2)] if c + 2 < CH else [("T", 2, c - 11)]
        ev += [("V", 0, c)]
        if c < 2:
            ev += [("N", c + 2)]
        if c == 2 and has_prev:
            ev += [("Y", 1)]
        if has_next:
            ev += {2: [("H", 13, 0, 1)], 3: [("H", 2, 3), ("S", 2), ("S", 3)], 5: [("H", 4, 5)], 6: [("H", 6, 7)],
                   8: [("H", 8, 9)], 9: [("H", 10, 11)], 10: [("H", 12)], 11: [("B",)]}.get(c, [])
        if c == 8:
            ev += [("P", 7)]
    return ev + [("O", 0)]


def unit_events(i, j, first):
    ev = [("A", i, j)]
    if j == 0 and i < PAIRS - 1:
        ev += [("Q", i + 1)]
    if j == 1 and i > first:
        ev += [("P", i - 1)]
    if j == 3:
        ev += [("E", i)]
    return ev


def t_uses(ev):
    return [e for e in ev if e[0] in "YTQ"]


K_BANK = ((0, 1), (2, 3), (2, 3), (3, 3))
X_FIRST, X_MID, X_END = plan_x(True, False, True), plan_x(True, True, True), plan_x(False, True, False) + [("Y", 1)]
X_LAST = plan_x(True, True, False)
Y_FIRST, Y_MID, Y_LAST = plan_y(False, True), plan_y(True, True), plan_y(True, False)
USE0 = {e: n for n, e in enumerate(t_uses(X_FIRST + Y_FIRST))}
USE = {e: n for n, e in enumerate(t_uses(X_MID + Y_MID))}
NUSE0, NUSE = len(USE0), len(USE)
USE_END = {e: n for n, e in enumerate(t_uses(X_END))}
assert NUSE % 2 == 0


class Batch:

    def __init__(self, off, turn=None):
        self.off, self.turn = off, turn

    def lin(self, k, c):
        n = self.off * k + c
        return n if self.turn is None else self.turn * k + n

    def use(self, e):
        if self.turn is None and self.off == 0:
            return USE0[e]
        return self.lin(NUSE, NUSE0 - NUSE + (USE_END if self.off == B else USE)[e])

    def bank(self, e):
        if self.turn is None and self.off == 0:
            return USE0[e] % 2
        return (NUSE0 + (USE_END if self.off == B else USE)[e]) % 2

    def least(self, k, c):
        return self.off * k + c


def wait(eng, sem, batch, k, c):
    assert batch.turn is None or batch.least(k, c) > 0
    if batch.least(k, c) > 0:
        eng.wait_ge(sem, batch.lin(k, c))


def apart(ins, sem):
    return ins.wait_op(sem, 1, "sem-ge")


def periods(eng, step):
    step(Batch(0), X_FIRST, Y_FIRST)
    step(Batch(1), X_MID, Y_MID)
    with eng.Fori(0, B - 3) as turn:
        step(Batch(2, turn), X_MID, Y_MID)
    step(Batch(B - 1), X_LAST, Y_LAST)
    step(Batch(B), X_END, [])


def value_bank(h, c):
    slot = (c + h) % 3
    mine = 13 * h + c
    for m in range(mine - 1, mine - 14, -1):
        hh, cc = (m // 13) % 2, m % 13
        if (cc + hh) % 3 == slot:
            return slot, m + 1


def split_pair(pe, out, weights, moving, first, last):
    for n, (a, b) in enumerate(HL3):
        mm = pe.matmul(out, weights(a), moving(b), start=first and n == 0, stop=last and n == 2)
    return mm


def block_0(nc, ins, lat_scratch, q_scratch, W, ctx):
    def sb(name, shape, dt):
        return ctx.enter_context(nc.sbuf_tensor(name, shape, dt))

    def sem(name):
        return ctx.enter_context(nc.semaphore(name))

    x = sb("x0_rows", [P, RT, D], F32)
    lat = sb("lat", [P, RT, D], F32)
    latT = sb("latT", [P, KD, 2, ROWS], F32R)
    wraw = sb("wraw", [P, 3, 2 * INNER], F32)
    wq = sb("wq", [P, KD, 2, INNER], F32R)
    qstage = sb("qstage", [P, B, PAIRS, L], F32)
    g2 = sb("g2", [P, D], F32)
    b2 = sb("b2", [P, D], F32)
    stats = sb("stats0", [P, 2, RT, 6], F32)
    mv = sb("mv", [P, 2, RT, 2], F32)
    veps = sb("veps", [P, 2, RT], F32)
    rstd = sb("rstd0", [P, 2, RT], F32)
    bank = [ctx.enter_context(nc.psum_tensor(f"bank0_{n}", [P, 512], F32)) for n in range(4)]

    x_in = sem("x_in0")
    w_in = [sem(f"w_in{n}") for n in range(3)]
    gb_in = sem("gb_in")
    ident_done = sem("ident_done")
    zero_done = sem("zero_done")
    mv_done = sem("mv_done")
    rstd0_done = sem("rstd0_done")
    pool0 = sem("pool0")
    dve0 = sem("dve0")
    lat_done = sem("lat_done")
    bank_full = sem("bank_full")
    high_done = sem("high_done")
    low_done = sem("low_done")
    q_done = sem("q_done")
    wh_done = sem("wh_done")
    wl_done = sem("wl_done")
    out0 = sem("out0")
    splits = [(wraw[:, 0, :].rearrange("p (k n) -> p k n", k=KD), wq[:, :, :, :]),
              (wraw[:, 1, :].rearrange("p (k n) -> p k n", k=PAIRS), W["wk"][:, :, :, :]),
              (wraw[:, 2, :].rearrange("p (k n) -> p k n", k=KD), W["wv"][:, :, :, :])]

    block = ctx.enter_context(nc.Block())

    @block.sync
    def _(sp):
        sp.dma_start(x[:, :, :], ins["x"].rearrange("(t p) d -> p t d", p=P)).then_inc(x_in, 16)
        sp.dma_start(wraw[:, 0, :].rearrange("p (k n) -> p k n", k=KD), ins["wq"].rearrange("(k p) n -> p k n", p=P)
                     ).then_inc(w_in[0], 16)
        sp.dma_start(g2[:, :], ins["g2"].partition_broadcast(P)).then_inc(gb_in, 16)
        sp.dma_start(b2[:, :], ins["b2x"].partition_broadcast(P)).then_inc(gb_in, 16)
        sp.dma_start(W["g1"][:, :], ins["g1"].partition_broadcast(P)).then_inc(gb_in, 16)
        sp.dma_start(W["b1"][:, :], ins["b1x"].partition_broadcast(P)).then_inc(gb_in, 16)
        sp.dma_start(wraw[:, 1, :].rearrange("p (k n) -> p k n", k=PAIRS), ins["wkT"].rearrange("(k p) n -> p k n", p=P)
                     ).then_inc(w_in[1], 16)
        sp.dma_start(wraw[:, 2, :].rearrange("p (k n) -> p k n", k=KD), ins["wv"].rearrange("(k p) n -> p k n", p=P)
                     ).then_inc(w_in[2], 16)
        sp.wait_ge(lat_done, RT)
        sp.dma_start(lat_scratch.rearrange("(t b) l d -> (b l) t d", b=2), lat[:, :, :]).then_inc(out0, 16)
        sp.wait_ge(q_done, 16)
        for b in range(B):
            sp.dma_start(q_scratch[b], qstage[:, b, :, :]).then_inc(out0, 16)
        sp.wait_ge(gb_in, 64)
        sp.wait_ge(out0, 16 * (B + 1))

    @block.gpsimd
    def _(pool):
        pool.memset(W["ident"][:, :], 0.0).then_inc(pool0, 1)
        pool.wait_ge(pool0, 1)
        pool.affine_select(out=W["ident"][:, :], in_=W["ident"][:, :], compare_op=ALU.not_equal, fill=1.0, base=0,
                           pattern=[[-1, P]], channel_multiplier=1).then_inc(ident_done, 1)
        pool.memset(W["neghalf"][:, :], -0.5).then_inc(pool0, 1)
        pool.memset(W["bias"][:, :], 0.0).then_inc(zero_done, 1)
        pool.wait_ge(pool0, 2)
        for turn in range(2):
            pool.wait_ge(mv_done, RT * (turn + 1))
            pool.tensor_scalar(veps[:, turn, :], mv[:, turn, :, 1], 1.0, EPS, ALU.mult, ALU.add).then_inc(pool0, 1)
            pool.wait_ge(pool0, 3 + turn)
            pool.tensor_tensor(rstd[:, turn, :], veps[:, turn, :], W["neghalf"][:, 0:RT], ALU.pow).then_inc(rstd0_done, 1)

    @block.vector
    def _(dve):
        chain = [0]

        def link(ins):
            chain[0] += 1
            ins.then_inc(dve0, 1)
            dve.wait_ge(dve0, chain[0])

        dve.wait_ge(x_in, 16)
        for turn in range(2):
            src = x if turn == 0 else lat
            for t in range(RT):
                link(dve.bn_stats(stats[:, turn, t, :], src[:, t, :]))
                dve.bn_aggr(mv[:, turn, t, :], stats[:, turn, t, :]).then_inc(mv_done, 1)
            dve.wait_ge(rstd0_done, turn + 1)
            for t in range(RT):
                link(dve.tensor_scalar(lat[:, t, :], src[:, t, :], mv[:, turn, t, 0:1], rstd[:, turn, t:t + 1],
                                       ALU.subtract, ALU.mult))
        dve.wait_ge(gb_in, 64)
        for t in range(RT):
            link(dve.tensor_tensor(lat[:, t, :], lat[:, t, :], g2[:, :], ALU.mult))
            dve.tensor_tensor(lat[:, t, :], lat[:, t, :], b2[:, :], ALU.add).then_inc(lat_done, 1)
        dve.memset(W["qblk"][:, :, :, :].bitcast(F32), 0.0).then_inc(zero_done, 1)
        for n in range(4):
            dve.wait_ge(high_done, n + 1)
            k, half = n % 2, n // 2
            s = slice(half * 512, half * 512 + 512)
            dve.tensor_tensor(latT[:, k, 1, s], bank[n][:, :], latT[:, k, 0, s].bitcast(F32), ALU.subtract
                              ).then_inc(low_done, 1)
        for n, (src, to) in enumerate(splits):
            dve.wait_ge(wh_done, n + 1)
            dve.tensor_tensor(to[:, :, 1, :], src, to[:, :, 0, :].bitcast(F32), ALU.subtract).then_inc(wl_done, 1)

    @block.scalar
    def _(act):
        act.wait_ge(w_in[0], 16)
        act.activation(splits[0][1][:, :, 0, :], splits[0][0], ACT.Copy).then_inc(wh_done, 1)
        for n in range(4):
            act.wait_ge(bank_full, n + 1)
            k, half = n % 2, n // 2
            act.activation(latT[:, k, 0, half * 512:half * 512 + 512], bank[n][:, :], ACT.Copy).then_inc(high_done, 1)
        for n in (1, 2):
            act.wait_ge(w_in[n], 16)
            act.activation(splits[n][1][:, :, 0, :], splits[n][0], ACT.Copy).then_inc(wh_done, 1)
        for n in range(16):
            pair, half = n // 2, n % 2
            act.wait_ge(bank_full, 5 + n)
            act.activation(qstage[:, 8 * half:8 * half + 8, pair, :], bank[n % 4][:, :].rearrange("p (b l) -> p b l", l=L),
                           ACT.Copy, scale=DX ** -0.5).then_inc(q_done, 1)

    @block.tensor
    def _(pe):
        pe.wait_ge(ident_done, 1)
        pe.wait_ge(lat_done, RT)
        for n in range(4):
            k, half = n % 2, n // 2
            for t in range(4):
                mm = pe.transpose(bank[n][:, t * P:(t + 1) * P], lat[:, 4 * half + t, k * P:(k + 1) * P], W["ident"][:, :])
            mm.then_inc(bank_full, 1)
        pe.wait_ge(low_done, 4)
        pe.wait_ge(wl_done, 1)
        for n in range(16):
            pair, half = n // 2, n % 2
            if n >= 4:
                pe.wait_ge(q_done, n - 3)
            for k in range(KD):
                mm = split_pair(pe, bank[n % 4][:, :], lambda q: wq[:, k, q, pair * P:(pair + 1) * P],
                                lambda q: latT[:, k, q, half * 512:half * 512 + 512], k == 0, k == KD - 1)
            mm.then_inc(bank_full, 1)


def block_1(nc, ctx_rows, lat_scratch, q_scratch, y_scratch, mask_cols, shared, ctx):
    W = shared

    def sb(name, shape, dt):
        return ctx.enter_context(nc.sbuf_tensor(name, shape, dt))

    def ps(name):
        return ctx.enter_context(nc.psum_tensor(name, [P, 512], F32))

    def sem(name):
        return ctx.enter_context(nc.semaphore(name))

    raw = sb("raw", [P, CH + 1, D], F32)
    keyT = sb("keyT", [P, KD, 2, KEYS], F32R)
    val = sb("val", [P, CH, 2, D], F32R)
    prob = sb("prob", [P, PAIRS, KEYS + 1], F32)
    probT = sb("probT", [P, 3, 2, 512], F32R)
    qkT = sb("qkT", [P, 2, KD, 2, P], F32R)
    outT = sb("outT", [P, KD, 2, 512], F32R)
    ystage = sb("ystage", [P, 2, 4, L], F32)
    q32 = sb("q32", [P, PAIRS, L], F32)
    mask8 = sb("mask8", [P, N], U8)
    xn0 = sb("xn0", [P, D], F32)
    stats = sb("stats", [P, CH + 1, 6], F32)
    small = sb("small", [P, 7, CH + 1], F32)
    shift = sb("shift", [P, CH + 1], F32)
    rstd = sb("rstd", [P, CH + 1], F32)
    x0next = sb("x0next", [P, KD], F32)
    x0T = sb("x0T", [P, KD], F32)
    maxes = sb("maxes", [P, PAIRS, 5], F32)
    negmax = sb("negmax", [P, PAIRS], F32)
    psum_ = sb("psums", [P, PAIRS], F32)
    rsum = sb("rsum", [P, PAIRS], F32)

    s_bank = [ps(f"s_bank{n}") for n in range(4)]
    t_bank = [ps(f"t_bank{n}") for n in range(2)]
    o_bank = [ps(f"o_bank{n}") for n in range(2)]

    rows_in = [sem(f"rows_in{g}") for g in range(5)]
    q_in = sem("q_in")
    mask_in = sem("mask_in")
    stat_done = sem("stat_done")
    rstd_done = sem("rstd_done")
    norm_done = sem("norm_done")
    pool_step = sem("pool_step")
    keys_done = sem("keys_done")
    mask_done = sem("mask_done")
    qblk_high = sem("qblk_high")
    qblk_done = sem("qblk_done")
    t_full = sem("t_full")
    t_high = sem("t_high")
    t_done = sem("t_done")
    k_full, k_high, k_done = sem("k_full"), sem("k_high"), sem("k_done1")
    x0_next = sem("x0_next")
    x0_done = sem("x0_done")
    val_high = sem("val_high")
    val_done = sem("val_done")
    score_full = sem("score_full")
    score_out = sem("score_out")
    max_done = sem("max_done")
    exp_done = sem("exp_done")
    rsum_done = sem("rsum_done")
    prob_done = sem("prob_done")
    pv_done = sem("pv_done")
    out_high = sem("out_high")
    out_done = sem("out_done")
    y_out = [sem(f"y_out{h}") for h in range(2)]

    block = ctx.enter_context(nc.Block())
    NPOOL = 25

    @block.sync
    def _(sp):
        def load_rows(n, index, g):
            if g > 0:
                wait(sp, val_done, n, 4, g - 3)
            if g < 3:
                load = sp.dma_start(raw[:, 4 * g:4 * g + 4, :].rearrange("p c d -> p (c d)"),
                                    ctx_rows[index, 0:TAIL, :].rearrange("(p c) d -> p (c d)", c=CPP)
                                    [:, 4 * g * D:(4 * g + 4) * D])
            else:
                load = sp.dma_start(raw[L:P, 12, :], ctx_rows[index, TAIL:LAST, :])
            load.then_inc(rows_in[g], 16)
            if g == 3:
                sp.dma_start(raw[0:L, 12, :], lat_scratch[index]).then_inc(rows_in[3], 16)

        def load_centre(n, index):
            wait(sp, keys_done, n, 4, 0)
            wait(sp, k_full, n, 8, 0)
            sp.dma_start(raw[:, 13, :], ctx_rows[index, LAST, :].partition_broadcast(P)).then_inc(rows_in[4], 16)

        def load_q_mask(n, index):
            wait(sp, mask_done, n, 2, 0)
            wait(sp, qblk_done, n, 2, 0)
            sp.dma_start(q32[:, :, :], q_scratch[index]).then_inc(q_in, 16)
            sp.dma_start(mask8[:, :], mask_cols[index, :].partition_broadcast(P)).then_inc(mask_in, 16)

        def store_y(b, h, e, index):
            sp.wait_ge(t_done, b.use(e) + 1)
            sp.dma_start(y_scratch[index, :, 4 * h:4 * h + 4, :], ystage[:, h, :, :]).then_inc(y_out[h], 16)

        first = Batch(0)
        load_centre(first, 0)
        for g in range(4):
            load_rows(first, 0, g)
        load_q_mask(first, 0)

        def step(b, x, y):
            nxt = Batch(b.off + 1, b.turn)
            if ("B",) in y:
                load_centre(nxt, nxt.lin(1, 0))
            if ("B",) in y:
                wait(sp, val_done, nxt, 4, -3)
            if ("Y", 0) in x:
                store_y(b, 0, ("Y", 0), b.lin(1, -1))
            if ("B",) in y:
                for g in range(4):
                    load_rows(nxt, nxt.lin(1, 0), g)
            if ("Y", 1) in x + y:
                store_y(b, 1, ("Y", 1), b.lin(1, -1))
            if ("B",) in y:
                load_q_mask(nxt, nxt.lin(1, 0))
        periods(sp, step)
        for h in range(2):
            sp.wait_ge(y_out[h], 16 * B)

    @block.gpsimd
    def _(pool):
        def prepare(n):
            k = [0]

            def link(ins):
                k[0] += 1
                ins.then_inc(pool_step, 1)
                pool.wait_ge(pool_step, n.lin(NPOOL, k[0]))

            def moments(part, cols):
                me, m2e, mo, m2o = (stats[:, cols, q] for q in (1, 2, 4, 5))
                total, diff, both, sq, quarter, var, negmean = (small[:, q, cols] for q in range(7))
                wait(pool, stat_done, n, 14, (9, 14)[part])
                link(pool.tensor_tensor(total, me, mo, ALU.add))
                link(pool.tensor_tensor(diff, me, mo, ALU.subtract))
                link(pool.tensor_tensor(both, m2e, m2o, ALU.add))
                link(apart(pool.tensor_scalar(negmean, total, -0.5, 0.0, ALU.mult, ALU.add), stat_done))
                link(pool.tensor_tensor(sq, diff, diff, ALU.mult))
                link(apart(pool.tensor_scalar(quarter, sq, 0.25, EPS, ALU.mult, ALU.add), stat_done))
                link(apart(pool.tensor_scalar(sq, both, 1.0 / D, 0.0, ALU.mult, ALU.add), stat_done))
                link(pool.tensor_tensor(var, sq, quarter, ALU.add))
                wait(pool, norm_done, n, 14, 0)
                link(pool.tensor_tensor(rstd[:, cols], var, W["neghalf"][:, cols], ALU.pow))
                pool.tensor_tensor(shift[:, cols], rstd[:, cols], negmean, ALU.mult).then_inc(rstd_done, 1)

            def centre(g):
                wait(pool, norm_done, n, 14, 4 * g + 5)
                rows = raw[:, 4 * g:4 * g + 4, :]
                link(pool.tensor_tensor(rows, rows, raw[:, 13:14, :].to_broadcast([P, 4, D]), ALU.subtract))
                pool.tensor_tensor(rows, rows, W["g1"][:, :].unsqueeze(1).to_broadcast([P, 4, D]), ALU.mult
                                   ).then_inc(keys_done, 1)

            moments(0, slice(0, 9))
            wait(pool, norm_done, n, 14, 1)
            if n.off > 0:
                wait(pool, k_full, n, 8, 0)
            link(pool.tensor_tensor(xn0[:, :], raw[:, 13, :], W["g1"][:, :], ALU.mult))
            link(pool.tensor_tensor(xn0[:, :], xn0[:, :], W["b1"][:, :], ALU.add))
            centre(0)
            moments(1, slice(9, CH + 1))
            centre(1)
            centre(2)
            wait(pool, norm_done, n, 14, 14)
            wait(pool, keys_done, n, 4, 3)
            link(pool.tensor_tensor(raw[L:P, 12, :], raw[L:P, 12, :], raw[L:P, 13, :], ALU.subtract))
            link(pool.tensor_tensor(raw[L:P, 12, :], raw[L:P, 12, :], W["g1"][L:P, :], ALU.mult))
            pool.tensor_tensor(raw[0:L, 12, :], raw[0:L, 12, :], xn0[0:L, :], ALU.subtract).then_inc(keys_done, 1)
            wait(pool, keys_done, n, 4, 4)
            assert k[0] == NPOOL

        def mask_bias(n):
            wait(pool, mask_in, n, 16, 16)
            wait(pool, score_out, n, 32, 0)
            apart(pool.tensor_scalar(W["bias"][:, 0:TAIL], mask8[:, 0:TAIL], -NEG, NEG, ALU.mult, ALU.add), stat_done
                  ).then_inc(mask_done, 1)
            pool.tensor_scalar(W["bias"][:, TAIL + L:KEYS + 1], mask8[:, TAIL:N], -NEG, NEG, ALU.mult, ALU.add
                               ).then_inc(mask_done, 1)

        prepare(Batch(0))

        def step(b, x, y):
            if ("Q", 0) in x:
                mask_bias(b)
            if ("B",) in y:
                prepare(Batch(b.off + 1, b.turn))
        periods(pool, step)

    @block.scalar
    def _(act):
        def q_block(n):
            wait(act, q_in, n, 16, 16)
            if n.off > 0:
                act.wait_ge(t_full, Batch(n.off - 1, n.turn).use(("Q", 7)) + 1)
            for h in range(2):
                s = slice(h * L, h * L + L)
                act.activation(W["qblk"][s, :, 0, s], q32[s, :, :], ACT.Copy).then_inc(qblk_high, 1)

        def normalise(n, *chunks):
            wait(act, rstd_done, n, 2, 1 if chunks[-1] < 8 else 2)
            for c in chunks:
                s = slice(L, P) if c == 12 else slice(0, P)
                m = STAT[c]
                act.activation(raw[s, c, :], raw[s, c, :], ACT.Identity, bias=shift[s, m:m + 1], scale=rstd[s, m:m + 1]
                               ).then_inc(norm_done, 1)

        def half(b, events):
            for e in events:
                kind = e[0]
                if kind in "YTQ":
                    act.wait_ge(t_full, b.use(e) + 1)
                    bank = t_bank[b.bank(e)]
                if kind == "Y":
                    wait(act, y_out[e[1]], b, 16, -16)
                    act.activation(ystage[0:L, e[1], :, :],
                                   bank[0:L, :].rearrange("p (a x) -> p a x", a=4)[:, :, 0:L], ACT.Copy).then_inc(t_high, 1)
                if kind == "T":
                    when, c = e[1:]
                    slot, need = value_bank(min(when, 1), c)
                    wait(act, pv_done, b, 26, need - (26 if when == 1 else 0))
                    act.activation(probT[:, slot, 0, :], bank[:, :], ACT.Copy).then_inc(t_high, 1)
                if kind == "Q":
                    wait(act, score_out, b, 32, 4 * e[1] - 4)
                    act.activation(qkT[:, e[1] % 2, :, 0, :], bank[:, 0:KD * P].rearrange("p (k x) -> p k x", k=KD),
                                   ACT.Copy).then_inc(t_high, 1)
                if kind == "K":
                    k, g = e[1:]
                    a, z = GROUPS[g]
                    bank, at = s_bank[K_BANK[g][k]], 2 * P * k if g == 3 else 0
                    wait(act, k_full, b, 8, 8 if g == 3 else 2 * g + k + 1)
                    wait(act, score_out, b, 32, 0)
                    if g == 3:
                        wait(act, x0_done, b, 1, 0)
                        act.activation(x0next[:, k:k + 1], bank[:, at + P:at + P + 1], ACT.Copy).then_inc(x0_next, 1)
                    act.activation(keyT[:, k, 0, a * P:z * P], bank[:, at:at + (z - a) * P], ACT.Copy).then_inc(k_high, 1)
                if kind == "E":
                    i = e[1]
                    wait(act, max_done, b, 8, i + 1)
                    act.activation(prob[:, i, :], prob[:, i, :], ACT.Exp, bias=negmax[:, i:i + 1],
                                   accum_out=psum_[:, i:i + 1]).then_inc(exp_done, 1)
                if kind == "O":
                    h = e[1]
                    wait(act, pv_done, b, 26, 13 * (h + 1) - 26 * h)
                    wait(act, x0_done, b, 1, 1 - h)
                    for k in range(KD):
                        act.activation(outT[:, k, 0, :], o_bank[k][:, :], ACT.Identity, bias=x0T[:, k:k + 1]).then_inc(out_high, 1)
                if kind == "N":
                    g = e[1]
                    a, z = GROUPS[g]
                    wait(act, keys_done, b, 4, g + 1)
                    wait(act, pv_done, b, 26, z - 13)
                    act.activation(val[:, a:z, 0, :], raw[:, a:z, :], ACT.Copy).then_inc(val_high, 1)
                if kind == "H":
                    normalise(Batch(b.off + 1, b.turn), *e[1:])
                if kind == "B":
                    q_block(Batch(b.off + 1, b.turn))

        normalise(Batch(0), 13, *range(8))
        normalise(Batch(0), *range(8, CH))
        q_block(Batch(0))
        periods(act, lambda b, x, y: (half(b, x), half(b, y)))

    @block.vector
    def _(dve):
        def q_block(n):
            for h in range(2):
                s = slice(h * L, h * L + L)
                wait(dve, qblk_high, n, 2, h + 1)
                dve.tensor_tensor(W["qblk"][s, :, 1, s], q32[s, :, :], W["qblk"][s, :, 0, s].bitcast(F32), ALU.subtract
                                  ).then_inc(qblk_done, 1)

        def moments(n, g):
            wait(dve, rows_in[g], n, 32 if g == 3 else 16, 32 if g == 3 else 16)
            for c in range(*GROUPS[g]) if g < 4 else [13]:
                dve.bn_stats(stats[:, STAT[c], :], raw[:, c, :]).then_inc(stat_done, 1)

        def half(b, events):
            for e in events:
                kind = e[0]
                if kind in "YTQ":
                    dve.wait_ge(t_high, b.use(e) + 1)
                    bank = t_bank[b.bank(e)]
                if kind == "Y":
                    wait(dve, y_out[e[1]], b, 16, -16)
                    dve.tensor_copy(ystage[L:P, e[1], :, :],
                                    bank[L:P, :].rearrange("p (a x) -> p a x", a=4)[:, :, L:P]).then_inc(t_done, 1)
                if kind == "T":
                    slot, _ = value_bank(min(e[1], 1), e[2])
                    dve.tensor_tensor(probT[:, slot, 1, :], bank[:, :], probT[:, slot, 0, :].bitcast(F32),
                                      ALU.subtract).then_inc(t_done, 1)
                if kind == "Q":
                    dve.tensor_tensor(qkT[:, e[1] % 2, :, 1, :], bank[:, 0:KD * P].rearrange("p (k x) -> p k x", k=KD),
                                      qkT[:, e[1] % 2, :, 0, :].bitcast(F32), ALU.subtract).then_inc(t_done, 1)
                if kind == "K":
                    k, g = e[1:]
                    a, z = GROUPS[g]
                    bank, at = s_bank[K_BANK[g][k]], 2 * P * k if g == 3 else 0
                    wait(dve, k_high, b, 8, 8 if g == 3 else 2 * g + k + 1)
                    dve.tensor_tensor(keyT[:, k, 1, a * P:z * P], bank[:, at:at + (z - a) * P],
                                      keyT[:, k, 0, a * P:z * P].bitcast(F32), ALU.subtract).then_inc(k_done, 1)
                if kind == "A":
                    i, j = e[1:]
                    if (i, j) == (0, 0):
                        wait(dve, mask_done, b, 2, 2)
                        dve.tensor_copy(maxes[:, :, 4:5], W["bias"][:, KEYS:KEYS + 1].unsqueeze(1).to_broadcast([P, PAIRS, 1]))
                    if j == 0:
                        dve.tensor_copy(prob[:, i, KEYS:KEYS + 1], W["bias"][:, KEYS:KEYS + 1])
                    wait(dve, score_full, b, 32, 4 * i + j + 1)
                    s = slice(j * QTR, (j + 1) * QTR)
                    apart(dve.tensor_tensor_reduce(out=prob[:, i, s], in0=s_bank[j][:, 0:QTR], in1=W["bias"][:, s],
                                                   scale=1.0, scalar=NEG, op0=ALU.add, op1=ALU.max,
                                                   accum_out=maxes[:, i, j:j + 1]), mask_done).then_inc(score_out, 1)
                    if j == 3:
                        wait(dve, score_out, b, 32, 4 * i + 4)
                        dve.tensor_reduce(negmax[:, i:i + 1], maxes[:, i, :], AX.X, ALU.max, negate=True
                                          ).then_inc(max_done, 1)
                if kind == "P":
                    i = e[1]
                    wait(dve, exp_done, b, 8, i + 1)
                    dve.reciprocal(rsum[:, i:i + 1], psum_[:, i:i + 1]).then_inc(rsum_done, 1)
                    wait(dve, rsum_done, b, 8, i + 1)
                    dve.tensor_scalar(prob[:, i, :], prob[:, i, :], rsum[:, i:i + 1], None, ALU.mult).then_inc(prob_done, 1)
                if kind == "O":
                    h = e[1]
                    for k in range(KD):
                        wait(dve, out_high, b, 4, 2 * h + k + 1 - 4 * h)
                        dve.scalar_tensor_tensor(out=outT[:, k, 1, :], in0=o_bank[k][:, :], scalar=x0T[:, k:k + 1],
                                                 in1=outT[:, k, 0, :].bitcast(F32), op0=ALU.add, op1=ALU.subtract
                                                 ).then_inc(out_done, 1)
                if kind == "C":
                    wait(dve, x0_next, b, 2, 2)
                    wait(dve, out_done, b, 4, 0)
                    dve.tensor_copy(x0T[:, :], x0next[:, :]).then_inc(x0_done, 1)
                if kind == "N":
                    g = e[1]
                    a, z = GROUPS[g]
                    wait(dve, val_high, b, 4, g + 1)
                    dve.tensor_tensor(val[:, a:z, 1, :], raw[:, a:z, :], val[:, a:z, 0, :].bitcast(F32), ALU.subtract
                                      ).then_inc(val_done, 1)
                n = Batch(b.off + 1, b.turn)
                if kind == "S":
                    moments(n, e[1])
                if kind == "B":
                    q_block(n)

        for g in (4, 0, 1, 2, 3):
            moments(Batch(0), g)
        q_block(Batch(0))
        periods(dve, lambda b, x, y: (half(b, x), half(b, y)))

    @block.tensor
    def _(pe):
        ident = W["ident"]

        def half(b, events):
            for e in events:
                kind = e[0]
                if kind in "YTQ":
                    bank = t_bank[b.bank(e)]
                    if b.turn is not None or b.off > 0 or b.use(e) >= 2:
                        pe.wait_ge(t_done, b.use(e) - 1)
                if kind == "Y":
                    h = e[1]
                    wait(pe, out_done, b, 4, 2 * h - 2)
                    for a in range(4):
                        pair = 4 * h + a
                        for k in range(KD):
                            mm = split_pair(pe, bank[:, a * P:(a + 1) * P],
                                            lambda q: W["wv"][:, k, q, pair * P:(pair + 1) * P],
                                            lambda q: outT[:, k, q, a * P:(a + 1) * P], k == 0, k == KD - 1)
                    mm.then_inc(t_full, 1)
                if kind == "T":
                    when, c = e[1:]
                    h = min(when, 1)
                    if c == 0:
                        wait(pe, prob_done, b, 8, 4 * h + 4)
                    for t in range(4):
                        mm = pe.transpose(bank[:, t * P:(t + 1) * P], prob[:, 4 * h + t, c * P:(c + 1) * P], ident[:, :])
                    mm.then_inc(t_full, 1)
                if kind == "Q":
                    i = e[1]
                    if i == 0:
                        wait(pe, qblk_done, b, 2, 2)
                    for k in range(KD):
                        mm = split_pair(pe, bank[:, k * P:(k + 1) * P],
                                        lambda q: W["wk"][:, i, q, k * P:(k + 1) * P],
                                        lambda q: W["qblk"][:, i, q, :], True, True)
                    mm.then_inc(t_full, 1)
                if kind == "K":
                    k, g = e[1:]
                    a, z = GROUPS[g]
                    bank, at = s_bank[K_BANK[g][k]], 2 * P * k if g == 3 else 0
                    wait(pe, keys_done, b, 4, g + 1)
                    if (g, k) == (0, 0):
                        wait(pe, score_out, b, 32, 0)
                    if g >= 2:
                        wait(pe, k_done, b, 8, 3 + k if g == 2 else 6)
                    for c in range(a, z):
                        mm = pe.transpose(bank[:, at + (c - a) * P:at + (c - a + 1) * P], raw[:, c, k * P:(k + 1) * P],
                                          ident[:, :])
                    if g == 3:
                        mm = pe.transpose(bank[:, at + P:at + 2 * P], xn0[:, k * P:(k + 1) * P], ident[:, :])
                    if (g, k) == (3, 1):
                        mm.then_inc(k_full, 2)
                    elif g < 3:
                        mm.then_inc(k_full, 1)
                if kind == "A":
                    i, j = e[1:]
                    if j == 0:
                        pe.wait_ge(t_done, b.use(("Q", i)) + 1)
                    if i == 0:
                        wait(pe, k_done, b, 8, 2 * j + 2)
                    wait(pe, score_out, b, 32, 4 * i + j - 3)
                    for k in range(KD):
                        mm = split_pair(pe, s_bank[j][:, 0:QTR], lambda q: qkT[:, i % 2, k, q, :],
                                        lambda q: keyT[:, k, q, j * QTR:(j + 1) * QTR], k == 0, k == KD - 1)
                    mm.then_inc(score_full, 1)
                if kind == "V":
                    h, c = e[1:]
                    slot, _ = value_bank(h, c)
                    if h == 1 and c < 2:
                        pe.wait_ge(t_done, Batch(b.off - 1, b.turn).use(("T", 2, c)) + 1)
                    else:
                        pe.wait_ge(t_done, b.use(("T", h, c)) + 1)
                    if h == 0 and c % 4 == 0:
                        wait(pe, val_done, b, 4, c // 4 + 1)
                    for k in range(KD):
                        if c == 0:
                            wait(pe, out_done, b, 4, k - 1 - 2 * h)
                        mm = split_pair(pe, o_bank[k][:, :], lambda q: val[:, c, q, k * P:(k + 1) * P],
                                        lambda q: probT[:, slot, q, :], c == 0, c == CH - 1)
                    mm.then_inc(pv_done, 1)
        periods(pe, lambda b, x, y: (half(b, x), half(b, y)))


def constants(nc, ctx):
    return {"ident": ctx.enter_context(nc.sbuf_tensor("ident", [P, P], F32)),
            "neghalf": ctx.enter_context(nc.sbuf_tensor("neghalf", [P, 16], F32))}


def shared(nc, ctx):
    def sb(name, shape, dt):
        return ctx.enter_context(nc.sbuf_tensor(name, shape, dt))

    return {
        "g1": sb("g1", [P, D], F32),
        "b1": sb("b1", [P, D], F32),
        "bias": sb("bias", [P, KEYS + 1], BF16),
        "qblk": sb("qblk", [P, PAIRS, 2, P], F32R),
        "wk": sb("wk", [P, PAIRS, 2, D], F32R),
        "wv": sb("wv", [P, KD, 2, INNER], F32R),
    }


def block_2(nc, ins, y_scratch, x2, xn2T, W, ctx):
    def sb(name, shape, dt):
        return ctx.enter_context(nc.sbuf_tensor(name, shape, dt))

    def sem(name):
        return ctx.enter_context(nc.semaphore(name))

    H, DH = 16, D // 16
    yraw = sb("yraw", [P, 2, 2, PAIRS, L], F32)
    ysplit = sb("ysplit", [P, 2, 2, PAIRS, 2, L], F32R)
    xin = sb("xin", [P, RT, D], F32)
    x1 = sb("x1", [P, RT, D], F32)
    xn = sb("xn", [P, 2, D], F32)
    xnT = sb("xnT", [P, 2, 2, KD, 2 * P], F32R)
    wout = sb("wout", [P, PAIRS, 2, D], F32R)
    wqk = sb("wqk", [P, KD, 2, 2 * D], F32R)
    wv = sb("wv_self", [P, KD, 2, D], F32R)
    wo = sb("wo_self", [P, KD, 2, D], F32R)
    wtmp = sb("wtmp", [P, PAIRS * D + 4 * KD * D], F32)
    bqk = sb("bqk", [P, 2 * D], F32)
    bv = sb("bv", [P, D], F32)
    bo = sb("bo", [P, D], F32)
    rot = sb("rot", [P, 2, 8], F32)
    causal = sb("causal", [P, L], F32)
    headmask = sb("headmask", [P, 8], F32)
    vmask = sb("vmask", [P, D], F32)
    qk = sb("qk", [P, 2, 2 * D], F32)
    rc = sb("rc", [P, 2, 2 * D], F32)
    rs = sb("rs", [P, 2, 2 * D], F32)
    rqk = sb("rqk", [P, 2, 2 * D], F32)
    vblk = sb("vblk", [P, 2, 2, D], F32)
    qT = sb("qT", [P, 2, 2, P], F32)
    kblk = sb("kblk", [P, 2, 2, 2, 8, L], F32)
    sc = sb("sc", [P, 2, H, L], F32)
    mx = sb("mx", [P, 2, H], F32)
    sm = sb("sm", [P, 2, H], F32)
    rsm = sb("rsm", [P, 2, H], F32)
    pt = sb("pt", [P, 2, PAIRS, P], F32)
    att = sb("att", [P, 2, D], F32)
    attT = sb("attT", [P, 2, KD, 2, P], F32R)
    xn2 = sb("xn2", [P, 2, D], F32)
    st = sb("st2", [P, 2, 2, 6], F32)
    mv = sb("mv2", [P, 2, 2, 2], F32)
    ve = sb("ve2", [P, 2, 2], F32)
    rstd = sb("rstd2", [P, 2, 2], F32)
    bank = [ctx.enter_context(nc.psum_tensor(f"bank2_{n}", [P, 512], F32)) for n in range(8)]

    w_in = sem("w2_in")
    c_in = sem("c2_in")
    x_in = sem("x2_in")
    y_in = [sem(f"y2_in{n}") for n in range(2)]
    wh_done, wl_done = sem("w2_high"), sem("w2_low")
    pool_mask = sem("pool_mask")
    names = ("y_high y_low x1_full x1_done a_stat a_rstd xn_done xnT_full xnT_high xnT_low qk_full v_full qk_biased v_masked "
             "rot_cs rot_done v_done x1b_done r_full qT_done k_done s_full s_max s_exp sum_done p_full p_out pv_full att_done "
             "attT_full attT_high attT_low o_full x2_done d_stat d_rstd xn2_done xn2T_full xn2T_high xn2T_low").split()
    S = {n: sem(n) for n in names}
    own = {n: sem(f"own_{n}") for n in ("dve", "pool")}

    def stages(run):
        for s in range(-1, RT + 3):
            for name, lag in (("a0", -1), ("c1", 2), ("a1", 0), ("d1", 3), ("b1", 1), ("c2", 2), ("a2", 0), ("d2", 3),
                              ("b2", 1), ("c3", 2), ("d3", 3)):
                if 0 <= s - lag < RT:
                    run(name, s - lag)

    def twice(ap):
        return ap.rearrange("p (a l) -> p a l", l=L).unsqueeze(2).to_broadcast([P, 2 * KD, 2, L])

    def doubled(ap):
        return ap.rearrange("p k (b u l) -> p (k b) u l", b=2, u=2)

    class Chain:

        def __init__(self, eng, sem_):
            self.eng, self.sem, self.n = eng, sem_, 0

        def __call__(self, ins):
            self.n += 1
            ins.then_inc(self.sem, 1)
            self.eng.wait_ge(self.sem, self.n)

    weights = []
    at = 0
    for name, to, k in (("wout", wout, PAIRS), ("wqk", wqk, KD), ("wvs", wv, KD), ("wos", wo, KD)):
        n = to.shape[-1]
        weights.append((name, wtmp[:, at:at + k * n].rearrange("p (k n) -> p k n", k=k), to))
        at += k * n

    block = ctx.enter_context(nc.Block())

    @block.sync
    def _(sp):
        for name, tmp, _ in weights:
            sp.dma_start(tmp, ins[name].rearrange("(k p) n -> p k n", p=P)).then_inc(w_in, 16)

        def load_y(rt):
            if rt >= 2:
                sp.wait_ge(S["y_low"], rt - 1)
            sp.dma_start(yraw[:, rt % 2, :, :, :].rearrange("p b a l -> p b (a l)"),
                         y_scratch[2 * rt:2 * rt + 2].rearrange("b p a l -> p b (a l)")).then_inc(y_in[rt % 2], 16)
        load_y(0)
        load_y(1)
        sp.dma_start(xin[:, :, :], ins["x"].rearrange("(t p) d -> p t d", p=P)).then_inc(x_in, 16)
        for to, name in ((bqk, "bqk"), (bv, "bv"), (bo, "bo")):
            sp.dma_start(to[:, :], ins[name].partition_broadcast(P)).then_inc(c_in, 16)
        sp.dma_start(rot[:, :, :], ins["rot"]).then_inc(c_in, 16)
        for to, name in ((causal, "causal"), (headmask, "headmask"), (vmask, "vmask")):
            sp.dma_start(to[:, :], ins[name]).then_inc(c_in, 16)
        for rt in range(2, RT):
            load_y(rt)

    @block.scalar
    def _(act):
        for _, tmp, to in weights:
            act.wait_ge(w_in, 16 * len(weights))
            act.activation(to[:, :, 0, :], tmp, ACT.Copy).then_inc(wh_done, 1)

        def run(name, t):
            z = t % 2
            if name == "a0":
                act.wait_ge(y_in[z], 16 * (t // 2 + 1))
                if t >= 2:
                    act.wait_ge(S["x1_full"], t - 1)
                act.activation(ysplit[:, z, 0, :, :, :], yraw[:, z, :, :, :].rearrange("p b a l -> p a b l"), ACT.Copy).then_inc(S["y_high"], 1)
            if name == "a2":
                act.wait_ge(S["xnT_full"], t + 1)
                if t >= 2:
                    act.wait_ge(S["v_full"], t - 1)
                act.activation(doubled(xnT[:, z, 0, :, :]), twice(bank[1][:, 0:D]), ACT.Copy
                               ).then_inc(S["xnT_high"], 1)
            if name == "b2":
                act.wait_ge(S["r_full"], t + 1)
                if t >= 2:
                    act.wait_ge(S["s_full"], t - 1)
                act.activation(qT[:, z, :, :], bank[2][:, 0:D].rearrange("p (k x) -> p k x", k=KD), ACT.Copy
                               ).then_inc(S["qT_done"], 1)
            if name == "c1":
                act.wait_ge(S["s_max"], t + 1)
                act.activation(sc[:, z, :, :], sc[:, z, :, :], ACT.Exp, scale=DH ** -0.5).then_inc(S["s_exp"], 1)
            if name == "c2":
                for r in range(2):
                    act.wait_ge(S["p_full"], 2 * t + r + 1)
                    if t >= 2:
                        act.wait_ge(S["pv_full"], t - 1)
                    act.activation(pt[:, z, 4 * r:4 * r + 4, :], bank[(6, 4)[r]][:, :].rearrange("p (a x) -> p a x", a=4),
                                   ACT.Copy).then_inc(S["p_out"], 1)
            if name == "d1":
                act.wait_ge(S["attT_full"], t + 1)
                if t >= 2:
                    act.wait_ge(S["o_full"], t - 1)
                act.activation(attT[:, z, :, 0, :], bank[7][:, 0:D].rearrange("p (k x) -> p k x", k=KD), ACT.Copy
                               ).then_inc(S["attT_high"], 1)
            if name == "d3":
                act.wait_ge(S["xn2T_full"], t + 1)
                act.activation(xn2T[:, :, 0, t * P:(t + 1) * P], bank[7][:, 0:D].rearrange("p (k x) -> p k x", k=KD),
                               ACT.Copy).then_inc(S["xn2T_high"], 1)
        stages(run)

    @block.gpsimd
    def _(pool):
        link = Chain(pool, own["pool"])
        pool.wait_ge(c_in, 16 * 7)
        pool.tensor_tensor(bv[:, :], bv[:, :], vmask[:, :], ALU.mult).then_inc(pool_mask, 1)
        pool.wait_ge(pool_mask, 1)

        def moments(chain, z, t, stat, done):
            pool.wait_ge(S[stat], t + 1)
            link(pool.tensor_scalar(ve[:, chain, z:z + 1], mv[:, chain, z, 1:2], 1.0, EPS, ALU.mult, ALU.add))
            pool.tensor_tensor(rstd[:, chain, z:z + 1], ve[:, chain, z:z + 1], W["neghalf"][:, 0:1], ALU.pow
                               ).then_inc(S[done], 1)

        def run(name, t):
            z = t % 2
            if name == "a1":
                moments(0, z, t, "a_stat", "a_rstd")
            if name == "b1":
                pool.wait_ge(S["qk_biased"], t + 1)
                if t >= 2:
                    pool.wait_ge(S["r_full"], t - 1)
                cos, sin = (rot[:, n, :].unsqueeze(1).to_broadcast([P, 64, 8]) for n in range(2))
                src = qk[:, z, :].rearrange("p (a i) -> p a i", i=8)
                link(pool.tensor_tensor(rc[:, z, :].rearrange("p (a i) -> p a i", i=8), src, cos, ALU.mult))
                link(pool.tensor_tensor(rs[:, z, :].rearrange("p (a i) -> p a i", i=8), src, sin, ALU.mult))
                c, s, r = (m[:, z, :].rearrange("p (h two i) -> p h two i", two=2, i=8) for m in (rc, rs, rqk))
                pool.tensor_tensor(r[:, :, 0, :], c[:, :, 0, :], s[:, :, 1, :], ALU.subtract).then_inc(S["rot_done"], 1)
                pool.tensor_tensor(r[:, :, 1, :], s[:, :, 0, :], c[:, :, 1, :], ALU.add).then_inc(S["rot_done"], 1)
                pool.wait_ge(S["v_masked"], t + 1)
                pool.tensor_tensor(vblk[:, z, :, :], vblk[:, z, :, :], bv[:, :].unsqueeze(1).to_broadcast([P, 2, D]), ALU.add
                                   ).then_inc(S["v_done"], 1)
                pool.wait_ge(S["xn_done"], t + 1)
                pool.tensor_tensor(x1[:, t, :], x1[:, t, :], bo[:, :], ALU.add).then_inc(S["x1b_done"], 1)
            if name == "d2":
                moments(1, z, t, "d_stat", "d_rstd")
        stages(run)

    @block.vector
    def _(dve):
        link = Chain(dve, own["dve"])
        for n, (_, tmp, to) in enumerate(weights):
            dve.wait_ge(wh_done, n + 1)
            dve.tensor_tensor(to[:, :, 1, :], tmp, to[:, :, 0, :].bitcast(F32), ALU.subtract).then_inc(wl_done, 1)
        dve.wait_ge(c_in, 16 * 7)
        dve.wait_ge(x_in, 16)

        def low(to, src, high, done):
            dve.tensor_tensor(to, src, high.bitcast(F32), ALU.subtract).then_inc(S[done], 1)

        def run(name, t):
            z = t % 2
            if name == "a0":
                dve.wait_ge(S["y_high"], t + 1)
                low(ysplit[:, z, 1, :, :, :], yraw[:, z, :, :, :].rearrange("p b a l -> p a b l"), ysplit[:, z, 0, :, :, :], "y_low")
            if name == "a1":
                dve.wait_ge(S["x1_full"], t + 1)
                dve.tensor_tensor(x1[:, t, :], bank[0][:, 0:D], xin[:, t, :], ALU.add).then_inc(S["x1_done"], 1)
                dve.wait_ge(S["x1_done"], t + 1)
                link(dve.bn_stats(st[:, 0, z, :], x1[:, t, :]))
                dve.bn_aggr(mv[:, 0, z, :], st[:, 0, z, :]).then_inc(S["a_stat"], 1)
            if name == "a2":
                dve.wait_ge(S["a_rstd"], t + 1)
                if t >= 2:
                    dve.wait_ge(S["xnT_full"], t - 1)
                dve.tensor_scalar(xn[:, z, :], x1[:, t, :], mv[:, 0, z, 0:1], rstd[:, 0, z:z + 1], ALU.subtract, ALU.mult
                                  ).then_inc(S["xn_done"], 1)
                dve.wait_ge(S["xnT_high"], t + 1)
                low(doubled(xnT[:, z, 1, :, :]), twice(bank[1][:, 0:D]), doubled(xnT[:, z, 0, :, :]), "xnT_low")
            if name == "b1":
                dve.wait_ge(S["qk_full"], t + 1)
                if t >= 2:
                    dve.wait_ge(S["rot_done"], 2 * t - 2)
                dve.tensor_tensor(qk[:, z, :], bank[2][:, :], bqk[:, :], ALU.add).then_inc(S["qk_biased"], 1)
                dve.wait_ge(S["v_full"], t + 1)
                if t >= 2:
                    dve.wait_ge(S["pv_full"], t - 1)
                dve.tensor_tensor(vblk[:, z, :, :], bank[3][:, :].rearrange("p (b d) -> p b d", b=2),
                                  vmask[:, :].unsqueeze(1).to_broadcast([P, 2, D]), ALU.mult).then_inc(S["v_masked"], 1)
            if name == "b2":
                dve.wait_ge(S["qT_done"], t + 1)
                for j in range(2):
                    for b in range(2):
                        src = bank[2][:, D + j * P + b * L:D + j * P + b * L + L]
                        dve.tensor_tensor(kblk[:, z, j, b, :, :], src.unsqueeze(1).to_broadcast([P, 8, L]),
                                          headmask[:, :].unsqueeze(2).to_broadcast([P, 8, L]), ALU.mult).then_inc(S["k_done"], 1)
            if name == "c1":
                dve.wait_ge(S["s_full"], t + 1)
                for j in range(2):
                    link(dve.tensor_tensor(sc[:, z, 8 * j:8 * j + 8, :], bank[4 + j][:, :].rearrange("p (h s) -> p h s", h=8),
                                           causal[:, :].unsqueeze(1).to_broadcast([P, 8, L]), ALU.add))
                link(dve.tensor_reduce(mx[:, z, :], sc[:, z, :, :], AX.X, ALU.max))
                dve.tensor_tensor(sc[:, z, :, :], sc[:, z, :, :], mx[:, z, :].unsqueeze(2).to_broadcast([P, H, L]),
                                  ALU.subtract).then_inc(S["s_max"], 1)
            if name == "c2":
                dve.wait_ge(S["s_exp"], t + 1)
                link(dve.tensor_reduce(sm[:, z, :], sc[:, z, :, :], AX.X, ALU.add))
                dve.reciprocal(rsm[:, z, :], sm[:, z, :]).then_inc(S["sum_done"], 1)
            if name == "c3":
                dve.wait_ge(S["sum_done"], t + 1)
                dve.wait_ge(S["pv_full"], t + 1)
                if t >= 2:
                    dve.wait_ge(S["attT_full"], t - 1)
                dve.tensor_tensor(att[:, z, :].rearrange("p (h i) -> p h i", h=H), bank[5][:, 0:D].rearrange("p (h i) -> p h i", h=H),
                                  rsm[:, z, :].unsqueeze(2).to_broadcast([P, H, DH]), ALU.mult).then_inc(S["att_done"], 1)
            if name == "d1":
                dve.wait_ge(S["attT_high"], t + 1)
                low(attT[:, z, :, 1, :], bank[7][:, 0:D].rearrange("p (k x) -> p k x", k=KD), attT[:, z, :, 0, :], "attT_low")
            if name == "d2":
                dve.wait_ge(S["o_full"], t + 1)
                dve.wait_ge(S["x1b_done"], t + 1)
                dve.tensor_tensor(x2[:, t, :], bank[7][:, 0:D], x1[:, t, :], ALU.add).then_inc(S["x2_done"], 1)
                dve.wait_ge(S["x2_done"], t + 1)
                link(dve.bn_stats(st[:, 1, z, :], x2[:, t, :]))
                dve.bn_aggr(mv[:, 1, z, :], st[:, 1, z, :]).then_inc(S["d_stat"], 1)
            if name == "d3":
                dve.wait_ge(S["d_rstd"], t + 1)
                dve.tensor_scalar(xn2[:, z, :], x2[:, t, :], mv[:, 1, z, 0:1], rstd[:, 1, z:z + 1], ALU.subtract, ALU.mult
                                  ).then_inc(S["xn2_done"], 1)
                dve.wait_ge(S["xn2T_high"], t + 1)
                low(xn2T[:, :, 1, t * P:(t + 1) * P], bank[7][:, 0:D].rearrange("p (k x) -> p k x", k=KD),
                    xn2T[:, :, 0, t * P:(t + 1) * P], "xn2T_low")
        stages(run)

    @block.tensor
    def _(pe):
        ident = W["ident"]
        pe.wait_ge(wl_done, len(weights))

        def run(name, t):
            z = t % 2
            if name == "a1":
                pe.wait_ge(S["y_low"], t + 1)
                if t >= 1:
                    pe.wait_ge(S["x1_done"], t)
                for a in range(PAIRS):
                    mm = split_pair(pe, bank[0][:, 0:D], lambda q: ysplit[:, z, q, a, :, :].rearrange("p b l -> p (b l)"),
                                    lambda q: wout[:, a, q, :], a == 0, a == PAIRS - 1)
                mm.then_inc(S["x1_full"], 1)
            if name == "a2":
                pe.wait_ge(S["xn_done"], t + 1)
                if t >= 1:
                    pe.wait_ge(S["xnT_low"], t)
                for k in range(KD):
                    mm = pe.transpose(bank[1][:, k * P:(k + 1) * P], xn[:, z, k * P:(k + 1) * P], ident[:, :])
                mm.then_inc(S["xnT_full"], 1)
            if name == "b1":
                pe.wait_ge(S["xnT_low"], t + 1)
                if t >= 1:
                    pe.wait_ge(S["k_done"], 4 * t)
                for k in range(KD):
                    mm = split_pair(pe, bank[2][:, :], lambda q: xnT[:, z, q, k, L:L + P], lambda q: wqk[:, k, q, :],
                                    k == 0, k == KD - 1)
                mm.then_inc(S["qk_full"], 1)
                if t >= 1:
                    pe.wait_ge(S["v_masked"], t)
                for b in range(2):
                    for k in range(KD):
                        mm = split_pair(pe, bank[3][:, b * D:(b + 1) * D],
                                        lambda q: xnT[:, z, q, k, b * P:(b + 1) * P],
                                        lambda q: wv[:, k, q, :], k == 0, k == KD - 1)
                mm.then_inc(S["v_full"], 1)
            if name == "b2":
                pe.wait_ge(S["rot_done"], 2 * t + 2)
                pe.wait_ge(S["qk_biased"], t + 1)
                for n in range(4):
                    mm = pe.transpose(bank[2][:, n * P:(n + 1) * P], rqk[:, z, n * P:(n + 1) * P], ident[:, :])
                mm.then_inc(S["r_full"], 1)
            if name == "c1":
                pe.wait_ge(S["k_done"], 4 * t + 4)
                if t >= 1:
                    pe.wait_ge(S["p_out"], 2 * t)
                    pe.wait_ge(S["att_done"], t)
                for j in range(2):
                    for b in range(2):
                        mm = pe.matmul(bank[4 + j][b * L:(b + 1) * L, :], qT[:, z, j, b * L:(b + 1) * L],
                                       kblk[:, z, j, b, :, :].rearrange("p h s -> p (h s)"), start=True, stop=True)
                mm.then_inc(S["s_full"], 1)
            if name == "c2":
                pe.wait_ge(S["s_exp"], t + 1)
                if t >= 1:
                    pe.wait_ge(S["p_out"], 2 * t - 1)
                for r in range(2):
                    for a in range(4):
                        hh = 8 * r + 2 * a
                        mm = pe.transpose(bank[(6, 4)[r]][:, a * P:(a + 1) * P],
                                          sc[:, z, hh:hh + 2, :].rearrange("p h s -> p (h s)"), ident[:, :])
                    mm.then_inc(S["p_full"], 1)
            if name == "c3":
                pe.wait_ge(S["p_out"], 2 * t + 2)
                pe.wait_ge(S["v_done"], t + 1)
                for b in range(2):
                    for a in range(PAIRS):
                        mm = pe.matmul(bank[5][b * L:(b + 1) * L, a * 32:(a + 1) * 32], pt[:, z, a, b * L:(b + 1) * L],
                                       vblk[:, z, b, a * 32:(a + 1) * 32], start=True, stop=True)
                mm.then_inc(S["pv_full"], 1)
            if name == "d1":
                pe.wait_ge(S["att_done"], t + 1)
                if t >= 1:
                    pe.wait_ge(S["xn2T_low"], t)
                for k in range(KD):
                    mm = pe.transpose(bank[7][:, k * P:(k + 1) * P], att[:, z, k * P:(k + 1) * P], ident[:, :])
                mm.then_inc(S["attT_full"], 1)
            if name == "d2":
                pe.wait_ge(S["attT_low"], t + 1)
                for k in range(KD):
                    mm = split_pair(pe, bank[7][:, 0:D], lambda q: attT[:, z, k, q, :], lambda q: wo[:, k, q, :],
                                    k == 0, k == KD - 1)
                mm.then_inc(S["o_full"], 1)
            if name == "d3":
                pe.wait_ge(S["xn2_done"], t + 1)
                for k in range(KD):
                    mm = pe.transpose(bank[7][:, k * P:(k + 1) * P], xn2[:, z, k * P:(k + 1) * P], ident[:, :])
                mm.then_inc(S["xn2T_full"], 1)
        stages(run)


E4, HID = 4, 1024
HT = HID // P


def block_3(nc, ins, out, x2, xn2T, ctx):
    def sb(name, shape, dt):
        return ctx.enter_context(nc.sbuf_tensor(name, shape, dt))

    def sem(name):
        return ctx.enter_context(nc.semaphore(name))

    w1raw = sb("w1raw", [P, KD, HID], F32)
    w2raw = sb("w2raw", [P, HT, D], F32)
    w1 = sb("w1", [P, KD, 2, HID], F32R)
    w2 = sb("w2", [P, HT, 2, D], F32R)
    b1 = sb("b1e", [P, 2, HT], F32)
    b2 = sb("b2e", [P, E4, D], F32)
    gb = sb("gb", [P, HT], F32)
    gbs = sb("gbs", [P, 2, HT, P], F32R)
    hid = sb("hid", [P, 3, 512], F32)
    hT = sb("hT", [P, HT, 2, ROWS], F32R)
    cexp = sb("cexp", [P, D], F32)
    csum = sb("csum", [P, D], F32)
    ydiff = sb("ydiff", [P, 2, D], F32)
    wrraw = sb("wrraw", [P, KD, E4], F32)
    wr = sb("wr", [P, KD, 2, E4], F32R)
    br = sb("br", [P, E4], F32)
    logit = sb("logit", [P, RT, E4], F32)
    rank = sb("rank", [P, RT, E4], F32)
    cmp = sb("cmp", [P, RT, E4], F32)
    top = sb("top", [P, RT], F32)
    gate = sb("gate", [P, RT, E4], F32)
    gsum = sb("gsum", [P, RT], F32)
    gcur = sb("gcur", [P, RT], F32)
    hbank = [ctx.enter_context(nc.psum_tensor(f"hbank{n}", [P, 512], F32)) for n in range(3)]
    ybank = [ctx.enter_context(nc.psum_tensor(f"ybank{n}", [P, 512], F32)) for n in range(3)]
    rbank = ctx.enter_context(nc.psum_tensor("rbank", [P, 512], F32))

    r_in = sem("r_in")
    b2_in = sem("b2_in")
    w1_in, w2_in, b1_in = sem("w1_in"), sem("w2_in3"), sem("b1_in")
    wr_high, wr_done = sem("wr_high"), sem("wr_done")
    r_full = sem("router_full")
    g_max, g_exp, g_done = sem("g_max"), sem("g_exp"), sem("g_done")
    own = sem("own_dve3")
    w1_high, w1_done = sem("w1_high"), sem("w1_done")
    w2_high, w2_done = sem("w2_high3"), sem("w2_done3")
    gb_done, gb_high, gb_low = sem("gb_done"), sem("gb_high"), sem("gb_low")
    h_full = sem("h_full")
    h_gelu = sem("h_gelu")
    h_high = sem("h_high")
    h_done = sem("h_done")
    y_full = sem("y_full")
    y_got = sem("y_got")
    y_add = sem("y_add")
    c_add = sem("c_add")
    g_cur = sem("g_cur")
    fin_done = sem("fin_done")
    out_done3 = sem("out_done3")

    def experts(eng, body):
        body(Batch(0), True)
        with eng.Fori(0, E4 - 2) as turn:
            body(Batch(1, turn), True)
        body(Batch(E4 - 1), False)

    block = ctx.enter_context(nc.Block())

    @block.sync
    def _(sp):
        def load_w1(n):
            wait(sp, w1_done, n, 1, 0)
            sp.dma_start(w1raw[:, :, :], ins["w1"][n.lin(1, 0)].rearrange("(k p) n -> p k n", p=P)).then_inc(w1_in, 16)

        def load_w2(n):
            wait(sp, w2_done, n, 1, 0)
            sp.dma_start(w2raw[:, :, :], ins["w2"][n.lin(1, 0)].rearrange("(k p) n -> p k n", p=P)).then_inc(w2_in, 16)
            wait(sp, h_gelu, n, 16, 0)
            wait(sp, gb_done, n, 1, 0)
            sp.dma_start(b1[:, 0, :], ins["b1"][n.lin(1, 0)]).then_inc(b1_in, 16)

        sp.dma_start(wrraw[:, :, :], ins["wr"].rearrange("(k p) n -> p k n", p=P)).then_inc(r_in, 16)
        sp.dma_start(br[:, :], ins["br"].partition_broadcast(P)).then_inc(r_in, 16)
        load_w1(Batch(0))
        load_w2(Batch(0))
        sp.dma_start(b2[:, :, :].rearrange("p e d -> p (e d)"), ins["b2e"].partition_broadcast(P)).then_inc(b2_in, 16)

        def body(e, more):
            if more:
                n = Batch(e.off + 1, e.turn)
                load_w1(n)
                load_w2(n)
        experts(sp, body)
        for t in range(RT):
            sp.wait_ge(fin_done, t + 1)
            sp.dma_start(out[t * P:(t + 1) * P, :], x2[:, t, :]).then_inc(out_done3, 16)
        sp.wait_ge(out_done3, 16 * RT)

    @block.scalar
    def _(act):
        def split_w1(e):
            wait(act, w1_in, e, 16, 16)
            wait(act, h_full, e, 16, 0)
            act.activation(w1[:, :, 0, :], w1raw[:, :, :], ACT.Copy).then_inc(w1_high, 1)

        act.wait_ge(r_in, 32)
        act.activation(wr[:, :, 0, :], wrraw[:, :, :], ACT.Copy).then_inc(wr_high, 1)
        act.wait_ge(g_max, 1)
        act.activation(gate[:, :, :], gate[:, :, :], ACT.Exp).then_inc(g_exp, 1)
        split_w1(Batch(0))

        def body(e, more):
            wait(act, b1_in, e, 16, 16)
            act.activation(gb[:, :], b1[:, 0, :], ACT.Gelu).then_inc(gb_done, 1)
            wait(act, w2_in, e, 16, 16)
            wait(act, y_full, e, 9, 0)
            wait(act, gb_done, e, 1, 1)
            act.activation(gbs[:, 0, :, :], gb[:, :].unsqueeze(2).to_broadcast([P, HT, P]), ACT.Copy).then_inc(gb_high, 1)
            for m in range(2 * HT):
                half, t = divmod(m, HT)
                z = m % 2
                s = slice(half * 512, half * 512 + 512)
                wait(act, h_full, e, 16, m + 1)
                wait(act, h_done, e, 16, m - 1)
                act.activation(hid[:, z, :], hbank[z][:, :], ACT.Gelu, bias=b1[:, 0, t:t + 1]).then_inc(h_gelu, 1)
                wait(act, h_gelu, e, 16, m + 1)
                act.activation(hT[:, t, 0, s], hid[:, z, :], ACT.Copy).then_inc(h_high, 1)
                if m == 3:
                    act.activation(w2[:, :, 0, :], w2raw[:, :, :], ACT.Copy).then_inc(w2_high, 1)
            if more:
                split_w1(Batch(e.off + 1, e.turn))
        experts(act, body)

    @block.vector
    def _(dve):
        chain = [0]

        def link(ins):
            chain[0] += 1
            ins.then_inc(own, 1)
            dve.wait_ge(own, chain[0])

        def split_w1(e):
            wait(dve, w1_high, e, 1, 1)
            dve.tensor_tensor(w1[:, :, 1, :], w1raw[:, :, :], w1[:, :, 0, :].bitcast(F32), ALU.subtract).then_inc(w1_done, 1)

        dve.wait_ge(wr_high, 1)
        dve.tensor_tensor(wr[:, :, 1, :], wrraw[:, :, :], wr[:, :, 0, :].bitcast(F32), ALU.subtract).then_inc(wr_done, 1)
        dve.wait_ge(r_full, 1)
        dve.wait_ge(r_in, 32)
        link(dve.tensor_tensor(logit[:, :, :], rbank[:, 0:RT * E4].rearrange("p (t e) -> p t e", e=E4),
                               br[:, :].unsqueeze(1).to_broadcast([P, RT, E4]), ALU.add))
        for e in range(E4):
            mine = logit[:, :, e:e + 1].to_broadcast([P, RT, E4])
            link(dve.tensor_tensor(cmp[:, :, :], logit[:, :, :], mine, ALU.is_gt))
            if e:
                link(dve.tensor_tensor(cmp[:, :, 0:e], logit[:, :, 0:e], logit[:, :, e:e + 1].to_broadcast([P, RT, e]), ALU.is_ge))
            link(dve.tensor_reduce(rank[:, :, e:e + 1], cmp[:, :, :], AX.X, ALU.add))
        link(dve.tensor_scalar(rank[:, :, :], rank[:, :, :], 2.0, None, ALU.is_lt))
        link(dve.tensor_reduce(top[:, :], logit[:, :, :], AX.X, ALU.max))
        dve.tensor_tensor(gate[:, :, :], logit[:, :, :], top[:, :].unsqueeze(2).to_broadcast([P, RT, E4]), ALU.subtract
                          ).then_inc(g_max, 1)
        dve.wait_ge(g_exp, 1)
        link(dve.tensor_tensor(gate[:, :, :], gate[:, :, :], rank[:, :, :], ALU.mult))
        link(dve.tensor_reduce(gsum[:, :], gate[:, :, :], AX.X, ALU.add))
        link(dve.reciprocal(gsum[:, :], gsum[:, :]))
        link(dve.tensor_tensor(gate[:, :, :], gate[:, :, :], gsum[:, :].unsqueeze(2).to_broadcast([P, RT, E4]), ALU.mult))
        dve.wait_ge(b2_in, 16)
        link(dve.tensor_tensor(b2[:, 0, :], b2[:, 0, :], b2[:, 1, :], ALU.add))
        link(dve.tensor_tensor(b2[:, 2, :], b2[:, 2, :], b2[:, 3, :], ALU.add))
        dve.tensor_tensor(csum[:, :], b2[:, 0, :], b2[:, 2, :], ALU.add).then_inc(c_add, 1)
        split_w1(Batch(0))

        def body(e, more):
            wait(dve, gb_high, e, 1, 1)
            dve.tensor_tensor(gbs[:, 1, :, :], gb[:, :].unsqueeze(2).to_broadcast([P, HT, P]), gbs[:, 0, :, :].bitcast(F32),
                              ALU.subtract).then_inc(gb_low, 1)
            wait(dve, y_add, e, 8, 0)
            dve.tensor_copy(gcur[:, :], gate[:, :, e.lin(1, 0)]).then_inc(g_cur, 1)
            for m in range(2 * HT):
                half, t = divmod(m, HT)
                s = slice(half * 512, half * 512 + 512)
                wait(dve, h_high, e, 16, m + 1)
                dve.tensor_tensor(hT[:, t, 1, s], hid[:, m % 2, :], hT[:, t, 0, s].bitcast(F32), ALU.subtract).then_inc(h_done, 1)
                if m == 3:
                    wait(dve, w2_high, e, 1, 1)
                    dve.tensor_tensor(w2[:, :, 1, :], w2raw[:, :, :], w2[:, :, 0, :].bitcast(F32), ALU.subtract
                                      ).then_inc(w2_done, 1)
            if more:
                split_w1(Batch(e.off + 1, e.turn))
            wait(dve, y_full, e, 9, 1)
            dve.tensor_copy(cexp[:, :], ybank[0][:, 0:D]).then_inc(y_got, 1)
            wait(dve, y_got, e, 9, 1)
            wait(dve, c_add, e, 1, 1)
            dve.tensor_tensor(csum[:, :], csum[:, :], cexp[:, :], ALU.add).then_inc(c_add, 1)
            wait(dve, g_cur, e, 1, 1)
            for t in range(RT):
                wait(dve, y_full, e, 9, t + 2)
                wait(dve, y_add, e, 8, t - 1)
                dve.tensor_tensor(ydiff[:, t % 2, :], ybank[(t + 1) % 3][:, 0:D], cexp[:, :], ALU.subtract).then_inc(y_got, 1)
                wait(dve, y_got, e, 9, t + 2)
                dve.scalar_tensor_tensor(out=x2[:, t, :], in0=ydiff[:, t % 2, :], scalar=gcur[:, t:t + 1], in1=x2[:, t, :],
                                         op0=ALU.mult, op1=ALU.add).then_inc(y_add, 1)
        experts(dve, body)
        dve.wait_ge(c_add, E4 + 1)
        dve.wait_ge(y_add, RT * E4)
        for t in range(RT):
            dve.tensor_tensor(x2[:, t, :], x2[:, t, :], csum[:, :], ALU.add).then_inc(fin_done, 1)

    @block.tensor
    def _(pe):
        pe.wait_ge(wr_done, 1)
        for t in range(RT):
            for k in range(KD):
                mm = split_pair(pe, rbank[:, t * E4:(t + 1) * E4], lambda q: xn2T[:, k, q, t * P:(t + 1) * P],
                                lambda q: wr[:, k, q, :], k == 0, k == KD - 1)
        mm.then_inc(r_full, 1)

        def body(e, more):
            wait(pe, w1_done, e, 1, 1)
            for m in range(2 * HT):
                half, t = divmod(m, HT)
                s = slice(half * 512, half * 512 + 512)
                wait(pe, h_gelu, e, 16, m - 1)
                for k in range(KD):
                    mm = split_pair(pe, hbank[m % 2][:, :], lambda q: w1[:, k, q, t * P:(t + 1) * P],
                                    lambda q: xn2T[:, k, q, s], k == 0, k == KD - 1)
                mm.then_inc(h_full, 1)
            wait(pe, w2_done, e, 1, 1)
            wait(pe, gb_low, e, 1, 1)
            for r in range(RT + 1):
                if r == 1:
                    wait(pe, h_done, e, 16, 8)
                if r == 5:
                    wait(pe, h_done, e, 16, 16)
                wait(pe, y_got, e, 9, r - 2)
                for t in range(HT):
                    mm = split_pair(pe, ybank[r % 3][:, 0:D],
                                    (lambda q: gbs[:, q, t, :]) if r == 0 else (lambda q: hT[:, t, q, (r - 1) * P:r * P]),
                                    lambda q: w2[:, t, q, :], t == 0, t == HT - 1)
                mm.then_inc(y_full, 1)
        experts(pe, body)


def build(nc, ins, out, lat_scratch, q_scratch, y_scratch):
    with ExitStack() as ctx:
        W = constants(nc, ctx)
        with ExitStack() as cross:
            X = W | shared(nc, cross)
            with ExitStack() as c:
                block_0(nc, ins, lat_scratch, q_scratch, X, c)
            with ExitStack() as c:
                block_1(nc, ins["ctx"], lat_scratch, q_scratch, y_scratch, ins["mask"], X, c)
        with ExitStack() as kept:
            x2 = kept.enter_context(nc.sbuf_tensor("x2", [P, RT, D], F32))
            xn2T = kept.enter_context(nc.sbuf_tensor("xn2T", [P, KD, 2, ROWS], F32R))
            with ExitStack() as c:
                block_2(nc, ins, y_scratch, x2, xn2T, W, c)
            with ExitStack() as c:
                block_3(nc, ins, out, x2, xn2T, c)


def kernel(**inputs):
    import concourse.bacc as bacc
    from concourse.bass_utils import run_bass_kernel_spmd

    def flat(name):
        return np.ascontiguousarray(inputs[name])

    def lay(a):
        return np.ascontiguousarray(a)

    order = np.array([h * 16 + i for h in range(16) for i in (*range(0, 16, 2), *range(1, 16, 2))])
    wkv = flat("L0_xattn_Wkv")
    mask = flat("mask_BxS2_bk0")
    mask = np.concatenate([mask[:, :TAIL].reshape(B, P, CPP).transpose(0, 2, 1).reshape(B, TAIL), mask[:, TAIL:]], 1)
    half = np.arange(8, dtype=np.float32)
    theta = np.float32(1.0) / np.float32(10000.0) ** (half / np.float32(8))
    angle = (np.arange(P) % L).astype(np.float32)[:, None] * theta[None, :]
    parts = np.arange(P)
    arrays = {
        "x": lay(flat("x").reshape(ROWS, D)), "ctx": flat("ctx_1024"), "mask": lay(mask),
        "g1": flat("L0_xattn_g1"), "b1x": flat("L0_xattn_b1"), "g2": flat("L0_xattn_g2"), "b2x": flat("L0_xattn_b2"),
        "wq": flat("L0_xattn_Wq"), "wkT": lay(wkv[:, :INNER].T), "wv": lay(wkv[:, INNER:]), "wout": flat("L0_xattn_Wout"),
        "wqk": lay(np.concatenate([flat("L0_attn_W_q")[order], flat("L0_attn_W_k")[order]], 0).T),
        "wvs": lay(flat("L0_attn_W_v").T), "wos": lay(flat("L0_attn_W_o").T),
        "bqk": lay(np.concatenate([flat("L0_attn_b_q")[order], flat("L0_attn_b_k")[order]])),
        "bv": flat("L0_attn_b_v"), "bo": flat("L0_attn_b_o"),
        "w1": flat("L0_ffn_w1"), "w2": flat("L0_ffn_w2"), "b1": lay(flat("L0_ffn_b1").reshape(E4, HT, P).transpose(0, 2, 1)),
        "b2e": lay(flat("L0_ffn_b2").reshape(-1)), "wr": flat("L0_ffn_wr"), "br": flat("L0_ffn_br"),
        "rot": lay(np.stack([np.cos(angle), np.sin(angle)], 1).astype(np.float32)),
        "causal": lay(np.where(np.arange(L)[None, :] <= (parts % L)[:, None], 0.0, NEG).astype(np.float32)),
        "headmask": lay((parts[:, None] // 16 == np.arange(8)[None, :]).astype(np.float32)),
        "vmask": lay((parts[:, None] // L == (np.arange(D)[None, :] // 16) % 2).astype(np.float32)),
    }
    nc = bacc.Bacc("TRN2", target_bir_lowering=False, num_devices=1)
    in_map, ins = {}, {}
    for name, a in arrays.items():
        in_map[f"in_{name}"] = a
        ins[name] = nc.dram_tensor(f"in_{name}", a.shape, mybir.dt.from_np(a.dtype), kind="ExternalInput").ap()
    out = nc.dram_tensor("out", (ROWS, D), F32, kind="ExternalOutput").ap()
    lat_scratch = nc.dram_tensor("lat_scratch", (B, L, D), F32, kind="Internal").ap()
    q_scratch = nc.dram_tensor("q_scratch", (B, P, PAIRS, L), F32, kind="Internal").ap()
    y_scratch = nc.dram_tensor("y_scratch", (B, P, PAIRS, L), F32, kind="Internal").ap()
    build(nc, ins, out, lat_scratch, q_scratch, y_scratch)
    r = run_bass_kernel_spmd(nc, [in_map], core_ids=[0])
    return r.results[0]["out"].reshape(B, L, D)
```

```python
from contextlib import ExitStack

import numpy as np

import concourse.bass as bass
from concourse import mybir

ALU = mybir.AluOpType
ACT = mybir.ActivationFunctionType
AX = mybir.AxisListType
F32 = mybir.dt.float32
F32R = mybir.dt.float32r
BF16 = mybir.dt.bfloat16
U8 = mybir.dt.uint8

P = 128
B, L, D = 16, 64, 256
N = 1601
KD = D // P
HX, DX = 16, 64
PAIRS = HX // 2
INNER = HX * DX
ROWS = B * L
RT = ROWS // P
CH = 13
KEYS = CH * P
LAST = N - 1
CPP = 12
TAIL = CPP * P
QTR = KEYS // 4
NEG = -3.0e38
EPS = 1e-5
GROUPS = [(0, 4), (4, 8), (8, 12), (12, 13)]

STAT = [*range(1, CH + 1), 0]

HL3 = ((0, 0), (0, 1), (1, 0))


X_UNITS = (0, 0, 0, 3, 3, 2, 2, 2, 2, 0, 0, 0, 0)
Y_UNITS = (2, 2, 2, 2, 2, 1, 1, 1, 0, 0, 0, 0, 0)


def plan_x(has_a, has_b, has_next):
    ev = []
    units = [(i, j) for i in range(4) for j in range(4)]
    at = 2
    if has_a:
        ev += [("K", 0, 0), ("K", 1, 0), ("Q", 0), ("K", 0, 1), ("K", 1, 1)]
    for c in range(CH):
        if has_a:
            if c == 1:
                ev += [("K", 0, 2), ("K", 1, 2)] + unit_events(0, 0, 0)
            if c == 2:
                ev += [("K", 0, 3), ("K", 1, 3)] + unit_events(0, 1, 0)
            for i, j in units[at:at + X_UNITS[c]]:
                ev += unit_events(i, j, 0)
            at += X_UNITS[c]
            if c == 10 and has_b:
                ev += [("P", 3)]
            if c == 12 and has_b:
                ev += [("T", 0, 0)]
        if has_b:
            if c + 2 < CH:
                ev += [("T", 1, c + 2)]
            ev += [("V", 1, c)]
            if c == 2:
                ev += [("Y", 0)]
            if has_a and c in (4, 8):
                ev += [("N", c // 4 - 1)]
        if has_next:
            ev += {6: [("S", 4)], 9: [("S", 0)], 12: [("S", 1)]}.get(c, []) if has_b else []
    if has_b:
        ev += [("O", 1)]
    if has_a:
        ev += [("C",)]
    return ev


def plan_y(has_prev, has_next):
    ev = [("T", 0, 1)] if has_prev else []
    units = [(i, j) for i in range(4, 8) for j in range(4)]
    at = 3
    for i, j in units[:at]:
        ev += unit_events(i, j, 4)
    if not has_prev:
        ev += [("P", 3), ("T", 0, 0), ("T", 0, 1), ("N", 0), ("N", 1)]
    for c in range(CH):
        for i, j in units[at:at + Y_UNITS[c]]:
            ev += unit_events(i, j, 4)
        at += Y_UNITS[c]
        ev += [("T", 0, c + 2)] if c + 2 < CH else [("T", 2, c - 11)]
        ev += [("V", 0, c)]
        if c < 2:
            ev += [("N", c + 2)]
        if c == 2 and has_prev:
            ev += [("Y", 1)]
        if not has_prev:
            ev += {0: [("S", 4)], 1: [("S", 0), ("S", 1)]}.get(c, [])
        if has_next:
            ev += {2: [("H", 13, 0, 1)], 3: [("H", 2, 3), ("S", 2), ("S", 3)], 5: [("H", 4, 5)], 6: [("H", 6, 7)],
                   8: [("H", 8, 9)], 9: [("H", 10, 11)], 10: [("H", 12)], 11: [("B",)]}.get(c, [])
        if c == 8:
            ev += [("P", 7)]
    return ev + [("O", 0)]


def unit_events(i, j, first):
    ev = [("A", i, j)]
    if j == 0 and i < PAIRS - 1:
        ev += [("Q", i + 1)]
    if j == 1 and i > first:
        ev += [("P", i - 1)]
    if j == 3:
        ev += [("E", i)]
    return ev


def t_uses(ev):
    return [e for e in ev if e[0] in "YTQ"]


K_BANK = ((0, 1), (2, 3), (2, 3), (3, 3))
X_FIRST, X_MID, X_END = plan_x(True, False, True), plan_x(True, True, True), plan_x(False, True, False) + [("Y", 1)]
X_LAST = plan_x(True, True, False)
Y_FIRST, Y_MID, Y_LAST = plan_y(False, True), plan_y(True, True), plan_y(True, False)
USE0 = {e: n for n, e in enumerate(t_uses(X_FIRST + Y_FIRST))}
USE = {e: n for n, e in enumerate(t_uses(X_MID + Y_MID))}
NUSE0, NUSE = len(USE0), len(USE)
USE_END = {e: n for n, e in enumerate(t_uses(X_END))}
assert NUSE % 2 == 0


class Batch:

    def __init__(self, off, turn=None):
        self.off, self.turn = off, turn

    def lin(self, k, c):
        n = self.off * k + c
        return n if self.turn is None else self.turn * k + n

    def use(self, e):
        if self.turn is None and self.off == 0:
            return USE0[e]
        return self.lin(NUSE, NUSE0 - NUSE + (USE_END if self.off == B else USE)[e])

    def bank(self, e):
        if self.turn is None and self.off == 0:
            return USE0[e] % 2
        return (NUSE0 + (USE_END if self.off == B else USE)[e]) % 2

    def least(self, k, c):
        return self.off * k + c


def wait(eng, sem, batch, k, c):
    assert batch.turn is None or batch.least(k, c) > 0
    if batch.least(k, c) > 0:
        eng.wait_ge(sem, batch.lin(k, c))


def apart(ins, sem):
    return ins.wait_op(sem, 1, "sem-ge")


def periods(eng, step):
    step(Batch(0), X_FIRST, Y_FIRST)
    step(Batch(1), X_MID, Y_MID)
    with eng.Fori(0, B - 3) as turn:
        step(Batch(2, turn), X_MID, Y_MID)
    step(Batch(B - 1), X_LAST, Y_LAST)
    step(Batch(B), X_END, [])


def value_bank(h, c):
    slot = (c + h) % 3
    mine = 13 * h + c
    for m in range(mine - 1, mine - 14, -1):
        hh, cc = (m // 13) % 2, m % 13
        if (cc + hh) % 3 == slot:
            return slot, m + 1


def split_pair(pe, out, weights, moving, first, last):
    for n, (a, b) in enumerate(HL3):
        mm = pe.matmul(out, weights(a), moving(b), start=first and n == 0, stop=last and n == 2)
    return mm


class Context:

    NPOOL = 25


    def __init__(self, nc, ins, lat_scratch, q_scratch, W, ctx):
        def sb(name, shape, dt):
            return ctx.enter_context(nc.sbuf_tensor(name, shape, dt))

        def sem(name):
            return ctx.enter_context(nc.semaphore(name))

        self.W, self.rows, self.mask = W, ins["ctx"], ins["mask"]
        self.lat_scratch, self.q_scratch = lat_scratch, q_scratch
        self.raw = sb("raw", [P, CH + 1, D], F32)
        self.mask8 = sb("mask8", [P, N], U8)
        self.xn0 = sb("xn0", [P, D], F32)
        self.stats = sb("stats", [P, CH + 1, 6], F32)
        self.small = sb("small", [P, 7, CH + 1], F32)
        self.shift = sb("shift", [P, CH + 1], F32)
        self.rstd = sb("rstd", [P, CH + 1], F32)
        self.rows_in = [sem(f"rows_in{g}") for g in range(5)]
        self.q_in = sem("q_in")
        self.mask_in = sem("mask_in")
        self.stat_done = sem("stat_done")
        self.rstd_done = sem("rstd_done")
        self.norm_done = sem("norm_done")
        self.pool_step = sem("pool_step")
        self.keys_done = sem("keys_done")
        self.mask_done = sem("mask_done")
        self.qblk_high = sem("qblk_high")
        self.qblk_done = sem("qblk_done")
        self.t_full = sem("t_full")
        self.k_full = sem("k_full")
        self.score_out = sem("score_out")
        self.val_done = sem("val_done")

    def load_rows(self, sp, n, index, g):
        if g > 0:
            wait(sp, self.val_done, n, 4, g - 3)
        if g < 3:
            sp.dma_start(self.raw[:, 4 * g:4 * g + 4, :].rearrange("p c d -> p (c d)"),
                         self.rows[index, 0:TAIL, :].rearrange("(p c) d -> p (c d)", c=CPP)[:, 4 * g * D:(4 * g + 4) * D]
                         ).then_inc(self.rows_in[g], 16)
        else:
            sp.dma_start(self.raw[L:P, 12, :], self.rows[index, TAIL:LAST, :]).then_inc(self.rows_in[3], 16)
            sp.dma_start(self.raw[0:L, 12, :], self.lat_scratch[index]).then_inc(self.rows_in[3], 16)

    def load_centre(self, sp, n, index):
        wait(sp, self.keys_done, n, 4, 0)
        wait(sp, self.k_full, n, 8, 0)
        sp.dma_start(self.raw[:, 13, :], self.rows[index, LAST, :].partition_broadcast(P)).then_inc(self.rows_in[4], 16)

    def moments(self, dve, n, g):
        wait(dve, self.rows_in[g], n, 32 if g == 3 else 16, 32 if g == 3 else 16)
        for c in range(*GROUPS[g]) if g < 4 else [13]:
            dve.bn_stats(self.stats[:, STAT[c], :], self.raw[:, c, :]).then_inc(self.stat_done, 1)

    def q_block_low(self, dve, n, queries):
        W = self.W
        for h in range(2):
            s = slice(h * L, h * L + L)
            wait(dve, self.qblk_high, n, 2, h + 1)
            dve.tensor_tensor(W["qblk"][s, :, 1, s], queries[s, :, :], W["qblk"][s, :, 0, s].bitcast(F32), ALU.subtract
                              ).then_inc(self.qblk_done, 1)

    def normalise(self, act, n, *chunks):
        wait(act, self.rstd_done, n, 2, 1 if chunks[-1] < 8 else 2)
        for c in chunks:
            s = slice(L, P) if c == 12 else slice(0, P)
            m = STAT[c]
            act.activation(self.raw[s, c, :], self.raw[s, c, :], ACT.Identity, bias=self.shift[s, m:m + 1],
                           scale=self.rstd[s, m:m + 1]).then_inc(self.norm_done, 1)

    def q_block_high(self, act, n, queries):
        for h in range(2):
            s = slice(h * L, h * L + L)
            act.activation(self.W["qblk"][s, :, 0, s], queries[s, :, :], ACT.Copy).then_inc(self.qblk_high, 1)

    def mask_bias(self, pool, n):
        bias, mask8 = self.W["bias"], self.mask8
        wait(pool, self.mask_in, n, 16, 16)
        wait(pool, self.score_out, n, 32, 0)
        apart(pool.tensor_scalar(bias[:, 0:TAIL], mask8[:, 0:TAIL], -NEG, NEG, ALU.mult, ALU.add), self.mask_in
              ).then_inc(self.mask_done, 1)
        pool.tensor_scalar(bias[:, TAIL + L:KEYS + 1], mask8[:, TAIL:N], -NEG, NEG, ALU.mult, ALU.add
                           ).then_inc(self.mask_done, 1)

    def prepare(self, pool, n):
        W, raw, xn0 = self.W, self.raw, self.xn0
        k = [0]

        def link(ins):
            k[0] += 1
            ins.then_inc(self.pool_step, 1)
            pool.wait_ge(self.pool_step, n.lin(self.NPOOL, k[0]))

        def deviations(part, cols):
            me, m2e, mo, m2o = (self.stats[:, cols, q] for q in (1, 2, 4, 5))
            total, diff, both, sq, quarter, var, negmean = (self.small[:, q, cols] for q in range(7))
            wait(pool, self.stat_done, n, 14, (9, 14)[part])
            link(pool.tensor_tensor(total, me, mo, ALU.add))
            link(pool.tensor_tensor(diff, me, mo, ALU.subtract))
            link(pool.tensor_tensor(both, m2e, m2o, ALU.add))
            link(apart(pool.tensor_scalar(negmean, total, -0.5, 0.0, ALU.mult, ALU.add), self.stat_done))
            link(pool.tensor_tensor(sq, diff, diff, ALU.mult))
            link(apart(pool.tensor_scalar(quarter, sq, 0.25, EPS, ALU.mult, ALU.add), self.stat_done))
            link(apart(pool.tensor_scalar(sq, both, 1.0 / D, 0.0, ALU.mult, ALU.add), self.stat_done))
            link(pool.tensor_tensor(var, sq, quarter, ALU.add))
            wait(pool, self.norm_done, n, 14, 0)
            link(pool.tensor_tensor(self.rstd[:, cols], var, W["neghalf"][:, cols], ALU.pow))
            pool.tensor_tensor(self.shift[:, cols], self.rstd[:, cols], negmean, ALU.mult).then_inc(self.rstd_done, 1)

        def centre(g):
            wait(pool, self.norm_done, n, 14, 4 * g + 5)
            rows = raw[:, 4 * g:4 * g + 4, :]
            link(pool.tensor_tensor(rows, rows, raw[:, 13:14, :].to_broadcast([P, 4, D]), ALU.subtract))
            pool.tensor_tensor(rows, rows, W["g1"][:, :].unsqueeze(1).to_broadcast([P, 4, D]), ALU.mult
                               ).then_inc(self.keys_done, 1)

        deviations(0, slice(0, 9))
        if n.off == 0:
            deviations(1, slice(9, CH + 1))
        wait(pool, self.norm_done, n, 14, 1)
        wait(pool, self.k_full, n, 8, 0)
        link(pool.tensor_tensor(xn0[:, :], raw[:, 13, :], W["g1"][:, :], ALU.mult))
        link(pool.tensor_tensor(xn0[:, :], xn0[:, :], W["b1"][:, :], ALU.add))
        centre(0)
        if n.off > 0:
            deviations(1, slice(9, CH + 1))
        centre(1)
        centre(2)
        wait(pool, self.norm_done, n, 14, 14)
        wait(pool, self.keys_done, n, 4, 3)
        link(pool.tensor_tensor(raw[L:P, 12, :], raw[L:P, 12, :], raw[L:P, 13, :], ALU.subtract))
        link(pool.tensor_tensor(raw[L:P, 12, :], raw[L:P, 12, :], W["g1"][L:P, :], ALU.mult))
        pool.tensor_tensor(raw[0:L, 12, :], raw[0:L, 12, :], xn0[0:L, :], ALU.subtract).then_inc(self.keys_done, 1)
        wait(pool, self.keys_done, n, 4, 4)
        assert k[0] == self.NPOOL


def block_0(nc, ins, F, W, ctx):
    def sb(name, shape, dt):
        return ctx.enter_context(nc.sbuf_tensor(name, shape, dt))

    def sem(name):
        return ctx.enter_context(nc.semaphore(name))

    x = sb("x0_rows", [P, RT, D], F32)
    lat = sb("lat", [P, RT, D], F32)
    latT = sb("latT", [P, KD, 2, ROWS], F32R)
    wraw = sb("wraw", [P, 3, 2 * INNER], F32)
    wq = sb("wq", [P, KD, 2, INNER], F32R)
    qstage = sb("qstage", [P, B, PAIRS, L], F32)
    g2 = sb("g2", [P, D], F32)
    b2 = sb("b2", [P, D], F32)
    stats = sb("stats0", [P, RT, 6], F32)
    mv = sb("mv", [P, RT, 2], F32)
    veps = sb("veps", [P, RT], F32)
    rstd1 = sb("rstd_first", [P, RT], F32)
    var2 = sb("var_second", [P, RT], F32)
    rstd2 = sb("rstd_second", [P, RT], F32)
    rboth = sb("rstd_both", [P, RT], F32)
    bank = [ctx.enter_context(nc.psum_tensor(f"bank0_{n}", [P, 512], F32)) for n in range(4)]

    x_in = sem("x_in0")
    w_in = [sem(f"w_in{n}") for n in range(3)]
    g2_in = sem("g2_in")
    g1_in = sem("g1_in")
    ident_done = sem("ident_done")
    zero_done = sem("zero_done")
    stat0 = sem("stat0")
    mv_done = sem("mv_done")
    rboth_done = sem("rboth_done")
    pool0 = sem("pool0")
    scaled = sem("scaled")
    lat_done = sem("lat_done")
    bank_full = sem("bank_full")
    high_done = sem("high_done")
    low_done = sem("low_done")
    q_done = sem("q_done")
    wh_done = sem("wh_done")
    wql_done = sem("wql_done")
    wl_done = sem("wl_done")
    lat_out, q_out = sem("lat_out"), sem("q_out")
    splits = [(wraw[:, 0, :].rearrange("p (k n) -> p k n", k=KD), wq[:, :, :, :]),
              (wraw[:, 1, :].rearrange("p (k n) -> p k n", k=PAIRS), W["wk"][:, :, :, :]),
              (wraw[:, 2, :].rearrange("p (k n) -> p k n", k=KD), W["wv"][:, :, :, :])]
    first = Batch(0)

    block = ctx.enter_context(nc.Block())

    @block.sync
    def _(sp):
        sp.dma_start(x[:, :, :], ins["x"].rearrange("(t p) d -> p t d", p=P)).then_inc(x_in, 16)
        sp.dma_start(g2[:, :], ins["g2"].partition_broadcast(P)).then_inc(g2_in, 16)
        sp.dma_start(b2[:, :], ins["b2x"].partition_broadcast(P)).then_inc(g2_in, 16)
        sp.dma_start(wraw[:, 0, :].rearrange("p (k n) -> p k n", k=KD), ins["wq"].rearrange("(k p) n -> p k n", p=P)
                     ).then_inc(w_in[0], 16)
        F.load_centre(sp, first, 0)
        for g in range(3):
            F.load_rows(sp, first, 0, g)
        sp.dma_start(W["g1"][:, :], ins["g1"].partition_broadcast(P)).then_inc(g1_in, 16)
        sp.dma_start(W["b1"][:, :], ins["b1x"].partition_broadcast(P)).then_inc(g1_in, 16)
        sp.dma_start(F.mask8[:, :], F.mask[0, :].partition_broadcast(P)).then_inc(F.mask_in, 16)
        sp.dma_start(wraw[:, 1, :].rearrange("p (k n) -> p k n", k=PAIRS), ins["wkT"].rearrange("(k p) n -> p k n", p=P)
                     ).then_inc(w_in[1], 16)
        sp.wait_ge(lat_done, RT)
        sp.dma_start(F.lat_scratch.rearrange("(t b) l d -> (b l) t d", b=2), lat[:, :, :]).then_inc(lat_out, 16)
        sp.wait_ge(lat_out, 16)
        F.load_rows(sp, first, 0, 3)
        sp.dma_start(wraw[:, 2, :].rearrange("p (k n) -> p k n", k=KD), ins["wv"].rearrange("(k p) n -> p k n", p=P)
                     ).then_inc(w_in[2], 16)
        for t in range(4):
            sp.wait_ge(q_done, 4 * t + 4)
            sp.dma_start(F.q_scratch[4 * t:4 * t + 4].rearrange("b p a l -> p b (a l)"),
                         qstage[:, 4 * t:4 * t + 4, :, :].rearrange("p b a l -> p b (a l)")).then_inc(q_out, 16)
        sp.wait_ge(q_out, 16 * 4)

    @block.gpsimd
    def _(pool):
        chain = [0]

        def link(ins):
            chain[0] += 1
            ins.then_inc(pool0, 1)
            pool.wait_ge(pool0, chain[0])

        link(pool.memset(W["ident"][:, :], 0.0))
        pool.affine_select(out=W["ident"][:, :], in_=W["ident"][:, :], compare_op=ALU.not_equal, fill=1.0, base=0,
                           pattern=[[-1, P]], channel_multiplier=1).then_inc(ident_done, 1)
        link(pool.memset(W["neghalf"][:, :], -0.5))
        pool.memset(W["qblk"][:, :, :, :].bitcast(F32), 0.0).then_inc(zero_done, 1)
        pool.wait_ge(mv_done, RT)
        link(pool.tensor_scalar(veps[:, :], mv[:, :, 1], 1.0, EPS, ALU.mult, ALU.add))
        link(pool.tensor_tensor(rstd1[:, :], veps[:, :], W["neghalf"][:, 0:RT], ALU.pow))
        link(pool.tensor_tensor(var2[:, :], rstd1[:, :], rstd1[:, :], ALU.mult))
        link(pool.tensor_tensor(var2[:, :], var2[:, :], mv[:, :, 1], ALU.mult))
        link(pool.tensor_scalar(var2[:, :], var2[:, :], 1.0, EPS, ALU.mult, ALU.add))
        link(pool.tensor_tensor(rstd2[:, :], var2[:, :], W["neghalf"][:, 0:RT], ALU.pow))
        pool.tensor_tensor(rboth[:, :], rstd1[:, :], rstd2[:, :], ALU.mult).then_inc(rboth_done, 1)
        pool.wait_ge(wh_done, 1)
        for k in range(KD):
            pool.tensor_tensor(wq[:, k, 1, :], splits[0][0][:, k, :], wq[:, k, 0, :].bitcast(F32), ALU.subtract
                               ).then_inc(wql_done, 1)
        link(pool.memset(W["bias"][:, :], 0.0))
        F.mask_bias(pool, first)
        pool.wait_ge(g1_in, 32)
        F.prepare(pool, first)

    @block.vector
    def _(dve):
        dve.wait_ge(x_in, 16)
        for t in range(RT):
            dve.bn_stats(stats[:, t, :], x[:, t, :]).then_inc(stat0, 1)
        for t in range(RT):
            dve.wait_ge(stat0, t + 1)
            dve.bn_aggr(mv[:, t, :], stats[:, t, :]).then_inc(mv_done, 1)
        dve.wait_ge(g2_in, 32)
        for t in range(RT):
            dve.wait_ge(mv_done, t + 1)
            dve.scalar_tensor_tensor(out=lat[:, t, :], in0=x[:, t, :], scalar=mv[:, t, 0:1], in1=g2[:, :],
                                     op0=ALU.subtract, op1=ALU.mult).then_inc(scaled, 1)
        dve.wait_ge(rboth_done, 1)
        for t in range(RT):
            dve.wait_ge(scaled, t + 1)
            dve.scalar_tensor_tensor(out=lat[:, t, :], in0=lat[:, t, :], scalar=rboth[:, t:t + 1], in1=b2[:, :],
                                     op0=ALU.mult, op1=ALU.add).then_inc(lat_done, 1)
        for n in range(4):
            dve.wait_ge(high_done, n + 1)
            k, half = n % 2, n // 2
            s = slice(half * 512, half * 512 + 512)
            dve.tensor_tensor(latT[:, k, 1, s], bank[n][:, :], latT[:, k, 0, s].bitcast(F32), ALU.subtract
                              ).then_inc(low_done, 1)
        for g in (4, 0, 1, 2, 3):
            F.moments(dve, first, g)
        F.q_block_low(dve, first, qstage[:, 0, :, :])
        for n in (1, 2):
            src, to = splits[n]
            dve.wait_ge(wh_done, n + 1)
            dve.tensor_tensor(to[:, :, 1, :], src, to[:, :, 0, :].bitcast(F32), ALU.subtract).then_inc(wl_done, 1)

    @block.scalar
    def _(act):
        act.wait_ge(w_in[0], 16)
        act.activation(splits[0][1][:, :, 0, :], splits[0][0], ACT.Copy).then_inc(wh_done, 1)
        for n in range(4):
            act.wait_ge(bank_full, n + 1)
            k, half = n % 2, n // 2
            act.activation(latT[:, k, 0, half * 512:half * 512 + 512], bank[n][:, :], ACT.Copy).then_inc(high_done, 1)
        between = {6: (13, 0, 1), 7: (2, 3), 8: (4, 5), 9: (6, 7), 10: (8, 9), 11: (10, 11), 12: (12,)}
        for n in range(16):
            t, a = n // 4, 2 * (n % 4)
            act.wait_ge(bank_full, 5 + n)
            act.activation(qstage[:, 4 * t:4 * t + 4, a:a + 2, :].rearrange("p b a l -> p a b l"),
                           bank[n % 4][:, :].rearrange("p (a b l) -> p a b l", a=2, l=L),
                           ACT.Copy, scale=DX ** -0.5).then_inc(q_done, 1)
            if n == 3:
                act.wait_ge(q_done, 4)
                act.wait_ge(zero_done, 1)
                F.q_block_high(act, first, qstage[:, 0, :, :])
            if n in between:
                F.normalise(act, first, *between[n])
            if n in (5, 13):
                m = 1 if n == 5 else 2
                act.wait_ge(w_in[m], 16)
                act.activation(splits[m][1][:, :, 0, :], splits[m][0], ACT.Copy).then_inc(wh_done, 1)

    @block.tensor
    def _(pe):
        pe.wait_ge(ident_done, 1)
        for n in range(4):
            k, half = n % 2, n // 2
            pe.wait_ge(lat_done, 4 * half + 4)
            for t in range(4):
                mm = pe.transpose(bank[n][:, t * P:(t + 1) * P], lat[:, 4 * half + t, k * P:(k + 1) * P], W["ident"][:, :])
            mm.then_inc(bank_full, 1)
        pe.wait_ge(wql_done, KD)
        for n in range(16):
            t = n // 4
            pe.wait_ge(low_done, 2 + 2 * (t // 2))
            if n >= 4:
                pe.wait_ge(q_done, n - 3)
            else:
                pe.wait_ge(low_done, n + 1)
            for half in range(2):
                pair = 2 * (n % 4) + half
                for k in range(KD):
                    mm = split_pair(pe, bank[n % 4][:, half * 256:(half + 1) * 256],
                                    lambda q: wq[:, k, q, pair * P:(pair + 1) * P],
                                    lambda q: latT[:, k, q, t * 256:(t + 1) * 256], k == 0, k == KD - 1)
            mm.then_inc(bank_full, 1)


def block_1(nc, F, y_scratch, shared, ctx):
    W = shared

    def sb(name, shape, dt):
        return ctx.enter_context(nc.sbuf_tensor(name, shape, dt))

    def ps(name):
        return ctx.enter_context(nc.psum_tensor(name, [P, 512], F32))

    def sem(name):
        return ctx.enter_context(nc.semaphore(name))

    raw, xn0, q_in, mask_in, val_done, score_out = F.raw, F.xn0, F.q_in, F.mask_in, F.val_done, F.score_out
    keys_done, mask_done, qblk_done, t_full, k_full = F.keys_done, F.mask_done, F.qblk_done, F.t_full, F.k_full
    keyT = sb("keyT", [P, KD, 2, KEYS], F32R)
    val = sb("val", [P, CH, 2, D], F32R)
    prob = sb("prob", [P, PAIRS, KEYS + 1], F32)
    probT = sb("probT", [P, 3, 2, 512], F32R)
    qkT = sb("qkT", [P, 2, KD, 2, P], F32R)
    outT = sb("outT", [P, KD, 2, 512], F32R)
    ystage = sb("ystage", [P, 2, 4, L], F32)
    q32 = sb("q32", [P, PAIRS, L], F32)
    x0next = sb("x0next", [P, KD], F32)
    x0T = sb("x0T", [P, KD], F32)
    maxes = sb("maxes", [P, PAIRS, 5], F32)
    negmax = sb("negmax", [P, PAIRS], F32)
    psum_ = sb("psums", [P, PAIRS], F32)
    rsum = sb("rsum", [P, PAIRS], F32)

    s_bank = [ps(f"s_bank{n}") for n in range(4)]
    t_bank = [ps(f"t_bank{n}") for n in range(2)]
    o_bank = [ps(f"o_bank{n}") for n in range(2)]

    t_high = sem("t_high")
    t_done = sem("t_done")
    k_high, k_done = sem("k_high"), sem("k_done1")
    x0_next = sem("x0_next")
    x0_done = sem("x0_done")
    val_high = sem("val_high")
    score_full = sem("score_full")
    max_done = sem("max_done")
    exp_done = sem("exp_done")
    rsum_done = sem("rsum_done")
    prob_done = sem("prob_done")
    pv_done = sem("pv_done")
    out_high = sem("out_high")
    out_done = sem("out_done")
    y_out = [sem(f"y_out{h}") for h in range(2)]

    block = ctx.enter_context(nc.Block())

    @block.sync
    def _(sp):
        def load_q_mask(n, index):
            wait(sp, mask_done, n, 2, 0)
            wait(sp, qblk_done, n, 2, 0)
            sp.dma_start(q32[:, :, :], F.q_scratch[index]).then_inc(q_in, 16)
            sp.dma_start(F.mask8[:, :], F.mask[index, :].partition_broadcast(P)).then_inc(mask_in, 16)

        def store_y(b, h, e, index):
            sp.wait_ge(t_done, b.use(e) + 1)
            sp.dma_start(y_scratch[index, :, 4 * h:4 * h + 4, :], ystage[:, h, :, :]).then_inc(y_out[h], 16)

        def step(b, x, y):
            nxt = Batch(b.off + 1, b.turn)
            if ("B",) in y:
                F.load_centre(sp, nxt, nxt.lin(1, 0))
            if ("B",) in y:
                wait(sp, val_done, nxt, 4, -3)
            if ("Y", 0) in x:
                store_y(b, 0, ("Y", 0), b.lin(1, -1))
            if ("B",) in y:
                for g in range(4):
                    F.load_rows(sp, nxt, nxt.lin(1, 0), g)
            if ("Y", 1) in x + y:
                store_y(b, 1, ("Y", 1), b.lin(1, -1))
            if ("B",) in y:
                load_q_mask(nxt, nxt.lin(1, 0))
        periods(sp, step)
        for h in range(2):
            sp.wait_ge(y_out[h], 16 * B)

    @block.gpsimd
    def _(pool):
        def step(b, x, y):
            if ("Q", 0) in x and b.off > 0:
                F.mask_bias(pool, b)
            if ("B",) in y:
                F.prepare(pool, Batch(b.off + 1, b.turn))
        periods(pool, step)

    @block.scalar
    def _(act):
        def half(b, events):
            for e in events:
                kind = e[0]
                if kind in "YTQ":
                    act.wait_ge(t_full, b.use(e) + 1)
                    bank = t_bank[b.bank(e)]
                if kind == "Y":
                    wait(act, y_out[e[1]], b, 16, -16)
                    act.activation(ystage[0:L, e[1], :, :],
                                   bank[0:L, :].rearrange("p (a x) -> p a x", a=4)[:, :, 0:L], ACT.Copy).then_inc(t_high, 1)
                if kind == "T":
                    when, c = e[1:]
                    slot, need = value_bank(min(when, 1), c)
                    wait(act, pv_done, b, 26, need - (26 if when == 1 else 0))
                    act.activation(probT[:, slot, 0, :], bank[:, :], ACT.Copy).then_inc(t_high, 1)
                if kind == "Q":
                    wait(act, score_out, b, 32, 4 * e[1] - 4)
                    act.activation(qkT[:, e[1] % 2, :, 0, :], bank[:, 0:KD * P].rearrange("p (k x) -> p k x", k=KD),
                                   ACT.Copy).then_inc(t_high, 1)
                if kind == "K":
                    k, g = e[1:]
                    a, z = GROUPS[g]
                    bank, at = s_bank[K_BANK[g][k]], 2 * P * k if g == 3 else 0
                    wait(act, k_full, b, 8, 8 if g == 3 else 2 * g + k + 1)
                    wait(act, score_out, b, 32, 0)
                    if g == 3:
                        wait(act, x0_done, b, 1, 0)
                        act.activation(x0next[:, k:k + 1], bank[:, at + P:at + P + 1], ACT.Copy).then_inc(x0_next, 1)
                    act.activation(keyT[:, k, 0, a * P:z * P], bank[:, at:at + (z - a) * P], ACT.Copy).then_inc(k_high, 1)
                if kind == "E":
                    i = e[1]
                    wait(act, max_done, b, 8, i + 1)
                    act.activation(prob[:, i, :], prob[:, i, :], ACT.Exp, bias=negmax[:, i:i + 1],
                                   accum_out=psum_[:, i:i + 1]).then_inc(exp_done, 1)
                if kind == "O":
                    h = e[1]
                    wait(act, pv_done, b, 26, 13 * (h + 1) - 26 * h)
                    wait(act, x0_done, b, 1, 1 - h)
                    for k in range(KD):
                        act.activation(outT[:, k, 0, :], o_bank[k][:, :], ACT.Identity, bias=x0T[:, k:k + 1]).then_inc(out_high, 1)
                if kind == "N":
                    g = e[1]
                    a, z = GROUPS[g]
                    wait(act, keys_done, b, 4, g + 1)
                    wait(act, pv_done, b, 26, z - 13)
                    act.activation(val[:, a:z, 0, :], raw[:, a:z, :], ACT.Copy).then_inc(val_high, 1)
                if kind == "H":
                    F.normalise(act, Batch(b.off + 1, b.turn), *e[1:])
                if kind == "B":
                    wait(act, q_in, b, 16, 16)
                    act.wait_ge(t_full, b.use(("Q", 7)) + 1)
                    F.q_block_high(act, Batch(b.off + 1, b.turn), q32)

        periods(act, lambda b, x, y: (half(b, x), half(b, y)))

    @block.vector
    def _(dve):
        def half(b, events):
            for e in events:
                kind = e[0]
                if kind in "YTQ":
                    dve.wait_ge(t_high, b.use(e) + 1)
                    bank = t_bank[b.bank(e)]
                if kind == "Y":
                    wait(dve, y_out[e[1]], b, 16, -16)
                    dve.tensor_copy(ystage[L:P, e[1], :, :],
                                    bank[L:P, :].rearrange("p (a x) -> p a x", a=4)[:, :, L:P]).then_inc(t_done, 1)
                if kind == "T":
                    slot, _ = value_bank(min(e[1], 1), e[2])
                    dve.tensor_tensor(probT[:, slot, 1, :], bank[:, :], probT[:, slot, 0, :].bitcast(F32),
                                      ALU.subtract).then_inc(t_done, 1)
                if kind == "Q":
                    dve.tensor_tensor(qkT[:, e[1] % 2, :, 1, :], bank[:, 0:KD * P].rearrange("p (k x) -> p k x", k=KD),
                                      qkT[:, e[1] % 2, :, 0, :].bitcast(F32), ALU.subtract).then_inc(t_done, 1)
                if kind == "K":
                    k, g = e[1:]
                    a, z = GROUPS[g]
                    bank, at = s_bank[K_BANK[g][k]], 2 * P * k if g == 3 else 0
                    wait(dve, k_high, b, 8, 8 if g == 3 else 2 * g + k + 1)
                    dve.tensor_tensor(keyT[:, k, 1, a * P:z * P], bank[:, at:at + (z - a) * P],
                                      keyT[:, k, 0, a * P:z * P].bitcast(F32), ALU.subtract).then_inc(k_done, 1)
                if kind == "A":
                    i, j = e[1:]
                    if (i, j) == (0, 0):
                        wait(dve, mask_done, b, 2, 2)
                        dve.tensor_copy(maxes[:, :, 4:5], W["bias"][:, KEYS:KEYS + 1].unsqueeze(1).to_broadcast([P, PAIRS, 1]))
                    if j == 0:
                        dve.tensor_copy(prob[:, i, KEYS:KEYS + 1], W["bias"][:, KEYS:KEYS + 1])
                    wait(dve, score_full, b, 32, 4 * i + j + 1)
                    s = slice(j * QTR, (j + 1) * QTR)
                    apart(dve.tensor_tensor_reduce(out=prob[:, i, s], in0=s_bank[j][:, 0:QTR], in1=W["bias"][:, s],
                                                   scale=1.0, scalar=NEG, op0=ALU.add, op1=ALU.max,
                                                   accum_out=maxes[:, i, j:j + 1]), mask_done).then_inc(score_out, 1)
                    if j == 3:
                        wait(dve, score_out, b, 32, 4 * i + 4)
                        dve.tensor_reduce(negmax[:, i:i + 1], maxes[:, i, :], AX.X, ALU.max, negate=True
                                          ).then_inc(max_done, 1)
                if kind == "P":
                    i = e[1]
                    wait(dve, exp_done, b, 8, i + 1)
                    dve.reciprocal(rsum[:, i:i + 1], psum_[:, i:i + 1]).then_inc(rsum_done, 1)
                    wait(dve, rsum_done, b, 8, i + 1)
                    dve.tensor_scalar(prob[:, i, :], prob[:, i, :], rsum[:, i:i + 1], None, ALU.mult).then_inc(prob_done, 1)
                if kind == "O":
                    h = e[1]
                    for k in range(KD):
                        wait(dve, out_high, b, 4, 2 * h + k + 1 - 4 * h)
                        dve.scalar_tensor_tensor(out=outT[:, k, 1, :], in0=o_bank[k][:, :], scalar=x0T[:, k:k + 1],
                                                 in1=outT[:, k, 0, :].bitcast(F32), op0=ALU.add, op1=ALU.subtract
                                                 ).then_inc(out_done, 1)
                if kind == "C":
                    wait(dve, x0_next, b, 2, 2)
                    wait(dve, out_done, b, 4, 0)
                    dve.tensor_copy(x0T[:, :], x0next[:, :]).then_inc(x0_done, 1)
                if kind == "N":
                    g = e[1]
                    a, z = GROUPS[g]
                    wait(dve, val_high, b, 4, g + 1)
                    dve.tensor_tensor(val[:, a:z, 1, :], raw[:, a:z, :], val[:, a:z, 0, :].bitcast(F32), ALU.subtract
                                      ).then_inc(val_done, 1)
                n = Batch(b.off + 1, b.turn)
                if kind == "S":
                    F.moments(dve, n, e[1])
                if kind == "B":
                    F.q_block_low(dve, n, q32)

        periods(dve, lambda b, x, y: (half(b, x), half(b, y)))

    @block.tensor
    def _(pe):
        ident = W["ident"]

        def half(b, events):
            for e in events:
                kind = e[0]
                if kind in "YTQ":
                    bank = t_bank[b.bank(e)]
                    if b.turn is not None or b.off > 0 or b.use(e) >= 2:
                        pe.wait_ge(t_done, b.use(e) - 1)
                if kind == "Y":
                    h = e[1]
                    wait(pe, out_done, b, 4, 2 * h - 2)
                    for a in range(4):
                        pair = 4 * h + a
                        for k in range(KD):
                            mm = split_pair(pe, bank[:, a * P:(a + 1) * P],
                                            lambda q: W["wv"][:, k, q, pair * P:(pair + 1) * P],
                                            lambda q: outT[:, k, q, a * P:(a + 1) * P], k == 0, k == KD - 1)
                    mm.then_inc(t_full, 1)
                if kind == "T":
                    when, c = e[1:]
                    h = min(when, 1)
                    if c == 0:
                        wait(pe, prob_done, b, 8, 4 * h + 4)
                    for t in range(4):
                        mm = pe.transpose(bank[:, t * P:(t + 1) * P], prob[:, 4 * h + t, c * P:(c + 1) * P], ident[:, :])
                    mm.then_inc(t_full, 1)
                if kind == "Q":
                    i = e[1]
                    if i == 0:
                        wait(pe, qblk_done, b, 2, 2)
                    for k in range(KD):
                        mm = split_pair(pe, bank[:, k * P:(k + 1) * P],
                                        lambda q: W["wk"][:, i, q, k * P:(k + 1) * P],
                                        lambda q: W["qblk"][:, i, q, :], True, True)
                    mm.then_inc(t_full, 1)
                if kind == "K":
                    k, g = e[1:]
                    a, z = GROUPS[g]
                    bank, at = s_bank[K_BANK[g][k]], 2 * P * k if g == 3 else 0
                    wait(pe, keys_done, b, 4, g + 1)
                    if (g, k) == (0, 0):
                        wait(pe, score_out, b, 32, 0)
                    if g >= 2:
                        wait(pe, k_done, b, 8, 3 + k if g == 2 else 6)
                    for c in range(a, z):
                        mm = pe.transpose(bank[:, at + (c - a) * P:at + (c - a + 1) * P], raw[:, c, k * P:(k + 1) * P],
                                          ident[:, :])
                    if g == 3:
                        mm = pe.transpose(bank[:, at + P:at + 2 * P], xn0[:, k * P:(k + 1) * P], ident[:, :])
                    if (g, k) == (3, 1):
                        mm.then_inc(k_full, 2)
                    elif g < 3:
                        mm.then_inc(k_full, 1)
                if kind == "A":
                    i, j = e[1:]
                    if j == 0:
                        pe.wait_ge(t_done, b.use(("Q", i)) + 1)
                    if i == 0:
                        wait(pe, k_done, b, 8, 2 * j + 2)
                    wait(pe, score_out, b, 32, 4 * i + j - 3)
                    for k in range(KD):
                        mm = split_pair(pe, s_bank[j][:, 0:QTR], lambda q: qkT[:, i % 2, k, q, :],
                                        lambda q: keyT[:, k, q, j * QTR:(j + 1) * QTR], k == 0, k == KD - 1)
                    mm.then_inc(score_full, 1)
                if kind == "V":
                    h, c = e[1:]
                    slot, _ = value_bank(h, c)
                    if h == 1 and c < 2:
                        pe.wait_ge(t_done, Batch(b.off - 1, b.turn).use(("T", 2, c)) + 1)
                    else:
                        pe.wait_ge(t_done, b.use(("T", h, c)) + 1)
                    if h == 0 and c % 4 == 0:
                        wait(pe, val_done, b, 4, c // 4 + 1)
                    for k in range(KD):
                        if c == 0:
                            wait(pe, out_done, b, 4, k - 1 - 2 * h)
                        mm = split_pair(pe, o_bank[k][:, :], lambda q: val[:, c, q, k * P:(k + 1) * P],
                                        lambda q: probT[:, slot, q, :], c == 0, c == CH - 1)
                    mm.then_inc(pv_done, 1)
        periods(pe, lambda b, x, y: (half(b, x), half(b, y)))


def constants(nc, ctx):
    return {"ident": ctx.enter_context(nc.sbuf_tensor("ident", [P, P], F32)),
            "neghalf": ctx.enter_context(nc.sbuf_tensor("neghalf", [P, 16], F32))}


def shared(nc, ctx):
    def sb(name, shape, dt):
        return ctx.enter_context(nc.sbuf_tensor(name, shape, dt))

    return {
        "g1": sb("g1", [P, D], F32),
        "b1": sb("b1", [P, D], F32),
        "bias": sb("bias", [P, KEYS + 1], BF16),
        "qblk": sb("qblk", [P, PAIRS, 2, P], F32R),
        "wk": sb("wk", [P, PAIRS, 2, D], F32R),
        "wv": sb("wv", [P, KD, 2, INNER], F32R),
    }


def block_2(nc, ins, y_scratch, x2, xn2T, W, ctx):
    def sb(name, shape, dt):
        return ctx.enter_context(nc.sbuf_tensor(name, shape, dt))

    def sem(name):
        return ctx.enter_context(nc.semaphore(name))

    H, DH = 16, D // 16
    yraw = sb("yraw", [P, 2, 2, PAIRS, L], F32)
    ysplit = sb("ysplit", [P, 2, 2, PAIRS, 2, L], F32R)
    xin = sb("xin", [P, RT, D], F32)
    x1 = sb("x1", [P, RT, D], F32)
    xn = sb("xn", [P, 2, D], F32)
    xnT = sb("xnT", [P, 2, 2, KD, 2 * P], F32R)
    wout = sb("wout", [P, PAIRS, 2, D], F32R)
    wqk = sb("wqk", [P, KD, 2, 2 * D], F32R)
    wv = sb("wv_self", [P, KD, 2, D], F32R)
    wo = sb("wo_self", [P, KD, 2, D], F32R)
    wtmp = sb("wtmp", [P, PAIRS * D + 4 * KD * D], F32)
    bqk = sb("bqk", [P, 2 * D], F32)
    bv = sb("bv", [P, D], F32)
    bo = sb("bo", [P, D], F32)
    rot = sb("rot", [P, 2, 8], F32)
    causal = sb("causal", [P, L], F32)
    headmask = sb("headmask", [P, 8], F32)
    vmask = sb("vmask", [P, D], F32)
    qk = sb("qk", [P, 2, 2 * D], F32)
    rc = sb("rc", [P, 2, 2 * D], F32)
    rs = sb("rs", [P, 2, 2 * D], F32)
    rqk = sb("rqk", [P, 2, 2 * D], F32)
    vblk = sb("vblk", [P, 2, 2, D], F32)
    qT = sb("qT", [P, 2, 4, P], F32)
    kblk = sb("kblk", [P, 2, 2, 2, 8, L], F32)
    sc = sb("sc", [P, 2, H, L], F32)
    mx = sb("mx", [P, 2, H], F32)
    sm = sb("sm", [P, 2, H], F32)
    rsm = sb("rsm", [P, 2, H], F32)
    pt = sb("pt", [P, 2, PAIRS, P], F32)
    att = sb("att", [P, 2, D], F32)
    attT = sb("attT", [P, 2, KD, 2, P], F32R)
    xn2 = sb("xn2", [P, 2, D], F32)
    st = sb("st2", [P, 2, 2, 6], F32)
    mv = sb("mv2", [P, 2, 2, 2], F32)
    ve = sb("ve2", [P, 2, 2], F32)
    rstd = sb("rstd2", [P, 2, 2], F32)
    bank = [ctx.enter_context(nc.psum_tensor(f"bank2_{n}", [P, 512], F32)) for n in range(8)]

    w_in = [sem(f"w2_in{n}") for n in range(4)]
    c_in = sem("c2_in")
    x_in = sem("x2_in")
    y_in = [sem(f"y2_in{n}") for n in range(2)]
    wh_done, wol_done, wl_done = sem("w2_high"), sem("wout_low"), sem("w2_low")
    y0_low = sem("y0_low")
    k_first = sem("k_first")
    pool_mask = sem("pool_mask")
    names = ("y_high y_low x1_full x1_done a_stat a_rstd xn_done xnT_full xnT_high xnT_low qk_full v_full qk_biased v_masked "
             "rot_cs rot_done v_done x1b_done r_full qT_done k_done s_full s_max s_exp sum_done p_full p_out pv_full att_done "
             "attT_full attT_high attT_low o_full x2_done d_stat d_rstd xn2_done xn2T_full xn2T_high xn2T_low").split()
    S = {n: sem(n) for n in names}
    own = {n: sem(f"own_{n}") for n in ("dve", "pool")}

    def stages(run):
        for s in range(-2, RT + 4):
            for name, lag in (("d3n", 4), ("a1", 0), ("d3", 4), ("a2n", 0), ("c1", 2), ("d1", 3), ("b1", 1), ("c1m", 2),
                              ("a2", 0), ("d2", 3), ("b1v", 1), ("c2", 2), ("b2", 1), ("c3", 2), ("a0", -2)):
                if 0 <= s - lag < RT:
                    run(name, s - lag)

    def twice(ap):
        return ap.rearrange("p (a l) -> p a l", l=L).unsqueeze(2).to_broadcast([P, 2 * KD, 2, L])

    def doubled(ap):
        return ap.rearrange("p k (b u l) -> p (k b) u l", b=2, u=2)

    def key_blocks(eng, z, t, j, done):
        eng.wait_ge(S["qT_done"], t + 1)
        if t >= 2:
            eng.wait_ge(S["s_full"], t - 1)
        for b in range(2):
            src = qT[:, z, 2 + j, b * L:b * L + L]
            eng.tensor_tensor(kblk[:, z, j, b, :, :], src.unsqueeze(1).to_broadcast([P, 8, L]),
                              headmask[:, :].unsqueeze(2).to_broadcast([P, 8, L]), ALU.mult).then_inc(done, 1)

    def y_low(eng, t):
        eng.wait_ge(S["y_high"], t + 1)
        eng.tensor_tensor(ysplit[:, t % 2, 1, :, :, :], yraw[:, t % 2, :, :, :].rearrange("p b a l -> p a b l"),
                          ysplit[:, t % 2, 0, :, :, :].bitcast(F32), ALU.subtract
                          ).then_inc(y0_low if t == 0 else S["y_low"], 1)

    def wait_y_low(eng, t):
        if t == 0:
            eng.wait_ge(y0_low, 1)
        else:
            eng.wait_ge(S["y_low"], t)

    class Chain:

        def __init__(self, eng, sem_):
            self.eng, self.sem, self.n = eng, sem_, 0

        def __call__(self, ins):
            self.n += 1
            ins.then_inc(self.sem, 1)
            self.eng.wait_ge(self.sem, self.n)

    weights = []
    at = 0
    for name, to, k in (("wout", wout, PAIRS), ("wqk", wqk, KD), ("wvs", wv, KD), ("wos", wo, KD)):
        n = to.shape[-1]
        weights.append((name, wtmp[:, at:at + k * n].rearrange("p (k n) -> p k n", k=k), to))
        at += k * n

    block = ctx.enter_context(nc.Block())

    @block.sync
    def _(sp):
        def load_weight(n):
            name, tmp, _ = weights[n]
            sp.dma_start(tmp, ins[name].rearrange("(k p) n -> p k n", p=P)).then_inc(w_in[n], 16)

        def load_y(rt):
            if rt >= 2:
                wait_y_low(sp, rt - 2)
            sp.dma_start(yraw[:, rt % 2, :, :, :].rearrange("p b a l -> p b (a l)"),
                         y_scratch[2 * rt:2 * rt + 2].rearrange("b p a l -> p b (a l)")).then_inc(y_in[rt % 2], 16)
        load_weight(0)
        load_y(0)
        load_weight(1)
        load_weight(2)
        load_y(1)
        sp.dma_start(xin[:, :, :], ins["x"].rearrange("(t p) d -> p t d", p=P)).then_inc(x_in, 16)
        for to, name in ((bqk, "bqk"), (bv, "bv"), (bo, "bo")):
            sp.dma_start(to[:, :], ins[name].partition_broadcast(P)).then_inc(c_in, 16)
        sp.dma_start(rot[:, :, :], ins["rot"]).then_inc(c_in, 16)
        for to, name in ((causal, "causal"), (headmask, "headmask"), (vmask, "vmask")):
            sp.dma_start(to[:, :], ins[name]).then_inc(c_in, 16)
        load_weight(3)
        for rt in range(2, RT):
            load_y(rt)

    @block.scalar
    def _(act):
        def high_weight(n):
            _, tmp, to = weights[n]
            act.wait_ge(w_in[n], 16)
            act.activation(to[:, :, 0, :], tmp, ACT.Copy).then_inc(wh_done, 1)

        high_weight(0)

        def run(name, t):
            z = t % 2
            if name == "a0":
                act.wait_ge(y_in[z], 16 * (t // 2 + 1))
                if t >= 2:
                    act.wait_ge(S["x1_full"], t - 1)
                act.activation(ysplit[:, z, 0, :, :, :], yraw[:, z, :, :, :].rearrange("p b a l -> p a b l"), ACT.Copy
                               ).then_inc(S["y_high"], 1)
                if t == 0:
                    for n in (1, 2, 3):
                        high_weight(n)
            if name == "a2":
                act.wait_ge(S["xnT_full"], t + 1)
                if t >= 2:
                    act.wait_ge(S["v_full"], t - 1)
                act.activation(doubled(xnT[:, z, 0, :, :]), twice(bank[1][:, 0:D]), ACT.Copy
                               ).then_inc(S["xnT_high"], 1)
            if name == "b2":
                act.wait_ge(S["r_full"], t + 1)
                if t >= 2:
                    act.wait_ge(S["s_full"], t - 1)
                    act.wait_ge(S["k_done"], 2 * t - 2)
                    act.wait_ge(k_first, 2 * t - 2)
                act.activation(qT[:, z, :, :], bank[2][:, :].rearrange("p (k x) -> p k x", k=4), ACT.Copy
                               ).then_inc(S["qT_done"], 1)
            if name == "c1m":
                act.wait_ge(S["s_max"], t + 1)
                act.activation(sc[:, z, :, :], sc[:, z, :, :], ACT.Exp, scale=DH ** -0.5).then_inc(S["s_exp"], 1)
            if name == "c2":
                for r in range(2):
                    act.wait_ge(S["p_full"], 2 * t + r + 1)
                    if t >= 2:
                        act.wait_ge(S["pv_full"], t - 1)
                    act.activation(pt[:, z, 4 * r:4 * r + 4, :], bank[(6, 4)[r]][:, :].rearrange("p (a x) -> p a x", a=4),
                                   ACT.Copy).then_inc(S["p_out"], 1)
            if name == "d1":
                act.wait_ge(S["attT_full"], t + 1)
                if t >= 2:
                    act.wait_ge(S["o_full"], t - 1)
                act.activation(attT[:, z, :, 0, :], bank[7][:, 0:D].rearrange("p (k x) -> p k x", k=KD), ACT.Copy
                               ).then_inc(S["attT_high"], 1)
            if name == "d3":
                act.wait_ge(S["xn2T_full"], t + 1)
                act.activation(xn2T[:, :, 0, t * P:(t + 1) * P], bank[7][:, 0:D].rearrange("p (k x) -> p k x", k=KD),
                               ACT.Copy).then_inc(S["xn2T_high"], 1)
        stages(run)

    @block.gpsimd
    def _(pool):
        link = Chain(pool, own["pool"])
        for n in (1, 2, 3):
            _, tmp, to = weights[n]
            pool.wait_ge(wh_done, n + 1)
            pool.tensor_tensor(to[:, :, 1, :], tmp, to[:, :, 0, :].bitcast(F32), ALU.subtract).then_inc(wl_done, 1)
        pool.wait_ge(c_in, 16 * 7)
        pool.tensor_tensor(bv[:, :], bv[:, :], vmask[:, :], ALU.mult).then_inc(pool_mask, 1)
        pool.wait_ge(pool_mask, 1)

        def moments(chain, z, t, stat, done):
            pool.wait_ge(S[stat], t + 1)
            link(pool.tensor_scalar(ve[:, chain, z:z + 1], mv[:, chain, z, 1:2], 1.0, EPS, ALU.mult, ALU.add))
            pool.tensor_tensor(rstd[:, chain, z:z + 1], ve[:, chain, z:z + 1], W["neghalf"][:, 0:1], ALU.pow
                               ).then_inc(S[done], 1)

        def run(name, t):
            z = t % 2
            if name == "a1":
                moments(0, z, t, "a_stat", "a_rstd")
            if name == "b1":
                pool.wait_ge(S["qk_biased"], t + 1)
                if t >= 2:
                    pool.wait_ge(S["r_full"], t - 1)
                cos, sin = (rot[:, n, :].unsqueeze(1).to_broadcast([P, 64, 8]) for n in range(2))
                src = qk[:, z, :].rearrange("p (a i) -> p a i", i=8)
                link(pool.tensor_tensor(rc[:, z, :].rearrange("p (a i) -> p a i", i=8), src, cos, ALU.mult))
                link(pool.tensor_tensor(rs[:, z, :].rearrange("p (a i) -> p a i", i=8), src, sin, ALU.mult))
                c, s, r = (m[:, z, :].rearrange("p (h two i) -> p h two i", two=2, i=8) for m in (rc, rs, rqk))
                pool.tensor_tensor(r[:, :, 0, :], c[:, :, 0, :], s[:, :, 1, :], ALU.subtract).then_inc(S["rot_done"], 1)
                pool.tensor_tensor(r[:, :, 1, :], s[:, :, 0, :], c[:, :, 1, :], ALU.add).then_inc(S["rot_done"], 1)
                pool.wait_ge(S["v_masked"], t + 1)
                pool.tensor_tensor(vblk[:, z, :, :], vblk[:, z, :, :], bv[:, :].unsqueeze(1).to_broadcast([P, 2, D]), ALU.add
                                   ).then_inc(S["v_done"], 1)
                pool.wait_ge(S["xn_done"], t + 1)
                pool.tensor_tensor(x1[:, t, :], x1[:, t, :], bo[:, :], ALU.add).then_inc(S["x1b_done"], 1)
            if name == "d2":
                moments(1, z, t, "d_stat", "d_rstd")
            if name == "b2":
                key_blocks(pool, z, t, 1, S["k_done"])
            if name == "a0" and t > 0:
                y_low(pool, t)
        stages(run)

    @block.vector
    def _(dve):
        link = Chain(dve, own["dve"])
        _, tmp, to = weights[0]
        dve.wait_ge(wh_done, 1)
        dve.tensor_tensor(to[:, :, 1, :], tmp, to[:, :, 0, :].bitcast(F32), ALU.subtract).then_inc(wol_done, 1)
        y_low(dve, 0)
        dve.wait_ge(c_in, 16 * 7)
        dve.wait_ge(x_in, 16)

        def low(to, src, high, done):
            dve.tensor_tensor(to, src, high.bitcast(F32), ALU.subtract).then_inc(S[done], 1)

        def run(name, t):
            z = t % 2
            if name == "a1":
                dve.wait_ge(S["x1_full"], t + 1)
                dve.tensor_tensor(x1[:, t, :], bank[0][:, 0:D], xin[:, t, :], ALU.add).then_inc(S["x1_done"], 1)
                dve.wait_ge(S["x1_done"], t + 1)
                link(dve.bn_stats(st[:, 0, z, :], x1[:, t, :]))
                dve.bn_aggr(mv[:, 0, z, :], st[:, 0, z, :]).then_inc(S["a_stat"], 1)
            if name == "a2n":
                dve.wait_ge(S["a_rstd"], t + 1)
                if t >= 2:
                    dve.wait_ge(S["xnT_full"], t - 1)
                dve.tensor_scalar(xn[:, z, :], x1[:, t, :], mv[:, 0, z, 0:1], rstd[:, 0, z:z + 1], ALU.subtract, ALU.mult
                                  ).then_inc(S["xn_done"], 1)
            if name == "a2":
                dve.wait_ge(S["xnT_high"], t + 1)
                low(doubled(xnT[:, z, 1, :, :]), twice(bank[1][:, 0:D]), doubled(xnT[:, z, 0, :, :]), "xnT_low")
            if name == "b1":
                dve.wait_ge(S["qk_full"], t + 1)
                if t >= 2:
                    dve.wait_ge(S["rot_done"], 2 * t - 2)
                dve.tensor_tensor(qk[:, z, :], bank[2][:, :], bqk[:, :], ALU.add).then_inc(S["qk_biased"], 1)
            if name == "b1v":
                dve.wait_ge(S["v_full"], t + 1)
                if t >= 2:
                    dve.wait_ge(S["pv_full"], t - 1)
                dve.tensor_tensor(vblk[:, z, :, :], bank[3][:, :].rearrange("p (b d) -> p b d", b=2),
                                  vmask[:, :].unsqueeze(1).to_broadcast([P, 2, D]), ALU.mult).then_inc(S["v_masked"], 1)
            if name == "b2":
                key_blocks(dve, z, t, 0, k_first)
            if name == "c1":
                dve.wait_ge(S["s_full"], t + 1)
                for j in range(2):
                    link(dve.tensor_tensor(sc[:, z, 8 * j:8 * j + 8, :], bank[4 + j][:, :].rearrange("p (h s) -> p h s", h=8),
                                           causal[:, :].unsqueeze(1).to_broadcast([P, 8, L]), ALU.add))
            if name == "c1m":
                link(dve.tensor_reduce(mx[:, z, :], sc[:, z, :, :], AX.X, ALU.max))
                dve.tensor_tensor(sc[:, z, :, :], sc[:, z, :, :], mx[:, z, :].unsqueeze(2).to_broadcast([P, H, L]),
                                  ALU.subtract).then_inc(S["s_max"], 1)
            if name == "c2":
                dve.wait_ge(S["s_exp"], t + 1)
                link(dve.tensor_reduce(sm[:, z, :], sc[:, z, :, :], AX.X, ALU.add))
                dve.reciprocal(rsm[:, z, :], sm[:, z, :]).then_inc(S["sum_done"], 1)
            if name == "c3":
                dve.wait_ge(S["sum_done"], t + 1)
                dve.wait_ge(S["pv_full"], t + 1)
                if t >= 2:
                    dve.wait_ge(S["attT_full"], t - 1)
                dve.tensor_tensor(att[:, z, :].rearrange("p (h i) -> p h i", h=H), bank[5][:, 0:D].rearrange("p (h i) -> p h i", h=H),
                                  rsm[:, z, :].unsqueeze(2).to_broadcast([P, H, DH]), ALU.mult).then_inc(S["att_done"], 1)
            if name == "d1":
                dve.wait_ge(S["attT_high"], t + 1)
                low(attT[:, z, :, 1, :], bank[7][:, 0:D].rearrange("p (k x) -> p k x", k=KD), attT[:, z, :, 0, :], "attT_low")
            if name == "d2":
                dve.wait_ge(S["o_full"], t + 1)
                dve.wait_ge(S["x1b_done"], t + 1)
                dve.tensor_tensor(x2[:, t, :], bank[7][:, 0:D], x1[:, t, :], ALU.add).then_inc(S["x2_done"], 1)
                dve.wait_ge(S["x2_done"], t + 1)
                link(dve.bn_stats(st[:, 1, z, :], x2[:, t, :]))
                dve.bn_aggr(mv[:, 1, z, :], st[:, 1, z, :]).then_inc(S["d_stat"], 1)
            if name == "d3n":
                dve.wait_ge(S["d_rstd"], t + 1)
                if t >= 2:
                    dve.wait_ge(S["xn2T_full"], t - 1)
                dve.tensor_scalar(xn2[:, z, :], x2[:, t, :], mv[:, 1, z, 0:1], rstd[:, 1, z:z + 1], ALU.subtract, ALU.mult
                                  ).then_inc(S["xn2_done"], 1)
            if name == "d3":
                dve.wait_ge(S["xn2T_high"], t + 1)
                low(xn2T[:, :, 1, t * P:(t + 1) * P], bank[7][:, 0:D].rearrange("p (k x) -> p k x", k=KD),
                    xn2T[:, :, 0, t * P:(t + 1) * P], "xn2T_low")
        stages(run)

    @block.tensor
    def _(pe):
        ident = W["ident"]
        def run(name, t):
            z = t % 2
            if name == "a1":
                pe.wait_ge(wol_done, 1)
                wait_y_low(pe, t)
                if t >= 1:
                    pe.wait_ge(S["x1_done"], t)
                for a in range(PAIRS):
                    mm = split_pair(pe, bank[0][:, 0:D], lambda q: ysplit[:, z, q, a, :, :].rearrange("p b l -> p (b l)"),
                                    lambda q: wout[:, a, q, :], a == 0, a == PAIRS - 1)
                mm.then_inc(S["x1_full"], 1)
            if name == "a2":
                pe.wait_ge(S["xn_done"], t + 1)
                if t >= 1:
                    pe.wait_ge(S["xnT_low"], t)
                for k in range(KD):
                    mm = pe.transpose(bank[1][:, k * P:(k + 1) * P], xn[:, z, k * P:(k + 1) * P], ident[:, :])
                mm.then_inc(S["xnT_full"], 1)
            if name == "b1":
                pe.wait_ge(S["xnT_low"], t + 1)
                pe.wait_ge(wl_done, 2)
                if t >= 1:
                    pe.wait_ge(S["qT_done"], t)
                for k in range(KD):
                    mm = split_pair(pe, bank[2][:, :], lambda q: xnT[:, z, q, k, L:L + P], lambda q: wqk[:, k, q, :],
                                    k == 0, k == KD - 1)
                mm.then_inc(S["qk_full"], 1)
                if t >= 1:
                    pe.wait_ge(S["v_masked"], t)
                for b in range(2):
                    for k in range(KD):
                        mm = split_pair(pe, bank[3][:, b * D:(b + 1) * D],
                                        lambda q: xnT[:, z, q, k, b * P:(b + 1) * P],
                                        lambda q: wv[:, k, q, :], k == 0, k == KD - 1)
                mm.then_inc(S["v_full"], 1)
            if name == "b2":
                pe.wait_ge(S["rot_done"], 2 * t + 2)
                pe.wait_ge(S["qk_biased"], t + 1)
                for n in range(4):
                    mm = pe.transpose(bank[2][:, n * P:(n + 1) * P], rqk[:, z, n * P:(n + 1) * P], ident[:, :])
                mm.then_inc(S["r_full"], 1)
            if name == "c1":
                pe.wait_ge(k_first, 2 * t + 2)
                pe.wait_ge(S["k_done"], 2 * t + 2)
                if t >= 1:
                    pe.wait_ge(S["p_out"], 2 * t)
                    pe.wait_ge(S["att_done"], t)
                for j in range(2):
                    for b in range(2):
                        mm = pe.matmul(bank[4 + j][b * L:(b + 1) * L, :], qT[:, z, j, b * L:(b + 1) * L],
                                       kblk[:, z, j, b, :, :].rearrange("p h s -> p (h s)"), start=True, stop=True)
                mm.then_inc(S["s_full"], 1)
            if name == "c2":
                pe.wait_ge(S["s_exp"], t + 1)
                if t >= 1:
                    pe.wait_ge(S["p_out"], 2 * t - 1)
                for r in range(2):
                    for a in range(4):
                        hh = 8 * r + 2 * a
                        mm = pe.transpose(bank[(6, 4)[r]][:, a * P:(a + 1) * P],
                                          sc[:, z, hh:hh + 2, :].rearrange("p h s -> p (h s)"), ident[:, :])
                    mm.then_inc(S["p_full"], 1)
            if name == "c3":
                pe.wait_ge(S["p_out"], 2 * t + 2)
                pe.wait_ge(S["v_done"], t + 1)
                for b in range(2):
                    for a in range(PAIRS):
                        mm = pe.matmul(bank[5][b * L:(b + 1) * L, a * 32:(a + 1) * 32], pt[:, z, a, b * L:(b + 1) * L],
                                       vblk[:, z, b, a * 32:(a + 1) * 32], start=True, stop=True)
                mm.then_inc(S["pv_full"], 1)
            if name == "d1":
                pe.wait_ge(S["att_done"], t + 1)
                if t >= 1:
                    pe.wait_ge(S["xn2T_low"], t)
                for k in range(KD):
                    mm = pe.transpose(bank[7][:, k * P:(k + 1) * P], att[:, z, k * P:(k + 1) * P], ident[:, :])
                mm.then_inc(S["attT_full"], 1)
            if name == "d2":
                pe.wait_ge(S["attT_low"], t + 1)
                pe.wait_ge(wl_done, 3)
                for k in range(KD):
                    mm = split_pair(pe, bank[7][:, 0:D], lambda q: attT[:, z, k, q, :], lambda q: wo[:, k, q, :],
                                    k == 0, k == KD - 1)
                mm.then_inc(S["o_full"], 1)
            if name == "d3":
                pe.wait_ge(S["xn2_done"], t + 1)
                for k in range(KD):
                    mm = pe.transpose(bank[7][:, k * P:(k + 1) * P], xn2[:, z, k * P:(k + 1) * P], ident[:, :])
                mm.then_inc(S["xn2T_full"], 1)
        stages(run)


E4, HID = 4, 1024
HT = HID // P


def block_3(nc, ins, out, x2, xn2T, ctx):
    def sb(name, shape, dt):
        return ctx.enter_context(nc.sbuf_tensor(name, shape, dt))

    def sem(name):
        return ctx.enter_context(nc.semaphore(name))

    w1raw = sb("w1raw", [P, KD, HID], F32)
    w2raw = sb("w2raw", [P, HT, D], F32)
    w1 = sb("w1", [P, KD, 2, HID], F32R)
    w2 = sb("w2", [P, HT, 2, D], F32R)
    b1 = sb("b1e", [P, 2, HT], F32)
    b2 = sb("b2e", [P, E4, D], F32)
    gb = sb("gb", [P, HT], F32)
    gbs = sb("gbs", [P, 2, HT, P], F32R)
    hid = sb("hid", [P, 3, 512], F32)
    hT = sb("hT", [P, HT, 2, ROWS], F32R)
    cexp = sb("cexp", [P, D], F32)
    csum = sb("csum", [P, D], F32)
    ydiff = sb("ydiff", [P, 2, D], F32)
    wrraw = sb("wrraw", [P, KD, E4], F32)
    wr = sb("wr", [P, KD, 2, E4], F32R)
    br = sb("br", [P, E4], F32)
    logit = sb("logit", [P, RT, E4], F32)
    rank = sb("rank", [P, RT, E4], F32)
    cmp = sb("cmp", [P, RT, E4], F32)
    top = sb("top", [P, RT], F32)
    gate = sb("gate", [P, RT, E4], F32)
    gsum = sb("gsum", [P, RT], F32)
    gcur = sb("gcur", [P, RT], F32)
    hbank = [ctx.enter_context(nc.psum_tensor(f"hbank{n}", [P, 512], F32)) for n in range(3)]
    ybank = [ctx.enter_context(nc.psum_tensor(f"ybank{n}", [P, 512], F32)) for n in range(3)]
    rbank = ctx.enter_context(nc.psum_tensor("rbank", [P, 512], F32))

    r_in = sem("r_in")
    b2_in = sem("b2_in")
    w1_in, w2_in, b1_in = sem("w1_in"), sem("w2_in3"), sem("b1_in")
    wr_high, wr_done = sem("wr_high"), sem("wr_done")
    r_full = sem("router_full")
    g_max, g_exp, g_done = sem("g_max"), sem("g_exp"), sem("g_done")
    own = sem("own_dve3")
    w1_high, w1_done = sem("w1_high"), sem("w1_done")
    w2_high, w2_done = sem("w2_high3"), sem("w2_done3")
    gb_done, gb_high, gb_low = sem("gb_done"), sem("gb_high"), sem("gb_low")
    h_full = sem("h_full")
    h_gelu = sem("h_gelu")
    h_high = sem("h_high")
    h_done = sem("h_done")
    y_full = sem("y_full")
    y_got = sem("y_got")
    y_add = sem("y_add")
    c_add = sem("c_add")
    g_cur = sem("g_cur")
    fin_done = sem("fin_done")
    out_done3 = sem("out_done3")

    def experts(eng, body):
        body(Batch(0), True)
        with eng.Fori(0, E4 - 2) as turn:
            body(Batch(1, turn), True)
        body(Batch(E4 - 1), False)

    block = ctx.enter_context(nc.Block())

    @block.sync
    def _(sp):
        def load_w1(n):
            wait(sp, w1_done, n, 1, 0)
            sp.dma_start(w1raw[:, :, :], ins["w1"][n.lin(1, 0)].rearrange("(k p) n -> p k n", p=P)).then_inc(w1_in, 16)

        def load_w2(n):
            wait(sp, w2_done, n, 1, 0)
            sp.dma_start(w2raw[:, :, :], ins["w2"][n.lin(1, 0)].rearrange("(k p) n -> p k n", p=P)).then_inc(w2_in, 16)
            wait(sp, h_gelu, n, 16, 0)
            wait(sp, gb_done, n, 1, 0)
            sp.dma_start(b1[:, 0, :], ins["b1"][n.lin(1, 0)]).then_inc(b1_in, 16)

        sp.dma_start(wrraw[:, :, :], ins["wr"].rearrange("(k p) n -> p k n", p=P)).then_inc(r_in, 16)
        sp.dma_start(br[:, :], ins["br"].partition_broadcast(P)).then_inc(r_in, 16)
        load_w1(Batch(0))
        load_w2(Batch(0))
        sp.dma_start(b2[:, :, :].rearrange("p e d -> p (e d)"), ins["b2e"].partition_broadcast(P)).then_inc(b2_in, 16)

        def body(e, more):
            if more:
                n = Batch(e.off + 1, e.turn)
                load_w1(n)
                load_w2(n)
        experts(sp, body)
        for t in range(RT):
            sp.wait_ge(fin_done, t + 1)
            sp.dma_start(out[t * P:(t + 1) * P, :], x2[:, t, :]).then_inc(out_done3, 16)
        sp.wait_ge(out_done3, 16 * RT)

    @block.scalar
    def _(act):
        def split_w1(e):
            wait(act, w1_in, e, 16, 16)
            wait(act, h_full, e, 16, 0)
            act.activation(w1[:, :, 0, :], w1raw[:, :, :], ACT.Copy).then_inc(w1_high, 1)

        act.wait_ge(r_in, 32)
        act.activation(wr[:, :, 0, :], wrraw[:, :, :], ACT.Copy).then_inc(wr_high, 1)
        act.wait_ge(g_max, 1)
        act.activation(gate[:, :, :], gate[:, :, :], ACT.Exp).then_inc(g_exp, 1)
        split_w1(Batch(0))

        def body(e, more):
            wait(act, b1_in, e, 16, 16)
            act.activation(gb[:, :], b1[:, 0, :], ACT.Gelu).then_inc(gb_done, 1)
            wait(act, w2_in, e, 16, 16)
            wait(act, y_full, e, 9, 0)
            wait(act, gb_done, e, 1, 1)
            act.activation(gbs[:, 0, :, :], gb[:, :].unsqueeze(2).to_broadcast([P, HT, P]), ACT.Copy).then_inc(gb_high, 1)
            for m in range(2 * HT):
                half, t = divmod(m, HT)
                z = m % 2
                s = slice(half * 512, half * 512 + 512)
                wait(act, h_full, e, 16, m + 1)
                wait(act, h_done, e, 16, m - 1)
                act.activation(hid[:, z, :], hbank[z][:, :], ACT.Gelu, bias=b1[:, 0, t:t + 1]).then_inc(h_gelu, 1)
                wait(act, h_gelu, e, 16, m + 1)
                act.activation(hT[:, t, 0, s], hid[:, z, :], ACT.Copy).then_inc(h_high, 1)
                if m == 3:
                    act.activation(w2[:, :, 0, :], w2raw[:, :, :], ACT.Copy).then_inc(w2_high, 1)
            if more:
                split_w1(Batch(e.off + 1, e.turn))
        experts(act, body)

    @block.vector
    def _(dve):
        chain = [0]

        def link(ins):
            chain[0] += 1
            ins.then_inc(own, 1)
            dve.wait_ge(own, chain[0])

        def split_w1(e):
            wait(dve, w1_high, e, 1, 1)
            dve.tensor_tensor(w1[:, :, 1, :], w1raw[:, :, :], w1[:, :, 0, :].bitcast(F32), ALU.subtract).then_inc(w1_done, 1)

        dve.wait_ge(wr_high, 1)
        dve.tensor_tensor(wr[:, :, 1, :], wrraw[:, :, :], wr[:, :, 0, :].bitcast(F32), ALU.subtract).then_inc(wr_done, 1)
        dve.wait_ge(r_full, 1)
        dve.wait_ge(r_in, 32)
        link(dve.tensor_tensor(logit[:, :, :], rbank[:, 0:RT * E4].rearrange("p (t e) -> p t e", e=E4),
                               br[:, :].unsqueeze(1).to_broadcast([P, RT, E4]), ALU.add))
        for e in range(E4):
            mine = logit[:, :, e:e + 1].to_broadcast([P, RT, E4])
            link(dve.tensor_tensor(cmp[:, :, :], logit[:, :, :], mine, ALU.is_gt))
            if e:
                link(dve.tensor_tensor(cmp[:, :, 0:e], logit[:, :, 0:e], logit[:, :, e:e + 1].to_broadcast([P, RT, e]), ALU.is_ge))
            link(dve.tensor_reduce(rank[:, :, e:e + 1], cmp[:, :, :], AX.X, ALU.add))
        link(dve.tensor_scalar(rank[:, :, :], rank[:, :, :], 2.0, None, ALU.is_lt))
        link(dve.tensor_reduce(top[:, :], logit[:, :, :], AX.X, ALU.max))
        dve.tensor_tensor(gate[:, :, :], logit[:, :, :], top[:, :].unsqueeze(2).to_broadcast([P, RT, E4]), ALU.subtract
                          ).then_inc(g_max, 1)
        dve.wait_ge(g_exp, 1)
        link(dve.tensor_tensor(gate[:, :, :], gate[:, :, :], rank[:, :, :], ALU.mult))
        link(dve.tensor_reduce(gsum[:, :], gate[:, :, :], AX.X, ALU.add))
        link(dve.reciprocal(gsum[:, :], gsum[:, :]))
        link(dve.tensor_tensor(gate[:, :, :], gate[:, :, :], gsum[:, :].unsqueeze(2).to_broadcast([P, RT, E4]), ALU.mult))
        dve.wait_ge(b2_in, 16)
        link(dve.tensor_tensor(b2[:, 0, :], b2[:, 0, :], b2[:, 1, :], ALU.add))
        link(dve.tensor_tensor(b2[:, 2, :], b2[:, 2, :], b2[:, 3, :], ALU.add))
        dve.tensor_tensor(csum[:, :], b2[:, 0, :], b2[:, 2, :], ALU.add).then_inc(c_add, 1)
        split_w1(Batch(0))

        def body(e, more):
            wait(dve, gb_high, e, 1, 1)
            dve.tensor_tensor(gbs[:, 1, :, :], gb[:, :].unsqueeze(2).to_broadcast([P, HT, P]), gbs[:, 0, :, :].bitcast(F32),
                              ALU.subtract).then_inc(gb_low, 1)
            wait(dve, y_add, e, 8, 0)
            dve.tensor_copy(gcur[:, :], gate[:, :, e.lin(1, 0)]).then_inc(g_cur, 1)
            for m in range(2 * HT):
                half, t = divmod(m, HT)
                s = slice(half * 512, half * 512 + 512)
                wait(dve, h_high, e, 16, m + 1)
                dve.tensor_tensor(hT[:, t, 1, s], hid[:, m % 2, :], hT[:, t, 0, s].bitcast(F32), ALU.subtract).then_inc(h_done, 1)
                if m == 3:
                    wait(dve, w2_high, e, 1, 1)
                    dve.tensor_tensor(w2[:, :, 1, :], w2raw[:, :, :], w2[:, :, 0, :].bitcast(F32), ALU.subtract
                                      ).then_inc(w2_done, 1)
            if more:
                split_w1(Batch(e.off + 1, e.turn))
            wait(dve, y_full, e, 9, 1)
            dve.tensor_copy(cexp[:, :], ybank[0][:, 0:D]).then_inc(y_got, 1)
            wait(dve, y_got, e, 9, 1)
            wait(dve, c_add, e, 1, 1)
            dve.tensor_tensor(csum[:, :], csum[:, :], cexp[:, :], ALU.add).then_inc(c_add, 1)
            wait(dve, g_cur, e, 1, 1)
            for t in range(RT):
                wait(dve, y_full, e, 9, t + 2)
                wait(dve, y_add, e, 8, t - 1)
                dve.tensor_tensor(ydiff[:, t % 2, :], ybank[(t + 1) % 3][:, 0:D], cexp[:, :], ALU.subtract).then_inc(y_got, 1)
                wait(dve, y_got, e, 9, t + 2)
                dve.scalar_tensor_tensor(out=x2[:, t, :], in0=ydiff[:, t % 2, :], scalar=gcur[:, t:t + 1], in1=x2[:, t, :],
                                         op0=ALU.mult, op1=ALU.add).then_inc(y_add, 1)
        experts(dve, body)
        dve.wait_ge(c_add, E4 + 1)
        dve.wait_ge(y_add, RT * E4)
        for t in range(RT):
            dve.tensor_tensor(x2[:, t, :], x2[:, t, :], csum[:, :], ALU.add).then_inc(fin_done, 1)

    @block.tensor
    def _(pe):
        pe.wait_ge(wr_done, 1)
        for t in range(RT):
            for k in range(KD):
                mm = split_pair(pe, rbank[:, t * E4:(t + 1) * E4], lambda q: xn2T[:, k, q, t * P:(t + 1) * P],
                                lambda q: wr[:, k, q, :], k == 0, k == KD - 1)
        mm.then_inc(r_full, 1)

        def body(e, more):
            wait(pe, w1_done, e, 1, 1)
            for m in range(2 * HT):
                half, t = divmod(m, HT)
                s = slice(half * 512, half * 512 + 512)
                wait(pe, h_gelu, e, 16, m - 1)
                for k in range(KD):
                    mm = split_pair(pe, hbank[m % 2][:, :], lambda q: w1[:, k, q, t * P:(t + 1) * P],
                                    lambda q: xn2T[:, k, q, s], k == 0, k == KD - 1)
                mm.then_inc(h_full, 1)
            wait(pe, w2_done, e, 1, 1)
            wait(pe, gb_low, e, 1, 1)
            for r in range(RT + 1):
                if r == 1:
                    wait(pe, h_done, e, 16, 8)
                if r == 5:
                    wait(pe, h_done, e, 16, 16)
                wait(pe, y_got, e, 9, r - 2)
                for t in range(HT):
                    mm = split_pair(pe, ybank[r % 3][:, 0:D],
                                    (lambda q: gbs[:, q, t, :]) if r == 0 else (lambda q: hT[:, t, q, (r - 1) * P:r * P]),
                                    lambda q: w2[:, t, q, :], t == 0, t == HT - 1)
                mm.then_inc(y_full, 1)
        experts(pe, body)


def build(nc, ins, out, lat_scratch, q_scratch, y_scratch):
    with ExitStack() as ctx:
        W = constants(nc, ctx)
        with ExitStack() as cross:
            X = W | shared(nc, cross)
            F = Context(nc, ins, lat_scratch, q_scratch, X, cross)
            with ExitStack() as c:
                block_0(nc, ins, F, X, c)
            with ExitStack() as c:
                block_1(nc, F, y_scratch, X, c)
        with ExitStack() as kept:
            x2 = kept.enter_context(nc.sbuf_tensor("x2", [P, RT, D], F32))
            xn2T = kept.enter_context(nc.sbuf_tensor("xn2T", [P, KD, 2, ROWS], F32R))
            with ExitStack() as c:
                block_2(nc, ins, y_scratch, x2, xn2T, W, c)
            with ExitStack() as c:
                block_3(nc, ins, out, x2, xn2T, c)


def kernel(**inputs):
    import concourse.bacc as bacc
    from concourse.bass_utils import run_bass_kernel_spmd

    def flat(name):
        return np.ascontiguousarray(inputs[name])

    def lay(a):
        return np.ascontiguousarray(a)

    order = np.array([h * 16 + i for h in range(16) for i in (*range(0, 16, 2), *range(1, 16, 2))])
    wkv = flat("L0_xattn_Wkv")
    mask = flat("mask_BxS2_bk0")
    mask = np.concatenate([mask[:, :TAIL].reshape(B, P, CPP).transpose(0, 2, 1).reshape(B, TAIL), mask[:, TAIL:]], 1)
    half = np.arange(8, dtype=np.float32)
    theta = np.float32(1.0) / np.float32(10000.0) ** (half / np.float32(8))
    angle = (np.arange(P) % L).astype(np.float32)[:, None] * theta[None, :]
    parts = np.arange(P)
    arrays = {
        "x": lay(flat("x").reshape(ROWS, D)), "ctx": flat("ctx_1024"), "mask": lay(mask),
        "g1": flat("L0_xattn_g1"), "b1x": flat("L0_xattn_b1"), "g2": flat("L0_xattn_g2"), "b2x": flat("L0_xattn_b2"),
        "wq": flat("L0_xattn_Wq"), "wkT": lay(wkv[:, :INNER].T), "wv": lay(wkv[:, INNER:]), "wout": flat("L0_xattn_Wout"),
        "wqk": lay(np.concatenate([flat("L0_attn_W_q")[order], flat("L0_attn_W_k")[order]], 0).T),
        "wvs": lay(flat("L0_attn_W_v").T), "wos": lay(flat("L0_attn_W_o").T),
        "bqk": lay(np.concatenate([flat("L0_attn_b_q")[order], flat("L0_attn_b_k")[order]])),
        "bv": flat("L0_attn_b_v"), "bo": flat("L0_attn_b_o"),
        "w1": flat("L0_ffn_w1"), "w2": flat("L0_ffn_w2"), "b1": lay(flat("L0_ffn_b1").reshape(E4, HT, P).transpose(0, 2, 1)),
        "b2e": lay(flat("L0_ffn_b2").reshape(-1)), "wr": flat("L0_ffn_wr"), "br": flat("L0_ffn_br"),
        "rot": lay(np.stack([np.cos(angle), np.sin(angle)], 1).astype(np.float32)),
        "causal": lay(np.where(np.arange(L)[None, :] <= (parts % L)[:, None], 0.0, NEG).astype(np.float32)),
        "headmask": lay((parts[:, None] // 16 == np.arange(8)[None, :]).astype(np.float32)),
        "vmask": lay((parts[:, None] // L == (np.arange(D)[None, :] // 16) % 2).astype(np.float32)),
    }
    nc = bacc.Bacc("TRN2", target_bir_lowering=False, num_devices=1)
    in_map, ins = {}, {}
    for name, a in arrays.items():
        in_map[f"in_{name}"] = a
        ins[name] = nc.dram_tensor(f"in_{name}", a.shape, mybir.dt.from_np(a.dtype), kind="ExternalInput").ap()
    out = nc.dram_tensor("out", (ROWS, D), F32, kind="ExternalOutput").ap()
    lat_scratch = nc.dram_tensor("lat_scratch", (B, L, D), F32, kind="Internal").ap()
    q_scratch = nc.dram_tensor("q_scratch", (B, P, PAIRS, L), F32, kind="Internal").ap()
    y_scratch = nc.dram_tensor("y_scratch", (B, P, PAIRS, L), F32, kind="Internal").ap()
    build(nc, ins, out, lat_scratch, q_scratch, y_scratch)
    r = run_bass_kernel_spmd(nc, [in_map], core_ids=[0])
    return r.results[0]["out"].reshape(B, L, D)
```

```python
from contextlib import ExitStack

import numpy as np

import concourse.bass as bass
from concourse import mybir

ALU = mybir.AluOpType
ACT = mybir.ActivationFunctionType
AX = mybir.AxisListType
F32 = mybir.dt.float32
F32R = mybir.dt.float32r
BF16 = mybir.dt.bfloat16
U8 = mybir.dt.uint8

P = 128
B, L, D = 16, 64, 256
N = 1601
KD = D // P
HX, DX = 16, 64
PAIRS = HX // 2
INNER = HX * DX
E4, HID = 4, 1024
HT = HID // P
ROWS = B * L
RT = ROWS // P
CH = 13
KEYS = CH * P
LAST = N - 1
CPP = 12
TAIL = CPP * P
QTR = KEYS // 4
NEG = -3.0e38
EPS = 1e-5
GROUPS = [(0, 4), (4, 8), (8, 12), (12, 13)]

STAT = [*range(1, CH + 1), 0]

HL3 = ((0, 0), (0, 1), (1, 0))


X_UNITS = (0, 0, 1, 2, 4, 2, 0, 3, 0, 2, 0, 0, 0)
Y_UNITS = (0, 2, 2, 2, 2, 3, 0, 2, 0, 0, 0, 0, 0)
X_AT = {"P3": 10, "Y0": 1, "N0": 3, "N1": 7, "S4": 6, "S0": 10, "S1": 12}
Y_AT = {"P7": 9, "Y1": 2, "N2": 0, "N3": 0, "S2": 3, "S3": 3, "H": (3, 3, 5, 6, 8, 9, 10), "B": 11}
H_CHUNKS = ((13, 0, 1), (2, 3), (4, 5), (6, 7), (8, 9), (10, 11), (12,))


def plan_x(has_a, has_b, has_next):
    ev = []
    units = [(i, j) for i in range(4) for j in range(4)]
    at = 2
    if has_a:
        ev += [("K", 0, 0), ("K", 1, 0), ("Q", 0), ("K", 0, 1), ("K", 1, 1)]
    for c in range(CH):
        if has_a:
            if c == 1:
                ev += [("K", 0, 2), ("K", 1, 2)] + unit_events(0, 0, 0)
            if c == 2:
                ev += [("K", 0, 3), ("K", 1, 3)] + unit_events(0, 1, 0)
            for i, j in units[at:at + X_UNITS[c]]:
                ev += unit_events(i, j, 0)
            at += X_UNITS[c]
            if c == X_AT["P3"] and has_b:
                ev += [("P", 3)]
            if c == 12 and has_b:
                ev += [("T", 0, 0)]
        if has_b:
            if c + 2 < CH:
                ev += [("T", 1, c + 2)]
            ev += [("V", 1, c)]
            if c == X_AT["Y0"]:
                ev += [("Y", 0)]
            if has_a:
                ev += [("N", g) for g in (0, 1) if c == X_AT[f"N{g}"]]
            if has_next:
                ev += [("S", g) for g in (4, 0, 1) if c == X_AT[f"S{g}"]]
    if has_b:
        ev += [("O", 1)]
    if has_a:
        ev += [("C",)]
    return ev


def plan_y(has_prev, has_next):
    ev = [("T", 0, 1)] if has_prev else []
    units = [(i, j) for i in range(4, 8) for j in range(4)]
    at = 3
    for i, j in units[:at]:
        ev += unit_events(i, j, 4)
    if not has_prev:
        ev += [("P", 3), ("T", 0, 0), ("T", 0, 1), ("N", 0), ("N", 1)]
    for c in range(CH):
        for i, j in units[at:at + Y_UNITS[c]]:
            ev += unit_events(i, j, 4)
        at += Y_UNITS[c]
        ev += [("T", 0, c + 2)] if c + 2 < CH else [("T", 2, c - 11)]
        ev += [("V", 0, c)]
        ev += [("N", g) for g in (2, 3) if c == Y_AT[f"N{g}"]]
        if c == Y_AT["Y1"] and has_prev:
            ev += [("Y", 1)]
        if not has_prev:
            ev += {0: [("S", 4)], 1: [("S", 0), ("S", 1)]}.get(c, [])
        if has_next:
            ev += [("H", *chunks) for at_c, chunks in zip(Y_AT["H"], H_CHUNKS) if c == at_c]
            ev += [("S", g) for g in (2, 3) if c == Y_AT[f"S{g}"]]
            ev += [("B",)] if c == Y_AT["B"] else []
        if c == Y_AT["P7"]:
            ev += [("P", 7)]
    return ev + [("O", 0)]


def unit_events(i, j, first):
    ev = [("A", i, j)]
    if j == 0 and i < PAIRS - 1:
        ev += [("Q", i + 1)]
    if j == 1 and i > first:
        ev += [("P", i - 1)]
    if j == 3:
        ev += [("E", i)]
    return ev


def t_uses(ev):
    return [e for e in ev if e[0] in "YTQ"]


K_BANK = ((0, 1), (2, 3), (2, 3), (3, 3))
X_FIRST, X_MID, X_END = plan_x(True, False, True), plan_x(True, True, True), plan_x(False, True, False) + [("Y", 1)]
X_LAST = plan_x(True, True, False)
Y_FIRST, Y_MID, Y_LAST = plan_y(False, True), plan_y(True, True), plan_y(True, False)
USE0 = {e: n for n, e in enumerate(t_uses(X_FIRST + Y_FIRST))}
USE = {e: n for n, e in enumerate(t_uses(X_MID + Y_MID))}
NUSE0, NUSE = len(USE0), len(USE)
USE_END = {e: n for n, e in enumerate(t_uses(X_END))}
assert NUSE % 2 == 0


class Batch:

    def __init__(self, off, turn=None):
        self.off, self.turn = off, turn

    def lin(self, k, c):
        n = self.off * k + c
        return n if self.turn is None else self.turn * k + n

    def use(self, e):
        if self.turn is None and self.off == 0:
            return USE0[e]
        return self.lin(NUSE, NUSE0 - NUSE + (USE_END if self.off == B else USE)[e])

    def bank(self, e):
        if self.turn is None and self.off == 0:
            return USE0[e] % 2
        return (NUSE0 + (USE_END if self.off == B else USE)[e]) % 2

    def least(self, k, c):
        return self.off * k + c


def wait(eng, sem, batch, k, c):
    assert batch.turn is None or batch.least(k, c) > 0
    if batch.least(k, c) > 0:
        eng.wait_ge(sem, batch.lin(k, c))


def apart(ins, sem):
    return ins.wait_op(sem, 1, "sem-ge")


def periods(eng, step):
    step(Batch(0), X_FIRST, Y_FIRST)
    step(Batch(1), X_MID, Y_MID)
    with eng.Fori(0, B - 3) as turn:
        step(Batch(2, turn), X_MID, Y_MID)
    step(Batch(B - 1), X_LAST, Y_LAST)
    step(Batch(B), X_END, [])


def value_bank(h, c):
    slot = (c + h) % 3
    mine = 13 * h + c
    for m in range(mine - 1, mine - 14, -1):
        hh, cc = (m // 13) % 2, m % 13
        if (cc + hh) % 3 == slot:
            return slot, m + 1


def split_pair(pe, out, weights, moving, first, last):
    for n, (a, b) in enumerate(HL3):
        mm = pe.matmul(out, weights(a), moving(b), start=first and n == 0, stop=last and n == 2)
    return mm


class Link:

    def __init__(self, eng, sem, n, each, before):
        self.eng, self.sem, self.n, self.each, self.k = eng, sem, n, each, before

    def __call__(self, ins):
        self.k += 1
        ins.then_inc(self.sem, 1)
        self.eng.wait_ge(self.sem, self.n.lin(self.each, self.k))


class Context:

    def __init__(self, nc, ins, lat_scratch, q_scratch, W, ctx):
        def sb(name, shape, dt):
            return ctx.enter_context(nc.sbuf_tensor(name, shape, dt))

        def sem(name):
            return ctx.enter_context(nc.semaphore(name))

        self.W, self.rows, self.mask = W, ins["ctx"], ins["mask"]
        self.lat_scratch, self.q_scratch = lat_scratch, q_scratch
        self.raw = W["stage"]
        self.mask8 = sb("mask8", [P, N], U8)
        self.xn0 = sb("xn0", [P, D], F32)
        self.stats = sb("stats", [P, CH + 1, 6], F32)
        self.small = sb("small", [P, 7, CH + 1], F32)
        self.shift = sb("shift", [P, CH + 1], F32)
        self.rstd = sb("rstd", [P, CH + 1], F32)
        self.rows_in = [sem(f"rows_in{g}") for g in range(5)]
        self.q_in = sem("q_in")
        self.mask_in = sem("mask_in")
        self.stat_done = sem("stat_done")
        self.rstd_done = sem("rstd_done")
        self.norm_done = sem("norm_done")
        self.pool_step = sem("pool_step")
        self.centre_step = sem("centre_step")
        self.keys_done = sem("keys_done")
        self.mask_done = sem("mask_done")
        self.qblk_high = sem("qblk_high")
        self.qblk_done = sem("qblk_done")
        self.t_full = sem("t_full")
        self.k_full = sem("k_full")
        self.score_out = sem("score_out")
        self.val_done = sem("val_done")

    def load_rows(self, sp, n, index, g):
        if g > 0:
            wait(sp, self.val_done, n, 4, g - 3)
        if g < 3:
            sp.dma_start(self.raw[:, 4 * g:4 * g + 4, :].rearrange("p c d -> p (c d)"),
                         self.rows[index, 0:TAIL, :].rearrange("(p c) d -> p (c d)", c=CPP)[:, 4 * g * D:(4 * g + 4) * D]
                         ).then_inc(self.rows_in[g], 16)
        else:
            sp.dma_start(self.raw[L:P, 12, :], self.rows[index, TAIL:LAST, :]).then_inc(self.rows_in[3], 16)
            sp.dma_start(self.raw[0:L, 12, :], self.lat_scratch[index]).then_inc(self.rows_in[3], 16)

    def load_centre(self, sp, n, index):
        wait(sp, self.keys_done, n, 4, 0)
        wait(sp, self.k_full, n, 8, 0)
        sp.dma_start(self.raw[:, 13, :], self.rows[index, LAST, :].partition_broadcast(P)).then_inc(self.rows_in[4], 16)

    def moments(self, dve, n, g):
        wait(dve, self.rows_in[g], n, 32 if g == 3 else 16, 32 if g == 3 else 16)
        for c in range(*GROUPS[g]) if g < 4 else [13]:
            dve.bn_stats(self.stats[:, STAT[c], :], self.raw[:, c, :]).then_inc(self.stat_done, 1)

    def q_block_low(self, dve, n, queries):
        W = self.W
        for h in range(2):
            s = slice(h * L, h * L + L)
            wait(dve, self.qblk_high, n, 2, h + 1)
            dve.tensor_tensor(W["qblk"][s, :, 1, s], queries[s, :, :], W["qblk"][s, :, 0, s].bitcast(F32), ALU.subtract
                              ).then_inc(self.qblk_done, 1)

    def normalise(self, act, n, *chunks):
        wait(act, self.rstd_done, n, 2, 1 if chunks[-1] < 8 else 2)
        for c in chunks:
            s = slice(L, P) if c == 12 else slice(0, P)
            m = STAT[c]
            act.activation(self.raw[s, c, :], self.raw[s, c, :], ACT.Identity, bias=self.shift[s, m:m + 1],
                           scale=self.rstd[s, m:m + 1]).then_inc(self.norm_done, 1)

    def q_block_high(self, act, n, queries):
        for h in range(2):
            s = slice(h * L, h * L + L)
            act.activation(self.W["qblk"][s, :, 0, s], queries[s, :, :], ACT.Copy).then_inc(self.qblk_high, 1)

    def mask_bias(self, pool, n):
        bias, mask8 = self.W["bias"], self.mask8
        wait(pool, self.mask_in, n, 16, 16)
        wait(pool, self.score_out, n, 32, 0)
        apart(pool.tensor_scalar(bias[:, 0:TAIL], mask8[:, 0:TAIL], -NEG, NEG, ALU.mult, ALU.add), self.mask_in
              ).then_inc(self.mask_done, 1)
        pool.tensor_scalar(bias[:, TAIL + L:KEYS + 1], mask8[:, TAIL:N], -NEG, NEG, ALU.mult, ALU.add
                           ).then_inc(self.mask_done, 1)

    def deviations(self, pool, n, part):
        cols = (slice(0, 9), slice(9, CH + 1))[part]
        me, m2e, mo, m2o = (self.stats[:, cols, q] for q in (1, 2, 4, 5))
        total, diff, both, sq, quarter, var, negmean = (self.small[:, q, cols] for q in range(7))
        link = Link(pool, self.pool_step, n, 18, 9 * part)
        wait(pool, self.stat_done, n, 14, (9, 14)[part])
        link(pool.tensor_tensor(total, me, mo, ALU.add))
        link(pool.tensor_tensor(diff, me, mo, ALU.subtract))
        link(pool.tensor_tensor(both, m2e, m2o, ALU.add))
        link(apart(pool.tensor_scalar(negmean, total, -0.5, 0.0, ALU.mult, ALU.add), self.stat_done))
        link(pool.tensor_tensor(sq, diff, diff, ALU.mult))
        link(apart(pool.tensor_scalar(quarter, sq, 0.25, EPS, ALU.mult, ALU.add), self.stat_done))
        link(apart(pool.tensor_scalar(sq, both, 1.0 / D, 0.0, ALU.mult, ALU.add), self.stat_done))
        link(pool.tensor_tensor(var, sq, quarter, ALU.add))
        wait(pool, self.norm_done, n, 14, 0)
        link(pool.tensor_tensor(self.rstd[:, cols], var, self.W["neghalf"][:, cols], ALU.pow))
        pool.tensor_tensor(self.shift[:, cols], self.rstd[:, cols], negmean, ALU.mult).then_inc(self.rstd_done, 1)

    def centre_key(self, eng, n):
        link = Link(eng, self.centre_step, n, 7, 0)
        wait(eng, self.norm_done, n, 14, 1)
        wait(eng, self.k_full, n, 8, 0)
        link(eng.tensor_tensor(self.xn0[:, :], self.raw[:, 13, :], self.W["g1"][:, :], ALU.mult))
        link(eng.tensor_tensor(self.xn0[:, :], self.xn0[:, :], self.W["b1"][:, :], ALU.add))

    def centre(self, eng, n, g):
        raw, g1 = self.raw, self.W["g1"]
        link = Link(eng, self.centre_step, n, 7, 2 + g)
        if g < 3:
            wait(eng, self.norm_done, n, 14, 4 * g + 5)
            rows = raw[:, 4 * g:4 * g + 4, :]
            link(eng.tensor_tensor(rows, rows, raw[:, 13:14, :].to_broadcast([P, 4, D]), ALU.subtract))
            eng.tensor_tensor(rows, rows, g1[:, :].unsqueeze(1).to_broadcast([P, 4, D]), ALU.mult
                              ).then_inc(self.keys_done, 1)
            return
        wait(eng, self.norm_done, n, 14, 14)
        wait(eng, self.keys_done, n, 4, 3)
        link(eng.tensor_tensor(raw[L:P, 12, :], raw[L:P, 12, :], raw[L:P, 13, :], ALU.subtract))
        link(eng.tensor_tensor(raw[L:P, 12, :], raw[L:P, 12, :], g1[L:P, :], ALU.mult))
        eng.tensor_tensor(raw[0:L, 12, :], raw[0:L, 12, :], self.xn0[0:L, :], ALU.subtract).then_inc(self.keys_done, 1)
        wait(eng, self.keys_done, n, 4, 4)

    def prepare(self, pool, n):
        self.deviations(pool, n, 0)
        self.centre_key(pool, n)
        self.centre(pool, n, 0)
        self.deviations(pool, n, 1)
        for g in range(1, 4):
            self.centre(pool, n, g)


def block_0(nc, ins, F, W, ctx):
    def sb(name, shape, dt):
        return ctx.enter_context(nc.sbuf_tensor(name, shape, dt))

    def sem(name):
        return ctx.enter_context(nc.semaphore(name))

    x = sb("x0_rows", [P, RT, D], F32)
    lat = sb("lat", [P, RT, D], F32)
    latT = sb("latT", [P, KD, 2, ROWS], F32R)
    wraw = sb("wraw", [P, 3, 2 * INNER], F32)
    wq = sb("wq", [P, KD, 2, INNER], F32R)
    qstage = sb("qstage", [P, B, PAIRS, L], F32)
    g2 = sb("g2", [P, D], F32)
    b2 = sb("b2", [P, D], F32)
    stats = sb("stats0", [P, RT, 6], F32)
    mv = sb("mv", [P, RT, 2], F32)
    veps = sb("veps", [P, RT], F32)
    rstd1 = sb("rstd_first", [P, RT], F32)
    var2 = sb("var_second", [P, RT], F32)
    rstd2 = sb("rstd_second", [P, RT], F32)
    rboth = sb("rstd_both", [P, RT], F32)
    bank = [ctx.enter_context(nc.psum_tensor(f"bank0_{n}", [P, 512], F32)) for n in range(4)]

    x_in = sem("x_in0")
    w_in = [sem(f"w_in{n}") for n in range(3)]
    g2_in = sem("g2_in")
    g1_in = sem("g1_in")
    ident_done = sem("ident_done")
    zero_done = sem("zero_done")
    stat0 = sem("stat0")
    mv_done = sem("mv_done")
    rboth_done = sem("rboth_done")
    pool0 = sem("pool0")
    scaled = sem("scaled")
    lat_done = sem("lat_done")
    bank_full = sem("bank_full")
    high_done = sem("high_done")
    low_done = sem("low_done")
    q_done = sem("q_done")
    wh_done = sem("wh_done")
    wql_done = sem("wql_done")
    wl_done = sem("wl_done")
    lat_out, q_out = sem("lat_out"), sem("q_out")
    splits = [(wraw[:, 0, :].rearrange("p (k n) -> p k n", k=KD), wq[:, :, :, :]),
              (wraw[:, 1, :].rearrange("p (k n) -> p k n", k=PAIRS), W["wk"][:, :, :, :]),
              (wraw[:, 2, :].rearrange("p (k n) -> p k n", k=KD), W["wv"][:, :, :, :])]
    first = Batch(0)

    block = ctx.enter_context(nc.Block())

    @block.sync
    def _(sp):
        sp.dma_start(x[:, :, :], ins["x"].rearrange("(t p) d -> p t d", p=P)).then_inc(x_in, 16)
        sp.dma_start(g2[:, :], ins["g2"].partition_broadcast(P)).then_inc(g2_in, 16)
        sp.dma_start(b2[:, :], ins["b2x"].partition_broadcast(P)).then_inc(g2_in, 16)
        sp.dma_start(wraw[:, 0, :].rearrange("p (k n) -> p k n", k=KD), ins["wq"].rearrange("(k p) n -> p k n", p=P)
                     ).then_inc(w_in[0], 16)
        F.load_centre(sp, first, 0)
        for g in range(3):
            F.load_rows(sp, first, 0, g)
        sp.dma_start(W["g1"][:, :], ins["g1"].partition_broadcast(P)).then_inc(g1_in, 16)
        sp.dma_start(W["b1"][:, :], ins["b1x"].partition_broadcast(P)).then_inc(g1_in, 16)
        sp.dma_start(F.mask8[:, :], F.mask[0, :].partition_broadcast(P)).then_inc(F.mask_in, 16)
        sp.dma_start(wraw[:, 1, :].rearrange("p (k n) -> p k n", k=PAIRS), ins["wkT"].rearrange("(k p) n -> p k n", p=P)
                     ).then_inc(w_in[1], 16)
        sp.wait_ge(lat_done, RT)
        sp.dma_start(F.lat_scratch.rearrange("(t b) l d -> (b l) t d", b=2), lat[:, :, :]).then_inc(lat_out, 16)
        sp.wait_ge(lat_out, 16)
        F.load_rows(sp, first, 0, 3)
        sp.dma_start(wraw[:, 2, :].rearrange("p (k n) -> p k n", k=KD), ins["wv"].rearrange("(k p) n -> p k n", p=P)
                     ).then_inc(w_in[2], 16)
        for t in range(4):
            sp.wait_ge(q_done, 4 * t + 4)
            sp.dma_start(F.q_scratch[4 * t:4 * t + 4].rearrange("b p a l -> p b (a l)"),
                         qstage[:, 4 * t:4 * t + 4, :, :].rearrange("p b a l -> p b (a l)")).then_inc(q_out, 16)
        sp.wait_ge(q_out, 16 * 4)

    @block.gpsimd
    def _(pool):
        chain = [0]

        def link(ins):
            chain[0] += 1
            ins.then_inc(pool0, 1)
            pool.wait_ge(pool0, chain[0])

        link(pool.memset(W["ident"][:, :], 0.0))
        pool.affine_select(out=W["ident"][:, :], in_=W["ident"][:, :], compare_op=ALU.not_equal, fill=1.0, base=0,
                           pattern=[[-1, P]], channel_multiplier=1).then_inc(ident_done, 1)
        link(pool.memset(W["neghalf"][:, :], -0.5))
        pool.memset(W["qblk"][:, :, :, :].bitcast(F32), 0.0).then_inc(zero_done, 1)
        pool.wait_ge(mv_done, RT)
        link(pool.tensor_scalar(veps[:, :], mv[:, :, 1], 1.0, EPS, ALU.mult, ALU.add))
        link(pool.tensor_tensor(rstd1[:, :], veps[:, :], W["neghalf"][:, 0:RT], ALU.pow))
        link(pool.tensor_tensor(var2[:, :], rstd1[:, :], rstd1[:, :], ALU.mult))
        link(pool.tensor_tensor(var2[:, :], var2[:, :], mv[:, :, 1], ALU.mult))
        link(pool.tensor_scalar(var2[:, :], var2[:, :], 1.0, EPS, ALU.mult, ALU.add))
        link(pool.tensor_tensor(rstd2[:, :], var2[:, :], W["neghalf"][:, 0:RT], ALU.pow))
        pool.tensor_tensor(rboth[:, :], rstd1[:, :], rstd2[:, :], ALU.mult).then_inc(rboth_done, 1)
        pool.wait_ge(wh_done, 1)
        for k in range(KD):
            pool.tensor_tensor(wq[:, k, 1, :], splits[0][0][:, k, :], wq[:, k, 0, :].bitcast(F32), ALU.subtract
                               ).then_inc(wql_done, 1)
        link(pool.memset(W["bias"][:, :], 0.0))
        F.mask_bias(pool, first)
        for part in range(2):
            F.deviations(pool, first, part)

    @block.vector
    def _(dve):
        dve.wait_ge(x_in, 16)
        for t in range(RT):
            dve.bn_stats(stats[:, t, :], x[:, t, :]).then_inc(stat0, 1)
        for t in range(RT):
            dve.wait_ge(stat0, t + 1)
            dve.bn_aggr(mv[:, t, :], stats[:, t, :]).then_inc(mv_done, 1)
        dve.wait_ge(g2_in, 32)
        for t in range(RT):
            dve.wait_ge(mv_done, t + 1)
            dve.scalar_tensor_tensor(out=lat[:, t, :], in0=x[:, t, :], scalar=mv[:, t, 0:1], in1=g2[:, :],
                                     op0=ALU.subtract, op1=ALU.mult).then_inc(scaled, 1)
        dve.wait_ge(rboth_done, 1)
        for t in range(RT):
            dve.wait_ge(scaled, t + 1)
            dve.scalar_tensor_tensor(out=lat[:, t, :], in0=lat[:, t, :], scalar=rboth[:, t:t + 1], in1=b2[:, :],
                                     op0=ALU.mult, op1=ALU.add).then_inc(lat_done, 1)
        for n in range(4):
            dve.wait_ge(high_done, n + 1)
            k, half = n % 2, n // 2
            s = slice(half * 512, half * 512 + 512)
            dve.tensor_tensor(latT[:, k, 1, s], bank[n][:, :], latT[:, k, 0, s].bitcast(F32), ALU.subtract
                              ).then_inc(low_done, 1)
        for g in (4, 0, 1, 2, 3):
            F.moments(dve, first, g)
        F.q_block_low(dve, first, qstage[:, 0, :, :])
        dve.wait_ge(g1_in, 32)
        F.centre_key(dve, first)
        for g in range(4):
            F.centre(dve, first, g)
            if g in (0, 3):
                n = 1 + g // 3
                src, to = splits[n]
                dve.wait_ge(wh_done, n + 1)
                dve.tensor_tensor(to[:, :, 1, :], src, to[:, :, 0, :].bitcast(F32), ALU.subtract).then_inc(wl_done, 1)

    @block.scalar
    def _(act):
        act.wait_ge(w_in[0], 16)
        act.activation(splits[0][1][:, :, 0, :], splits[0][0], ACT.Copy).then_inc(wh_done, 1)
        for n in range(4):
            act.wait_ge(bank_full, n + 1)
            k, half = n % 2, n // 2
            act.activation(latT[:, k, 0, half * 512:half * 512 + 512], bank[n][:, :], ACT.Copy).then_inc(high_done, 1)
        between = {5: (13, 0, 1), 6: (2, 3), 7: (4, 5), 8: (6, 7), 9: (8, 9), 10: (10, 11), 11: (12,)}
        for n in range(16):
            t, a = n // 4, 2 * (n % 4)
            act.wait_ge(bank_full, 5 + n)
            act.activation(qstage[:, 4 * t:4 * t + 4, a:a + 2, :].rearrange("p b a l -> p a b l"),
                           bank[n % 4][:, :].rearrange("p (a b l) -> p a b l", a=2, l=L),
                           ACT.Copy, scale=DX ** -0.5).then_inc(q_done, 1)
            if n == 3:
                act.wait_ge(q_done, 4)
                act.wait_ge(zero_done, 1)
                F.q_block_high(act, first, qstage[:, 0, :, :])
            if n in between:
                F.normalise(act, first, *between[n])
            if n in (4, 15):
                m = 1 if n == 4 else 2
                act.wait_ge(w_in[m], 16)
                act.activation(splits[m][1][:, :, 0, :], splits[m][0], ACT.Copy).then_inc(wh_done, 1)

    @block.tensor
    def _(pe):
        pe.wait_ge(ident_done, 1)
        for n in range(4):
            k, half = n % 2, n // 2
            pe.wait_ge(lat_done, 4 * half + 4)
            for t in range(4):
                mm = pe.transpose(bank[n][:, t * P:(t + 1) * P], lat[:, 4 * half + t, k * P:(k + 1) * P], W["ident"][:, :])
            mm.then_inc(bank_full, 1)
        pe.wait_ge(wql_done, KD)
        for n in range(16):
            t = n // 4
            pe.wait_ge(low_done, 2 + 2 * (t // 2))
            if n >= 4:
                pe.wait_ge(q_done, n - 3)
            else:
                pe.wait_ge(low_done, n + 1)
            for half in range(2):
                pair = 2 * (n % 4) + half
                for k in range(KD):
                    mm = split_pair(pe, bank[n % 4][:, half * 256:(half + 1) * 256],
                                    lambda q: wq[:, k, q, pair * P:(pair + 1) * P],
                                    lambda q: latT[:, k, q, t * 256:(t + 1) * 256], k == 0, k == KD - 1)
            mm.then_inc(bank_full, 1)


STAGED = (("wout", 0, PAIRS, D), ("wqk", PAIRS * D, KD, 2 * D), ("wvs", (PAIRS + 2 * KD) * D, KD, D))


def staged(stage, at, k, width):
    return stage[:, :, :].rearrange("p c d -> p (c d)")[:, at:at + k * width].rearrange("p (k n) -> p k n", k=k)


def block_1(nc, ins, F, y_scratch, shared, ctx):
    W = shared

    def sb(name, shape, dt):
        return ctx.enter_context(nc.sbuf_tensor(name, shape, dt))

    def ps(name):
        return ctx.enter_context(nc.psum_tensor(name, [P, 512], F32))

    def sem(name):
        return ctx.enter_context(nc.semaphore(name))

    raw, xn0, q_in, mask_in, val_done, score_out = F.raw, F.xn0, F.q_in, F.mask_in, F.val_done, F.score_out
    keys_done, mask_done, qblk_done, t_full, k_full = F.keys_done, F.mask_done, F.qblk_done, F.t_full, F.k_full
    keyT = sb("keyT", [P, KD, 2, KEYS], F32R)
    val = sb("val", [P, CH, 2, D], F32R)
    prob = sb("prob", [P, PAIRS, KEYS + 1], F32)
    probT = sb("probT", [P, 3, 2, 512], F32R)
    qkT = sb("qkT", [P, 2, KD, 2, P], F32R)
    outT = sb("outT", [P, KD, 2, 512], F32R)
    ystage, y_out = W["ystage"], W["y_out"]
    q32 = sb("q32", [P, PAIRS, L], F32)
    x0next = sb("x0next", [P, KD], F32)
    x0T = sb("x0T", [P, KD], F32)
    maxes = sb("maxes", [P, PAIRS, 5], F32)
    negmax = sb("negmax", [P, PAIRS], F32)
    psum_ = sb("psums", [P, PAIRS], F32)
    rsum = sb("rsum", [P, PAIRS], F32)

    s_bank = [ps(f"s_bank{n}") for n in range(4)]
    t_bank = [ps(f"t_bank{n}") for n in range(2)]
    o_bank = [ps(f"o_bank{n}") for n in range(2)]

    t_high = sem("t_high")
    t_done = sem("t_done")
    k_high, k_done = sem("k_high"), sem("k_done1")
    x0_next = sem("x0_next")
    x0_done = sem("x0_done")
    val_high = sem("val_high")
    score_full = sem("score_full")
    max_done = sem("max_done")
    exp_done = sem("exp_done")
    rsum_done = sem("rsum_done")
    prob_done = sem("prob_done")
    pv_done = sem("pv_done")
    out_high = sem("out_high")
    out_done = sem("out_done")

    block = ctx.enter_context(nc.Block())

    @block.sync
    def _(sp):
        def load_q_mask(n, index):
            wait(sp, mask_done, n, 2, 0)
            wait(sp, qblk_done, n, 2, 0)
            sp.dma_start(q32[:, :, :], F.q_scratch[index]).then_inc(q_in, 16)
            sp.dma_start(F.mask8[:, :], F.mask[index, :].partition_broadcast(P)).then_inc(mask_in, 16)

        def store_y(b, h, e, index):
            sp.wait_ge(t_done, b.use(e) + 1)
            sp.dma_start(y_scratch[index, :, 4 * h:4 * h + 4, :], ystage[:, h, :, :]).then_inc(y_out[h], 16)

        def step(b, x, y):
            nxt = Batch(b.off + 1, b.turn)
            if b.off == B:
                sp.wait_ge(val_done, 4 * B)
                for n, (name, at, k, width) in enumerate(STAGED):
                    sp.dma_start(staged(W["stage"], at, k, width), ins[name].rearrange("(k p) n -> p k n", p=P)
                                 ).then_inc(W["self_in"][n], 16)
            if ("B",) in y:
                F.load_centre(sp, nxt, nxt.lin(1, 0))
                wait(sp, val_done, nxt, 4, -3)
            if ("Y", 0) in x:
                store_y(b, 0, ("Y", 0), b.lin(1, -1))
            if ("B",) in y:
                for g in range(4):
                    F.load_rows(sp, nxt, nxt.lin(1, 0), g)
            if ("Y", 1) in x + y:
                store_y(b, 1, ("Y", 1), b.lin(1, -1))
            if ("B",) in y:
                load_q_mask(nxt, nxt.lin(1, 0))
        periods(sp, step)

    @block.gpsimd
    def _(pool):
        def step(b, x, y):
            if ("Q", 0) in x and b.off > 0:
                F.mask_bias(pool, b)
            if ("B",) in y:
                F.prepare(pool, Batch(b.off + 1, b.turn))
        periods(pool, step)

    @block.scalar
    def _(act):
        def half(b, events):
            for e in events:
                kind = e[0]
                if kind in "YTQ":
                    act.wait_ge(t_full, b.use(e) + 1)
                    bank = t_bank[b.bank(e)]
                if kind == "Y":
                    wait(act, y_out[e[1]], b, 16, -16)
                    act.activation(ystage[0:L, e[1], :, :],
                                   bank[0:L, :].rearrange("p (a x) -> p a x", a=4)[:, :, 0:L], ACT.Copy).then_inc(t_high, 1)
                if kind == "T":
                    when, c = e[1:]
                    slot, need = value_bank(min(when, 1), c)
                    wait(act, pv_done, b, 26, need - (26 if when == 1 else 0))
                    act.activation(probT[:, slot, 0, :], bank[:, :], ACT.Copy).then_inc(t_high, 1)
                if kind == "Q":
                    wait(act, score_out, b, 32, 4 * e[1] - 4)
                    act.activation(qkT[:, e[1] % 2, :, 0, :], bank[:, 0:KD * P].rearrange("p (k x) -> p k x", k=KD),
                                   ACT.Copy).then_inc(t_high, 1)
                if kind == "K":
                    k, g = e[1:]
                    a, z = GROUPS[g]
                    bank, at = s_bank[K_BANK[g][k]], 2 * P * k if g == 3 else 0
                    wait(act, k_full, b, 8, 8 if g == 3 else 2 * g + k + 1)
                    wait(act, score_out, b, 32, 0)
                    if g == 3:
                        wait(act, x0_done, b, 1, 0)
                        act.activation(x0next[:, k:k + 1], bank[:, at + P:at + P + 1], ACT.Copy).then_inc(x0_next, 1)
                    act.activation(keyT[:, k, 0, a * P:z * P], bank[:, at:at + (z - a) * P], ACT.Copy).then_inc(k_high, 1)
                if kind == "E":
                    i = e[1]
                    wait(act, max_done, b, 8, i + 1)
                    act.activation(prob[:, i, :], prob[:, i, :], ACT.Exp, bias=negmax[:, i:i + 1],
                                   accum_out=psum_[:, i:i + 1]).then_inc(exp_done, 1)
                if kind == "O":
                    h = e[1]
                    wait(act, pv_done, b, 26, 13 * (h + 1) - 26 * h)
                    wait(act, x0_done, b, 1, 1 - h)
                    for k in range(KD):
                        act.activation(outT[:, k, 0, :], o_bank[k][:, :], ACT.Identity, bias=x0T[:, k:k + 1]).then_inc(out_high, 1)
                if kind == "N":
                    g = e[1]
                    a, z = GROUPS[g]
                    wait(act, keys_done, b, 4, g + 1)
                    wait(act, pv_done, b, 26, z - 13)
                    act.activation(val[:, a:z, 0, :], raw[:, a:z, :], ACT.Copy).then_inc(val_high, 1)
                if kind == "H":
                    F.normalise(act, Batch(b.off + 1, b.turn), *e[1:])
                if kind == "B":
                    wait(act, q_in, b, 16, 16)
                    act.wait_ge(t_full, b.use(("Q", 7)) + 1)
                    F.q_block_high(act, Batch(b.off + 1, b.turn), q32)

        periods(act, lambda b, x, y: (half(b, x), half(b, y)))

    @block.vector
    def _(dve):
        def half(b, events):
            for e in events:
                kind = e[0]
                if kind in "YTQ":
                    dve.wait_ge(t_high, b.use(e) + 1)
                    bank = t_bank[b.bank(e)]
                if kind == "Y":
                    wait(dve, y_out[e[1]], b, 16, -16)
                    dve.tensor_copy(ystage[L:P, e[1], :, :],
                                    bank[L:P, :].rearrange("p (a x) -> p a x", a=4)[:, :, L:P]).then_inc(t_done, 1)
                if kind == "T":
                    slot, _ = value_bank(min(e[1], 1), e[2])
                    dve.tensor_tensor(probT[:, slot, 1, :], bank[:, :], probT[:, slot, 0, :].bitcast(F32),
                                      ALU.subtract).then_inc(t_done, 1)
                if kind == "Q":
                    dve.tensor_tensor(qkT[:, e[1] % 2, :, 1, :], bank[:, 0:KD * P].rearrange("p (k x) -> p k x", k=KD),
                                      qkT[:, e[1] % 2, :, 0, :].bitcast(F32), ALU.subtract).then_inc(t_done, 1)
                if kind == "K":
                    k, g = e[1:]
                    a, z = GROUPS[g]
                    bank, at = s_bank[K_BANK[g][k]], 2 * P * k if g == 3 else 0
                    wait(dve, k_high, b, 8, 8 if g == 3 else 2 * g + k + 1)
                    dve.tensor_tensor(keyT[:, k, 1, a * P:z * P], bank[:, at:at + (z - a) * P],
                                      keyT[:, k, 0, a * P:z * P].bitcast(F32), ALU.subtract).then_inc(k_done, 1)
                if kind == "A":
                    i, j = e[1:]
                    if (i, j) == (0, 0):
                        wait(dve, mask_done, b, 2, 2)
                        dve.tensor_copy(maxes[:, :, 4:5], W["bias"][:, KEYS:KEYS + 1].unsqueeze(1).to_broadcast([P, PAIRS, 1]))
                    if j == 0:
                        dve.tensor_copy(prob[:, i, KEYS:KEYS + 1], W["bias"][:, KEYS:KEYS + 1])
                    wait(dve, score_full, b, 32, 4 * i + j + 1)
                    s = slice(j * QTR, (j + 1) * QTR)
                    apart(dve.tensor_tensor_reduce(out=prob[:, i, s], in0=s_bank[j][:, 0:QTR], in1=W["bias"][:, s],
                                                   scale=1.0, scalar=NEG, op0=ALU.add, op1=ALU.max,
                                                   accum_out=maxes[:, i, j:j + 1]), mask_done).then_inc(score_out, 1)
                    if j == 3:
                        wait(dve, score_out, b, 32, 4 * i + 4)
                        dve.tensor_reduce(negmax[:, i:i + 1], maxes[:, i, :], AX.X, ALU.max, negate=True
                                          ).then_inc(max_done, 1)
                if kind == "P":
                    i = e[1]
                    wait(dve, exp_done, b, 8, i + 1)
                    dve.reciprocal(rsum[:, i:i + 1], psum_[:, i:i + 1]).then_inc(rsum_done, 1)
                    wait(dve, rsum_done, b, 8, i + 1)
                    dve.tensor_scalar(prob[:, i, :], prob[:, i, :], rsum[:, i:i + 1], None, ALU.mult).then_inc(prob_done, 1)
                if kind == "O":
                    h = e[1]
                    for k in range(KD):
                        wait(dve, out_high, b, 4, 2 * h + k + 1 - 4 * h)
                        dve.scalar_tensor_tensor(out=outT[:, k, 1, :], in0=o_bank[k][:, :], scalar=x0T[:, k:k + 1],
                                                 in1=outT[:, k, 0, :].bitcast(F32), op0=ALU.add, op1=ALU.subtract
                                                 ).then_inc(out_done, 1)
                if kind == "C":
                    wait(dve, x0_next, b, 2, 2)
                    wait(dve, out_done, b, 4, 0)
                    dve.tensor_copy(x0T[:, :], x0next[:, :]).then_inc(x0_done, 1)
                if kind == "N":
                    g = e[1]
                    a, z = GROUPS[g]
                    wait(dve, val_high, b, 4, g + 1)
                    dve.tensor_tensor(val[:, a:z, 1, :], raw[:, a:z, :], val[:, a:z, 0, :].bitcast(F32), ALU.subtract
                                      ).then_inc(val_done, 1)
                n = Batch(b.off + 1, b.turn)
                if kind == "S":
                    F.moments(dve, n, e[1])
                if kind == "B":
                    F.q_block_low(dve, n, q32)

        periods(dve, lambda b, x, y: (half(b, x), half(b, y)))

    @block.tensor
    def _(pe):
        ident = W["ident"]

        def half(b, events):
            for e in events:
                kind = e[0]
                if kind in "YTQ":
                    bank = t_bank[b.bank(e)]
                    if b.turn is not None or b.off > 0 or b.use(e) >= 2:
                        pe.wait_ge(t_done, b.use(e) - 1)
                if kind == "Y":
                    h = e[1]
                    wait(pe, out_done, b, 4, 2 * h - 2)
                    for a in range(4):
                        pair = 4 * h + a
                        for k in range(KD):
                            mm = split_pair(pe, bank[:, a * P:(a + 1) * P],
                                            lambda q: W["wv"][:, k, q, pair * P:(pair + 1) * P],
                                            lambda q: outT[:, k, q, a * P:(a + 1) * P], k == 0, k == KD - 1)
                    mm.then_inc(t_full, 1)
                if kind == "T":
                    when, c = e[1:]
                    h = min(when, 1)
                    if c == 0:
                        wait(pe, prob_done, b, 8, 4 * h + 4)
                    for t in range(4):
                        mm = pe.transpose(bank[:, t * P:(t + 1) * P], prob[:, 4 * h + t, c * P:(c + 1) * P], ident[:, :])
                    mm.then_inc(t_full, 1)
                if kind == "Q":
                    i = e[1]
                    if i == 0:
                        wait(pe, qblk_done, b, 2, 2)
                    for k in range(KD):
                        mm = split_pair(pe, bank[:, k * P:(k + 1) * P],
                                        lambda q: W["wk"][:, i, q, k * P:(k + 1) * P],
                                        lambda q: W["qblk"][:, i, q, :], True, True)
                    mm.then_inc(t_full, 1)
                if kind == "K":
                    k, g = e[1:]
                    a, z = GROUPS[g]
                    bank, at = s_bank[K_BANK[g][k]], 2 * P * k if g == 3 else 0
                    wait(pe, keys_done, b, 4, g + 1)
                    if (g, k) == (0, 0):
                        wait(pe, score_out, b, 32, 0)
                    if g >= 2:
                        wait(pe, k_done, b, 8, 3 + k if g == 2 else 6)
                    for c in range(a, z):
                        mm = pe.transpose(bank[:, at + (c - a) * P:at + (c - a + 1) * P], raw[:, c, k * P:(k + 1) * P],
                                          ident[:, :])
                    if g == 3:
                        mm = pe.transpose(bank[:, at + P:at + 2 * P], xn0[:, k * P:(k + 1) * P], ident[:, :])
                    if (g, k) == (3, 1):
                        mm.then_inc(k_full, 2)
                    elif g < 3:
                        mm.then_inc(k_full, 1)
                if kind == "A":
                    i, j = e[1:]
                    if j == 0:
                        pe.wait_ge(t_done, b.use(("Q", i)) + 1)
                    if i == 0:
                        wait(pe, k_done, b, 8, 2 * j + 2)
                    wait(pe, score_out, b, 32, 4 * i + j - 3)
                    for k in range(KD):
                        mm = split_pair(pe, s_bank[j][:, 0:QTR], lambda q: qkT[:, i % 2, k, q, :],
                                        lambda q: keyT[:, k, q, j * QTR:(j + 1) * QTR], k == 0, k == KD - 1)
                    mm.then_inc(score_full, 1)
                if kind == "V":
                    h, c = e[1:]
                    slot, _ = value_bank(h, c)
                    if h == 1 and c < 2:
                        pe.wait_ge(t_done, Batch(b.off - 1, b.turn).use(("T", 2, c)) + 1)
                    else:
                        pe.wait_ge(t_done, b.use(("T", h, c)) + 1)
                    if h == 0 and c % 4 == 0:
                        wait(pe, val_done, b, 4, c // 4 + 1)
                    for k in range(KD):
                        if c == 0:
                            wait(pe, out_done, b, 4, k - 1 - 2 * h)
                        mm = split_pair(pe, o_bank[k][:, :], lambda q: val[:, c, q, k * P:(k + 1) * P],
                                        lambda q: probT[:, slot, q, :], c == 0, c == CH - 1)
                    mm.then_inc(pv_done, 1)
        periods(pe, lambda b, x, y: (half(b, x), half(b, y)))


def constants(nc, ctx):
    return {"stage": ctx.enter_context(nc.sbuf_tensor("stage", [P, CH + 1, D], F32)),
            "ystage": ctx.enter_context(nc.sbuf_tensor("ystage", [P, 2, 4, L], F32)),
            "y_out": [ctx.enter_context(nc.semaphore(f"y_out{h}")) for h in range(2)],
            "self_in": [ctx.enter_context(nc.semaphore(f"self_in{n}")) for n in range(4)],
            "w1_in": ctx.enter_context(nc.semaphore("w1_in")),
            "ident": ctx.enter_context(nc.sbuf_tensor("ident", [P, P], F32)),
            "neghalf": ctx.enter_context(nc.sbuf_tensor("neghalf", [P, 16], F32))}


def shared(nc, ctx):
    def sb(name, shape, dt):
        return ctx.enter_context(nc.sbuf_tensor(name, shape, dt))

    return {
        "g1": sb("g1", [P, D], F32),
        "b1": sb("b1", [P, D], F32),
        "bias": sb("bias", [P, KEYS + 1], BF16),
        "qblk": sb("qblk", [P, PAIRS, 2, P], F32R),
        "wk": sb("wk", [P, PAIRS, 2, D], F32R),
        "wv": sb("wv", [P, KD, 2, INNER], F32R),
    }


def block_2(nc, ins, y_scratch, x2, xn2T, W, ctx):
    def sb(name, shape, dt):
        return ctx.enter_context(nc.sbuf_tensor(name, shape, dt))

    def sem(name):
        return ctx.enter_context(nc.semaphore(name))

    H, DH = 16, D // 16
    yraw = sb("yraw", [P, 2, 2, PAIRS, L], F32)
    ysplit = sb("ysplit", [P, 2, 2, PAIRS, 2, L], F32R)
    xin = sb("xin", [P, RT, D], F32)
    x1 = sb("x1", [P, RT, D], F32)
    xn = sb("xn", [P, 2, D], F32)
    xnT = sb("xnT", [P, 2, 2, KD, 2 * P], F32R)
    wout = sb("wout", [P, PAIRS, 2, D], F32R)
    wqk = sb("wqk", [P, KD, 2, 2 * D], F32R)
    wv = sb("wv_self", [P, KD, 2, D], F32R)
    wo = sb("wo_self", [P, KD, 2, D], F32R)
    wtmp = sb("wtmp", [P, KD, D], F32)
    bqk = sb("bqk", [P, 2 * D], F32)
    bv = sb("bv", [P, D], F32)
    bo = sb("bo", [P, D], F32)
    rot = sb("rot", [P, 2, 8], F32)
    causal = sb("causal", [P, L], F32)
    headmask = sb("headmask", [P, 8], F32)
    vmask = sb("vmask", [P, D], F32)
    qk = sb("qk", [P, 2, 2 * D], F32)
    rc = sb("rc", [P, 2, 2 * D], F32)
    rs = sb("rs", [P, 2, 2 * D], F32)
    rqk = sb("rqk", [P, 2, 2 * D], F32)
    vblk = sb("vblk", [P, 2, 2, D], F32)
    qT = sb("qT", [P, 2, 4, P], F32)
    kblk = sb("kblk", [P, 2, 2, 2, 8, L], F32)
    sc = sb("sc", [P, 2, H, L], F32)
    mx = sb("mx", [P, 2, H], F32)
    sm = sb("sm", [P, 2, H], F32)
    rsm = sb("rsm", [P, 2, H], F32)
    pt = sb("pt", [P, 2, PAIRS, P], F32)
    att = sb("att", [P, 2, D], F32)
    attT = sb("attT", [P, 2, KD, 2, P], F32R)
    xn2 = sb("xn2", [P, 2, D], F32)
    st = sb("st2", [P, 2, 2, 6], F32)
    mv = sb("mv2", [P, 2, 2, 2], F32)
    ve = sb("ve2", [P, 2, 2], F32)
    rstd = sb("rstd2", [P, 2, 2], F32)
    bank = [ctx.enter_context(nc.psum_tensor(f"bank2_{n}", [P, 512], F32)) for n in range(8)]

    w_in = W["self_in"]
    c_in = sem("c2_in")
    x_in = sem("x2_in")
    y_in = [sem(f"y2_in{n}") for n in range(2)]
    wh_done = sem("self_high")
    wol_done, wl_done = sem("wout_low"), sem("self_low")
    y0_low = sem("y0_low")
    k_first = sem("k_first")
    pool_mask = sem("pool_mask")
    names = ("y_high y_low x1_full x1_done a_stat a_rstd xn_done xnT_full xnT_high xnT_low qk_full v_full qk_biased v_masked "
             "rot_done v_done x1b_done r_full qT_done k_done s_full s_max s_exp sum_done p_full p_out pv_full att_done "
             "attT_full attT_high attT_low o_full x2_done d_stat d_rstd xn2_done xn2T_full xn2T_high xn2T_low").split()
    S = {n: sem(n) for n in names}
    own = {n: sem(f"own_{n}") for n in ("dve", "pool")}

    def stages(run):
        for s in range(-2, RT + 4):
            for name, lag in (("d3n", 4), ("a1", 0), ("d3", 4), ("c1", 2), ("d1", 3), ("b1", 1), ("c1m", 2),
                              ("a2n", 0), ("b1v", 1), ("a2", 0), ("d2", 3), ("c2", 2), ("b2", 1), ("c3", 2), ("a0", -2)):
                if 0 <= s - lag < RT:
                    run(name, s - lag)

    def twice(ap):
        return ap.rearrange("p (a l) -> p a l", l=L).unsqueeze(2).to_broadcast([P, 2 * KD, 2, L])

    def doubled(ap):
        return ap.rearrange("p k (b u l) -> p (k b) u l", b=2, u=2)

    def key_blocks(eng, z, t, j, done):
        eng.wait_ge(S["qT_done"], t + 1)
        if t >= 2:
            eng.wait_ge(S["s_full"], t - 1)
        for b in range(2):
            src = qT[:, z, 2 + j, b * L:b * L + L]
            eng.tensor_tensor(kblk[:, z, j, b, :, :], src.unsqueeze(1).to_broadcast([P, 8, L]),
                              headmask[:, :].unsqueeze(2).to_broadcast([P, 8, L]), ALU.mult).then_inc(done, 1)

    def y_low(eng, t):
        eng.wait_ge(S["y_high"], t + 1)
        eng.tensor_tensor(ysplit[:, t % 2, 1, :, :, :], yraw[:, t % 2, :, :, :].rearrange("p b a l -> p a b l"),
                          ysplit[:, t % 2, 0, :, :, :].bitcast(F32), ALU.subtract
                          ).then_inc(y0_low if t < 2 else S["y_low"], 1)

    def wait_y_low(eng, t):
        if t < 2:
            eng.wait_ge(y0_low, t + 1)
        else:
            eng.wait_ge(S["y_low"], t - 1)

    class Chain:

        def __init__(self, eng, sem_):
            self.eng, self.sem, self.n = eng, sem_, 0

        def __call__(self, ins):
            self.n += 1
            ins.then_inc(self.sem, 1)
            self.eng.wait_ge(self.sem, self.n)

    weights = [(staged(W["stage"], *where), to) for (_, *where), to in zip(STAGED, (wout, wqk, wv))] + [(wtmp, wo)]

    block = ctx.enter_context(nc.Block())

    @block.sync
    def _(sp):
        def load_y(rt):
            if rt == RT - 1:
                for h in range(2):
                    sp.wait_ge(W["y_out"][h], 16 * B)
            if rt >= 2:
                wait_y_low(sp, rt - 2)
            sp.dma_start(yraw[:, rt % 2, :, :, :].rearrange("p b a l -> p b (a l)"),
                         y_scratch[2 * rt:2 * rt + 2].rearrange("b p a l -> p b (a l)")).then_inc(y_in[rt % 2], 16)
        load_y(0)
        load_y(1)
        sp.dma_start(xin[:, :, :], ins["x"].rearrange("(t p) d -> p t d", p=P)).then_inc(x_in, 16)
        for to, name in ((bqk, "bqk"), (bv, "bv"), (bo, "bo")):
            sp.dma_start(to[:, :], ins[name].partition_broadcast(P)).then_inc(c_in, 16)
        sp.dma_start(rot[:, :, :], ins["rot"]).then_inc(c_in, 16)
        for to, name in ((causal, "causal"), (headmask, "headmask"), (vmask, "vmask")):
            sp.dma_start(to[:, :], ins[name]).then_inc(c_in, 16)
        sp.dma_start(wtmp[:, :, :], ins["wos"].rearrange("(k p) n -> p k n", p=P)).then_inc(w_in[3], 16)
        sp.wait_ge(wol_done, 1)
        sp.dma_start(staged(W["stage"], 0, KD, HID), ins["w1"][0].rearrange("(k p) n -> p k n", p=P)).then_inc(W["w1_in"], 16)
        for rt in range(2, RT):
            load_y(rt)

    @block.scalar
    def _(act):
        def high_weight(n):
            tmp, to = weights[n]
            act.wait_ge(w_in[n], 16)
            act.activation(to[:, :, 0, :], tmp[:, :, :], ACT.Copy).then_inc(wh_done, 1)

        high_weight(0)

        def run(name, t):
            z = t % 2
            if name == "a0":
                act.wait_ge(y_in[z], 16 * (t // 2 + 1))
                if t >= 2:
                    act.wait_ge(S["x1_full"], t - 1)
                act.activation(ysplit[:, z, 0, :, :, :], yraw[:, z, :, :, :].rearrange("p b a l -> p a b l"), ACT.Copy
                               ).then_inc(S["y_high"], 1)
                if t == 0:
                    high_weight(1)
                    high_weight(2)
            if name == "a2":
                act.wait_ge(S["xnT_full"], t + 1)
                if t >= 2:
                    act.wait_ge(S["v_full"], t - 1)
                act.activation(doubled(xnT[:, z, 0, :, :]), twice(bank[1][:, 0:D]), ACT.Copy
                               ).then_inc(S["xnT_high"], 1)
            if (name, t) == ("a2", 1):
                high_weight(3)
            if name == "b2":
                act.wait_ge(S["r_full"], t + 1)
                if t >= 2:
                    act.wait_ge(S["s_full"], t - 1)
                    act.wait_ge(S["k_done"], 2 * t - 2)
                    act.wait_ge(k_first, 2 * t - 2)
                act.activation(qT[:, z, :, :], bank[2][:, :].rearrange("p (k x) -> p k x", k=4), ACT.Copy
                               ).then_inc(S["qT_done"], 1)
            if name == "c1m":
                act.wait_ge(S["s_max"], t + 1)
                act.activation(sc[:, z, :, :], sc[:, z, :, :], ACT.Exp, scale=DH ** -0.5).then_inc(S["s_exp"], 1)
            if name == "c2":
                for r in range(2):
                    act.wait_ge(S["p_full"], 2 * t + r + 1)
                    if t >= 2:
                        act.wait_ge(S["pv_full"], t - 1)
                    act.activation(pt[:, z, 4 * r:4 * r + 4, :], bank[(6, 4)[r]][:, :].rearrange("p (a x) -> p a x", a=4),
                                   ACT.Copy).then_inc(S["p_out"], 1)
            if name == "d1":
                act.wait_ge(S["attT_full"], t + 1)
                if t >= 2:
                    act.wait_ge(S["o_full"], t - 1)
                act.activation(attT[:, z, :, 0, :], bank[7][:, 0:D].rearrange("p (k x) -> p k x", k=KD), ACT.Copy
                               ).then_inc(S["attT_high"], 1)
            if name == "d3":
                act.wait_ge(S["xn2T_full"], t + 1)
                act.activation(xn2T[:, :, 0, t * P:(t + 1) * P], bank[7][:, 0:D].rearrange("p (k x) -> p k x", k=KD),
                               ACT.Copy).then_inc(S["xn2T_high"], 1)
        stages(run)

    @block.gpsimd
    def _(pool):
        link = Chain(pool, own["pool"])

        def low_weight(n):
            tmp, to = weights[n]
            pool.wait_ge(wh_done, n + 1)
            pool.tensor_tensor(to[:, :, 1, :], tmp[:, :, :], to[:, :, 0, :].bitcast(F32), ALU.subtract).then_inc(wl_done, 1)

        low_weight(1)
        low_weight(2)

        def moments(chain, z, t, stat, done):
            pool.wait_ge(S[stat], t + 1)
            link(pool.tensor_scalar(ve[:, chain, z:z + 1], mv[:, chain, z, 1:2], 1.0, EPS, ALU.mult, ALU.add))
            pool.tensor_tensor(rstd[:, chain, z:z + 1], ve[:, chain, z:z + 1], W["neghalf"][:, 0:1], ALU.pow
                               ).then_inc(S[done], 1)

        def run(name, t):
            z = t % 2
            if name == "a1":
                moments(0, z, t, "a_stat", "a_rstd")
            if (name, t) == ("b1", 0):
                pool.wait_ge(c_in, 16 * 7)
                pool.tensor_tensor(bv[:, :], bv[:, :], vmask[:, :], ALU.mult).then_inc(pool_mask, 1)
                pool.wait_ge(pool_mask, 1)
            if (name, t) == ("b2", 0):
                low_weight(3)
            if name == "b1":
                pool.wait_ge(S["qk_biased"], t + 1)
                if t >= 2:
                    pool.wait_ge(S["r_full"], t - 1)
                cos, sin = (rot[:, n, :].unsqueeze(1).to_broadcast([P, 64, 8]) for n in range(2))
                src = qk[:, z, :].rearrange("p (a i) -> p a i", i=8)
                link(pool.tensor_tensor(rc[:, z, :].rearrange("p (a i) -> p a i", i=8), src, cos, ALU.mult))
                link(pool.tensor_tensor(rs[:, z, :].rearrange("p (a i) -> p a i", i=8), src, sin, ALU.mult))
                c, s, r = (m[:, z, :].rearrange("p (h two i) -> p h two i", two=2, i=8) for m in (rc, rs, rqk))
                pool.tensor_tensor(r[:, :, 0, :], c[:, :, 0, :], s[:, :, 1, :], ALU.subtract).then_inc(S["rot_done"], 1)
                pool.tensor_tensor(r[:, :, 1, :], s[:, :, 0, :], c[:, :, 1, :], ALU.add).then_inc(S["rot_done"], 1)
                pool.wait_ge(S["v_masked"], t + 1)
                pool.tensor_tensor(vblk[:, z, :, :], vblk[:, z, :, :], bv[:, :].unsqueeze(1).to_broadcast([P, 2, D]), ALU.add
                                   ).then_inc(S["v_done"], 1)
                pool.wait_ge(S["xn_done"], t + 1)
                pool.tensor_tensor(x1[:, t, :], x1[:, t, :], bo[:, :], ALU.add).then_inc(S["x1b_done"], 1)
            if name == "d2":
                moments(1, z, t, "d_stat", "d_rstd")
            if name == "b2":
                key_blocks(pool, z, t, 1, S["k_done"])
            if name == "a0" and t > 1:
                y_low(pool, t)
        stages(run)

    @block.vector
    def _(dve):
        link = Chain(dve, own["dve"])
        tmp, to = weights[0]
        dve.wait_ge(wh_done, 1)
        dve.tensor_tensor(to[:, :, 1, :], tmp, to[:, :, 0, :].bitcast(F32), ALU.subtract).then_inc(wol_done, 1)
        y_low(dve, 0)
        y_low(dve, 1)
        dve.wait_ge(c_in, 16 * 7)
        dve.wait_ge(x_in, 16)

        def low(to, src, high, done):
            dve.tensor_tensor(to, src, high.bitcast(F32), ALU.subtract).then_inc(S[done], 1)

        def run(name, t):
            z = t % 2
            if name == "a1":
                dve.wait_ge(S["x1_full"], t + 1)
                dve.tensor_tensor(x1[:, t, :], bank[0][:, 0:D], xin[:, t, :], ALU.add).then_inc(S["x1_done"], 1)
                dve.wait_ge(S["x1_done"], t + 1)
                link(dve.bn_stats(st[:, 0, z, :], x1[:, t, :]))
                dve.bn_aggr(mv[:, 0, z, :], st[:, 0, z, :]).then_inc(S["a_stat"], 1)
            if name == "a2n":
                dve.wait_ge(S["a_rstd"], t + 1)
                if t >= 2:
                    dve.wait_ge(S["xnT_full"], t - 1)
                dve.tensor_scalar(xn[:, z, :], x1[:, t, :], mv[:, 0, z, 0:1], rstd[:, 0, z:z + 1], ALU.subtract, ALU.mult
                                  ).then_inc(S["xn_done"], 1)
            if name == "a2":
                dve.wait_ge(S["xnT_high"], t + 1)
                low(doubled(xnT[:, z, 1, :, :]), twice(bank[1][:, 0:D]), doubled(xnT[:, z, 0, :, :]), "xnT_low")
            if name == "b1":
                dve.wait_ge(S["qk_full"], t + 1)
                if t >= 2:
                    dve.wait_ge(S["rot_done"], 2 * t - 2)
                dve.tensor_tensor(qk[:, z, :], bank[2][:, :], bqk[:, :], ALU.add).then_inc(S["qk_biased"], 1)
            if name == "b1v":
                dve.wait_ge(S["v_full"], t + 1)
                if t >= 2:
                    dve.wait_ge(S["pv_full"], t - 1)
                dve.tensor_tensor(vblk[:, z, :, :], bank[3][:, :].rearrange("p (b d) -> p b d", b=2),
                                  vmask[:, :].unsqueeze(1).to_broadcast([P, 2, D]), ALU.mult).then_inc(S["v_masked"], 1)
            if name == "b2":
                key_blocks(dve, z, t, 0, k_first)
            if name == "c1":
                dve.wait_ge(S["s_full"], t + 1)
                for j in range(2):
                    link(dve.tensor_tensor(sc[:, z, 8 * j:8 * j + 8, :], bank[4 + j][:, :].rearrange("p (h s) -> p h s", h=8),
                                           causal[:, :].unsqueeze(1).to_broadcast([P, 8, L]), ALU.add))
            if name == "c1m":
                link(dve.tensor_reduce(mx[:, z, :], sc[:, z, :, :], AX.X, ALU.max))
                dve.tensor_tensor(sc[:, z, :, :], sc[:, z, :, :], mx[:, z, :].unsqueeze(2).to_broadcast([P, H, L]),
                                  ALU.subtract).then_inc(S["s_max"], 1)
            if name == "c2":
                dve.wait_ge(S["s_exp"], t + 1)
                link(dve.tensor_reduce(sm[:, z, :], sc[:, z, :, :], AX.X, ALU.add))
                dve.reciprocal(rsm[:, z, :], sm[:, z, :]).then_inc(S["sum_done"], 1)
            if name == "c3":
                dve.wait_ge(S["sum_done"], t + 1)
                dve.wait_ge(S["pv_full"], t + 1)
                if t >= 2:
                    dve.wait_ge(S["attT_full"], t - 1)
                dve.tensor_tensor(att[:, z, :].rearrange("p (h i) -> p h i", h=H), bank[5][:, 0:D].rearrange("p (h i) -> p h i", h=H),
                                  rsm[:, z, :].unsqueeze(2).to_broadcast([P, H, DH]), ALU.mult).then_inc(S["att_done"], 1)
            if name == "d1":
                dve.wait_ge(S["attT_high"], t + 1)
                low(attT[:, z, :, 1, :], bank[7][:, 0:D].rearrange("p (k x) -> p k x", k=KD), attT[:, z, :, 0, :], "attT_low")
            if name == "d2":
                dve.wait_ge(S["o_full"], t + 1)
                dve.wait_ge(S["x1b_done"], t + 1)
                dve.tensor_tensor(x2[:, t, :], bank[7][:, 0:D], x1[:, t, :], ALU.add).then_inc(S["x2_done"], 1)
                dve.wait_ge(S["x2_done"], t + 1)
                link(dve.bn_stats(st[:, 1, z, :], x2[:, t, :]))
                dve.bn_aggr(mv[:, 1, z, :], st[:, 1, z, :]).then_inc(S["d_stat"], 1)
            if name == "d3n":
                dve.wait_ge(S["d_rstd"], t + 1)
                if t >= 2:
                    dve.wait_ge(S["xn2T_full"], t - 1)
                dve.tensor_scalar(xn2[:, z, :], x2[:, t, :], mv[:, 1, z, 0:1], rstd[:, 1, z:z + 1], ALU.subtract, ALU.mult
                                  ).then_inc(S["xn2_done"], 1)
            if name == "d3":
                dve.wait_ge(S["xn2T_high"], t + 1)
                low(xn2T[:, :, 1, t * P:(t + 1) * P], bank[7][:, 0:D].rearrange("p (k x) -> p k x", k=KD),
                    xn2T[:, :, 0, t * P:(t + 1) * P], "xn2T_low")
        stages(run)

    @block.tensor
    def _(pe):
        ident = W["ident"]
        def run(name, t):
            z = t % 2
            if name == "a1":
                pe.wait_ge(wol_done, 1)
                wait_y_low(pe, t)
                if t >= 1:
                    pe.wait_ge(S["x1_done"], t)
                for a in range(PAIRS):
                    mm = split_pair(pe, bank[0][:, 0:D], lambda q: ysplit[:, z, q, a, :, :].rearrange("p b l -> p (b l)"),
                                    lambda q: wout[:, a, q, :], a == 0, a == PAIRS - 1)
                mm.then_inc(S["x1_full"], 1)
            if name == "a2":
                pe.wait_ge(S["xn_done"], t + 1)
                if t >= 1:
                    pe.wait_ge(S["xnT_low"], t)
                for k in range(KD):
                    mm = pe.transpose(bank[1][:, k * P:(k + 1) * P], xn[:, z, k * P:(k + 1) * P], ident[:, :])
                mm.then_inc(S["xnT_full"], 1)
            if name == "b1":
                pe.wait_ge(S["xnT_low"], t + 1)
                pe.wait_ge(wl_done, 2)
                if t >= 1:
                    pe.wait_ge(S["qT_done"], t)
                for k in range(KD):
                    mm = split_pair(pe, bank[2][:, :], lambda q: xnT[:, z, q, k, L:L + P], lambda q: wqk[:, k, q, :],
                                    k == 0, k == KD - 1)
                mm.then_inc(S["qk_full"], 1)
                if t >= 1:
                    pe.wait_ge(S["v_masked"], t)
                for b in range(2):
                    for k in range(KD):
                        mm = split_pair(pe, bank[3][:, b * D:(b + 1) * D],
                                        lambda q: xnT[:, z, q, k, b * P:(b + 1) * P],
                                        lambda q: wv[:, k, q, :], k == 0, k == KD - 1)
                mm.then_inc(S["v_full"], 1)
            if name == "b2":
                pe.wait_ge(S["rot_done"], 2 * t + 2)
                pe.wait_ge(S["qk_biased"], t + 1)
                for n in range(4):
                    mm = pe.transpose(bank[2][:, n * P:(n + 1) * P], rqk[:, z, n * P:(n + 1) * P], ident[:, :])
                mm.then_inc(S["r_full"], 1)
            if name == "c1":
                pe.wait_ge(k_first, 2 * t + 2)
                pe.wait_ge(S["k_done"], 2 * t + 2)
                if t >= 1:
                    pe.wait_ge(S["p_out"], 2 * t)
                    pe.wait_ge(S["att_done"], t)
                for j in range(2):
                    for b in range(2):
                        mm = pe.matmul(bank[4 + j][b * L:(b + 1) * L, :], qT[:, z, j, b * L:(b + 1) * L],
                                       kblk[:, z, j, b, :, :].rearrange("p h s -> p (h s)"), start=True, stop=True)
                mm.then_inc(S["s_full"], 1)
            if name == "c2":
                pe.wait_ge(S["s_exp"], t + 1)
                if t >= 1:
                    pe.wait_ge(S["p_out"], 2 * t - 1)
                for r in range(2):
                    for a in range(4):
                        hh = 8 * r + 2 * a
                        mm = pe.transpose(bank[(6, 4)[r]][:, a * P:(a + 1) * P],
                                          sc[:, z, hh:hh + 2, :].rearrange("p h s -> p (h s)"), ident[:, :])
                    mm.then_inc(S["p_full"], 1)
            if name == "c3":
                pe.wait_ge(S["p_out"], 2 * t + 2)
                pe.wait_ge(S["v_done"], t + 1)
                for b in range(2):
                    for a in range(PAIRS):
                        mm = pe.matmul(bank[5][b * L:(b + 1) * L, a * 32:(a + 1) * 32], pt[:, z, a, b * L:(b + 1) * L],
                                       vblk[:, z, b, a * 32:(a + 1) * 32], start=True, stop=True)
                mm.then_inc(S["pv_full"], 1)
            if name == "d1":
                pe.wait_ge(S["att_done"], t + 1)
                if t >= 1:
                    pe.wait_ge(S["xn2T_low"], t)
                for k in range(KD):
                    mm = pe.transpose(bank[7][:, k * P:(k + 1) * P], att[:, z, k * P:(k + 1) * P], ident[:, :])
                mm.then_inc(S["attT_full"], 1)
            if name == "d2":
                pe.wait_ge(S["attT_low"], t + 1)
                pe.wait_ge(wl_done, 3)
                for k in range(KD):
                    mm = split_pair(pe, bank[7][:, 0:D], lambda q: attT[:, z, k, q, :], lambda q: wo[:, k, q, :],
                                    k == 0, k == KD - 1)
                mm.then_inc(S["o_full"], 1)
            if name == "d3":
                pe.wait_ge(S["xn2_done"], t + 1)
                for k in range(KD):
                    mm = pe.transpose(bank[7][:, k * P:(k + 1) * P], xn2[:, z, k * P:(k + 1) * P], ident[:, :])
                mm.then_inc(S["xn2T_full"], 1)
        stages(run)


def block_3(nc, ins, out, x2, xn2T, W, ctx):
    def sb(name, shape, dt):
        return ctx.enter_context(nc.sbuf_tensor(name, shape, dt))

    def sem(name):
        return ctx.enter_context(nc.semaphore(name))

    w1raw = staged(W["stage"], 0, KD, HID)
    w2raw = sb("w2raw", [P, HT, D], F32)
    w1 = sb("w1", [P, KD, 2, HID], F32R)
    w2 = sb("w2", [P, HT, 2, D], F32R)
    b1 = sb("b1e", [P, HT], F32)
    b2 = sb("b2e", [P, E4, D], F32)
    gb = sb("gb", [P, HT], F32)
    gbs = sb("gbs", [P, 2, HT, P], F32R)
    hid = sb("hid", [P, 2, 512], F32)
    hT = sb("hT", [P, HT, 2, ROWS], F32R)
    cexp = sb("cexp", [P, D], F32)
    csum = sb("csum", [P, D], F32)
    ydiff = sb("ydiff", [P, 2, D], F32)
    wrraw = sb("wrraw", [P, KD, E4], F32)
    wr = sb("wr", [P, KD, 2, E4], F32R)
    rT = sb("rT", [E4, ROWS], F32)
    br = sb("br", [P, E4], F32)
    logit = sb("logit", [P, RT, E4], F32)
    rank = sb("rank", [P, RT, E4], F32)
    cmp = sb("cmp", [P, RT, E4], F32)
    top = sb("top", [P, RT, 1], F32)
    gate = sb("gate", [P, RT, E4], F32)
    gsum = sb("gsum", [P, RT, 1], F32)
    gcur = sb("gcur", [P, RT], F32)
    hbank = [ctx.enter_context(nc.psum_tensor(f"hbank{n}", [P, 512], F32)) for n in range(2)]
    ybank = [ctx.enter_context(nc.psum_tensor(f"ybank{n}", [P, 512], F32)) for n in range(3)]
    rbank = [ctx.enter_context(nc.psum_tensor(f"rbank{n}", [P, 512], F32)) for n in range(3)]

    r_in = sem("r_in")
    b2_in = sem("b2_in")
    w1_in, w2_in, b1_in = W["w1_in"], sem("w2_in3"), sem("b1_in")
    wr_high, wr_done = sem("wr_high"), sem("wr_done")
    rT_full, rT_out = sem("rT_full"), sem("rT_out")
    r_full = sem("router_full")
    g_max, g_exp, g_done = sem("g_max"), sem("g_exp"), sem("g_done")
    dve_step = sem("dve_step3")
    b2_sum = sem("b2_sum")
    pool_step = sem("pool_step3")
    w1_high, w1_done = sem("w1_high"), sem("w1_done")
    w2_high, w2_done = sem("w2_high3"), sem("w2_done3")
    gb_done, gb_high, gb_low = sem("gb_done"), sem("gb_high"), sem("gb_low")
    h_full = sem("h_full")
    h_gelu = sem("h_gelu")
    h_high = sem("h_high")
    h_done = sem("h_done")
    y_full = sem("y_full")
    y_got = sem("y_got")
    y_add = sem("y_add")
    c_add = sem("c_add")
    g_cur = sem("g_cur")
    fin_done = sem("fin_done")
    out_done3 = sem("out_done3")

    def experts(eng, body):
        body(Batch(0), True)
        with eng.Fori(0, E4 - 2) as turn:
            body(Batch(1, turn), True)
        body(Batch(E4 - 1), False)

    block = ctx.enter_context(nc.Block())

    @block.sync
    def _(sp):
        def load_w1(n):
            wait(sp, w1_done, n, 1, 0)
            sp.dma_start(w1raw[:, :, :], ins["w1"][n.lin(1, 0)].rearrange("(k p) n -> p k n", p=P)).then_inc(w1_in, 16)

        def load_w2(n):
            wait(sp, w2_done, n, 1, 0)
            sp.dma_start(w2raw[:, :, :], ins["w2"][n.lin(1, 0)].rearrange("(k p) n -> p k n", p=P)).then_inc(w2_in, 16)
            wait(sp, h_gelu, n, 16, 0)
            wait(sp, gb_done, n, 1, 0)
            sp.dma_start(b1[:, :], ins["b1"][n.lin(1, 0)]).then_inc(b1_in, 16)

        sp.dma_start(wrraw[:, :, :], ins["wr"].rearrange("(k p) n -> p k n", p=P)).then_inc(r_in, 16)
        sp.dma_start(br[:, :], ins["br"].partition_broadcast(P)).then_inc(b2_in, 16)
        load_w2(Batch(0))
        sp.dma_start(b2[:, :, :].rearrange("p e d -> p (e d)"), ins["b2e"].partition_broadcast(P)).then_inc(b2_in, 16)

        def body(e, more):
            if more:
                n = Batch(e.off + 1, e.turn)
                load_w1(n)
                load_w2(n)
        experts(sp, body)
        for t in range(RT):
            sp.wait_ge(fin_done, t + 1)
            sp.dma_start(out[t * P:(t + 1) * P, :], x2[:, t, :]).then_inc(out_done3, 16)
        sp.wait_ge(out_done3, 16 * RT)

    @block.scalar
    def _(act):
        def split_w1(e):
            wait(act, w1_in, e, 16, 16)
            wait(act, h_full, e, 16, 0)
            act.activation(w1[:, :, 0, :], w1raw[:, :, :], ACT.Copy).then_inc(w1_high, 1)

        act.wait_ge(r_in, 16)
        act.activation(wr[:, :, 0, :], wrraw[:, :, :], ACT.Copy).then_inc(wr_high, 1)
        split_w1(Batch(0))
        for half in range(2):
            act.wait_ge(rT_full, half + 1)
            act.activation(rT[:, half * 512:(half + 1) * 512], rbank[half][0:E4, :], ACT.Copy).then_inc(rT_out, 1)

        def body(e, more):
            wait(act, b1_in, e, 16, 16)
            act.activation(gb[:, :], b1[:, :], ACT.Gelu).then_inc(gb_done, 1)
            wait(act, y_full, e, 9, 0)
            wait(act, gb_done, e, 1, 1)
            act.activation(gbs[:, 0, :, :], gb[:, :].unsqueeze(2).to_broadcast([P, HT, P]), ACT.Copy).then_inc(gb_high, 1)
            for m in range(2 * HT):
                half, t = divmod(m, HT)
                z = m % 2
                s = slice(half * 512, half * 512 + 512)
                wait(act, h_full, e, 16, m + 1)
                wait(act, h_done, e, 16, m - 1)
                act.activation(hid[:, z, :], hbank[z][:, :], ACT.Gelu, bias=b1[:, t:t + 1]).then_inc(h_gelu, 1)
                wait(act, h_gelu, e, 16, m + 1)
                act.activation(hT[:, t, 0, s], hid[:, z, :], ACT.Copy).then_inc(h_high, 1)
            if e.turn is None and e.off == 0:
                act.wait_ge(g_max, 1)
                act.activation(gate[:, :, :], gate[:, :, :], ACT.Exp).then_inc(g_exp, 1)
            if more:
                split_w1(Batch(e.off + 1, e.turn))
        experts(act, body)

    @block.vector
    def _(dve):
        def split_w1(e):
            wait(dve, w1_high, e, 1, 1)
            dve.tensor_tensor(w1[:, :, 1, :], w1raw[:, :, :], w1[:, :, 0, :].bitcast(F32), ALU.subtract).then_inc(w1_done, 1)

        dve.wait_ge(wr_high, 1)
        dve.tensor_tensor(wr[:, :, 1, :], wrraw[:, :, :], wr[:, :, 0, :].bitcast(F32), ALU.subtract).then_inc(wr_done, 1)
        split_w1(Batch(0))
        dve.wait_ge(r_full, 1)
        dve.wait_ge(b2_in, 32)
        dve.tensor_tensor(logit[:, :, :], rbank[2][:, 0:RT * E4].rearrange("p (t e) -> p t e", e=E4),
                          br[:, :].unsqueeze(1).to_broadcast([P, RT, E4]), ALU.add).then_inc(dve_step, 1)
        dve.wait_ge(dve_step, 1)
        chain = [1]

        def link(ins):
            chain[0] += 1
            ins.then_inc(dve_step, 1)
            dve.wait_ge(dve_step, chain[0])

        def rank_of(e):
            mine = logit[:, :, e:e + 1]
            link(dve.tensor_tensor(cmp[:, :, :], logit[:, :, :], mine.to_broadcast([P, RT, E4]), ALU.is_gt))
            if e:
                link(dve.tensor_tensor(cmp[:, :, 0:e], logit[:, :, 0:e], mine.to_broadcast([P, RT, e]), ALU.is_ge))
            link(dve.tensor_reduce(rank[:, :, e:e + 1], cmp[:, :, :], AX.X, ALU.add))

        def chosen():
            link(dve.tensor_scalar(rank[:, :, :], rank[:, :, :], 2.0, None, ALU.is_lt))
            link(dve.tensor_reduce(top[:, :, :], logit[:, :, :], AX.X, ALU.max))
            dve.tensor_tensor(gate[:, :, :], logit[:, :, :], top[:, :, :].to_broadcast([P, RT, E4]), ALU.subtract
                              ).then_inc(g_max, 1)

        def gates():
            dve.wait_ge(g_exp, 1)
            link(dve.tensor_tensor(gate[:, :, :], gate[:, :, :], rank[:, :, :], ALU.mult))
            link(dve.tensor_reduce(gsum[:, :, :], gate[:, :, :], AX.X, ALU.add))
            link(dve.reciprocal(gsum[:, :, :], gsum[:, :, :]))
            dve.tensor_tensor(gate[:, :, :], gate[:, :, :], gsum[:, :, :].to_broadcast([P, RT, E4]), ALU.mult
                              ).then_inc(g_done, 1)

        def body(e, more):
            for m in range(2 * HT):
                half, t = divmod(m, HT)
                s = slice(half * 512, half * 512 + 512)
                wait(dve, h_high, e, 16, m + 1)
                dve.tensor_tensor(hT[:, t, 1, s], hid[:, m % 2, :], hT[:, t, 0, s].bitcast(F32), ALU.subtract).then_inc(h_done, 1)
                if 4 <= m < 8:
                    if m == 4:
                        wait(dve, w2_in, e, 16, 16)
                    q = slice(2 * m - 8, 2 * m - 6)
                    dve.tensor_copy(w2[:, q, 0, :], w2raw[:, q, :]).then_inc(w2_high, 1)
                if e.turn is None and e.off == 0:
                    if m in (1, 3, 5, 7):
                        rank_of(m // 2)
                    if m == 12:
                        chosen()
            if more:
                split_w1(Batch(e.off + 1, e.turn))
            if e.turn is None and e.off == 0:
                gates()
            wait(dve, y_full, e, 9, 1)
            dve.tensor_copy(cexp[:, :], ybank[0][:, 0:D]).then_inc(y_got, 1)
            wait(dve, y_got, e, 9, 1)
            dve.wait_ge(b2_sum, 1)
            wait(dve, c_add, e, 1, 0)
            dve.tensor_tensor(csum[:, :], csum[:, :], cexp[:, :], ALU.add).then_inc(c_add, 1)
            dve.wait_ge(g_done, 1)
            wait(dve, y_add, e, 8, 0)
            dve.tensor_copy(gcur[:, :], gate[:, :, e.lin(1, 0)]).then_inc(g_cur, 1)
            wait(dve, g_cur, e, 1, 1)
            for t in range(RT):
                wait(dve, y_full, e, 9, t + 2)
                wait(dve, y_add, e, 8, t - 1)
                dve.tensor_tensor(ydiff[:, t % 2, :], ybank[(t + 1) % 3][:, 0:D], cexp[:, :], ALU.subtract).then_inc(y_got, 1)
                wait(dve, y_got, e, 9, t + 2)
                dve.scalar_tensor_tensor(out=x2[:, t, :], in0=ydiff[:, t % 2, :], scalar=gcur[:, t:t + 1], in1=x2[:, t, :],
                                         op0=ALU.mult, op1=ALU.add).then_inc(y_add, 1)
                if not more:
                    dve.wait_ge(c_add, E4)
                    wait(dve, y_add, e, 8, t + 1)
                    dve.tensor_tensor(x2[:, t, :], x2[:, t, :], csum[:, :], ALU.add).then_inc(fin_done, 1)
        experts(dve, body)

    @block.gpsimd
    def _(pool):
        chain = [0]

        def link(ins):
            chain[0] += 1
            ins.then_inc(pool_step, 1)
            pool.wait_ge(pool_step, chain[0])

        pool.wait_ge(b2_in, 32)
        link(pool.tensor_tensor(b2[:, 0, :], b2[:, 0, :], b2[:, 1, :], ALU.add))
        link(pool.tensor_tensor(b2[:, 2, :], b2[:, 2, :], b2[:, 3, :], ALU.add))
        pool.tensor_tensor(csum[:, :], b2[:, 0, :], b2[:, 2, :], ALU.add).then_inc(b2_sum, 1)

        def body(e, more):
            wait(pool, gb_high, e, 1, 1)
            pool.tensor_tensor(gbs[:, 1, :, :], gb[:, :].unsqueeze(2).to_broadcast([P, HT, P]), gbs[:, 0, :, :].bitcast(F32),
                               ALU.subtract).then_inc(gb_low, 1)
            wait(pool, w2_high, e, 4, 4)
            pool.tensor_tensor(w2[:, :, 1, :], w2raw[:, :, :], w2[:, :, 0, :].bitcast(F32), ALU.subtract
                               ).then_inc(w2_done, 1)
        experts(pool, body)

    @block.tensor
    def _(pe):
        pe.wait_ge(wr_done, 1)
        for side in range(2):
            for k in range(KD):
                mm = split_pair(pe, rbank[side][0:E4, :], lambda q: wr[:, k, q, :],
                                lambda q: xn2T[:, k, q, side * 512:(side + 1) * 512], k == 0, k == KD - 1)
            mm.then_inc(rT_full, 1)
        for t in range(RT):
            pe.wait_ge(rT_out, 1 + t // 4)
            mm = pe.transpose(rbank[2][:, t * E4:(t + 1) * E4], rT[:, t * P:(t + 1) * P], W["ident"][0:E4, 0:E4])
        mm.then_inc(r_full, 1)

        def body(e, more):
            wait(pe, w1_done, e, 1, 1)
            for m in range(2 * HT):
                half, t = divmod(m, HT)
                s = slice(half * 512, half * 512 + 512)
                wait(pe, h_gelu, e, 16, m - 1)
                for k in range(KD):
                    mm = split_pair(pe, hbank[m % 2][:, :], lambda q: w1[:, k, q, t * P:(t + 1) * P],
                                    lambda q: xn2T[:, k, q, s], k == 0, k == KD - 1)
                mm.then_inc(h_full, 1)
            wait(pe, w2_done, e, 1, 1)
            wait(pe, gb_low, e, 1, 1)
            for r in range(RT + 1):
                if r == 1:
                    wait(pe, h_done, e, 16, 8)
                if r == 5:
                    wait(pe, h_done, e, 16, 16)
                wait(pe, y_got, e, 9, r - 2)
                for t in range(HT):
                    mm = split_pair(pe, ybank[r % 3][:, 0:D],
                                    (lambda q: gbs[:, q, t, :]) if r == 0 else (lambda q: hT[:, t, q, (r - 1) * P:r * P]),
                                    lambda q: w2[:, t, q, :], t == 0, t == HT - 1)
                mm.then_inc(y_full, 1)
        experts(pe, body)


def build(nc, ins, out, lat_scratch, q_scratch, y_scratch):
    with ExitStack() as ctx:
        W = constants(nc, ctx)
        with ExitStack() as cross:
            X = W | shared(nc, cross)
            F = Context(nc, ins, lat_scratch, q_scratch, X, cross)
            with ExitStack() as c:
                block_0(nc, ins, F, X, c)
            with ExitStack() as c:
                block_1(nc, ins, F, y_scratch, X, c)
        with ExitStack() as kept:
            x2 = kept.enter_context(nc.sbuf_tensor("x2", [P, RT, D], F32))
            xn2T = kept.enter_context(nc.sbuf_tensor("xn2T", [P, KD, 2, ROWS], F32R))
            with ExitStack() as c:
                block_2(nc, ins, y_scratch, x2, xn2T, W, c)
            with ExitStack() as c:
                block_3(nc, ins, out, x2, xn2T, W, c)


def kernel(**inputs):
    import concourse.bacc as bacc
    from concourse.bass_utils import run_bass_kernel_spmd

    def flat(name):
        return np.ascontiguousarray(inputs[name])

    def lay(a):
        return np.ascontiguousarray(a)

    order = np.array([h * 16 + i for h in range(16) for i in (*range(0, 16, 2), *range(1, 16, 2))])
    wkv = flat("L0_xattn_Wkv")
    mask = flat("mask_BxS2_bk0")
    mask = np.concatenate([mask[:, :TAIL].reshape(B, P, CPP).transpose(0, 2, 1).reshape(B, TAIL), mask[:, TAIL:]], 1)
    half = np.arange(8, dtype=np.float32)
    theta = np.float32(1.0) / np.float32(10000.0) ** (half / np.float32(8))
    angle = (np.arange(P) % L).astype(np.float32)[:, None] * theta[None, :]
    parts = np.arange(P)
    arrays = {
        "x": lay(flat("x").reshape(ROWS, D)), "ctx": flat("ctx_1024"), "mask": lay(mask),
        "g1": flat("L0_xattn_g1"), "b1x": flat("L0_xattn_b1"), "g2": flat("L0_xattn_g2"), "b2x": flat("L0_xattn_b2"),
        "wq": flat("L0_xattn_Wq"), "wkT": lay(wkv[:, :INNER].T), "wv": lay(wkv[:, INNER:]), "wout": flat("L0_xattn_Wout"),
        "wqk": lay(np.concatenate([flat("L0_attn_W_q")[order], flat("L0_attn_W_k")[order]], 0).T),
        "wvs": lay(flat("L0_attn_W_v").T), "wos": lay(flat("L0_attn_W_o").T),
        "bqk": lay(np.concatenate([flat("L0_attn_b_q")[order], flat("L0_attn_b_k")[order]])),
        "bv": flat("L0_attn_b_v"), "bo": flat("L0_attn_b_o"),
        "w1": flat("L0_ffn_w1"), "w2": flat("L0_ffn_w2"), "b1": lay(flat("L0_ffn_b1").reshape(E4, HT, P).transpose(0, 2, 1)),
        "b2e": lay(flat("L0_ffn_b2").reshape(-1)), "wr": flat("L0_ffn_wr"), "br": flat("L0_ffn_br"),
        "rot": lay(np.stack([np.cos(angle), np.sin(angle)], 1).astype(np.float32)),
        "causal": lay(np.where(np.arange(L)[None, :] <= (parts % L)[:, None], 0.0, NEG).astype(np.float32)),
        "headmask": lay((parts[:, None] // 16 == np.arange(8)[None, :]).astype(np.float32)),
        "vmask": lay((parts[:, None] // L == (np.arange(D)[None, :] // 16) % 2).astype(np.float32)),
    }
    nc = bacc.Bacc("TRN2", target_bir_lowering=False, num_devices=1)
    in_map, ins = {}, {}
    for name, a in arrays.items():
        in_map[f"in_{name}"] = a
        ins[name] = nc.dram_tensor(f"in_{name}", a.shape, mybir.dt.from_np(a.dtype), kind="ExternalInput").ap()
    out = nc.dram_tensor("out", (ROWS, D), F32, kind="ExternalOutput").ap()
    lat_scratch = nc.dram_tensor("lat_scratch", (B, L, D), F32, kind="Internal").ap()
    q_scratch = nc.dram_tensor("q_scratch", (B, P, PAIRS, L), F32, kind="Internal").ap()
    y_scratch = nc.dram_tensor("y_scratch", (B, P, PAIRS, L), F32, kind="Internal").ap()
    build(nc, ins, out, lat_scratch, q_scratch, y_scratch)
    r = run_bass_kernel_spmd(nc, [in_map], core_ids=[0])
    return r.results[0]["out"].reshape(B, L, D)
```
